# Optimizing a Trainium2 kernel written in Bass

```python
import numpy as np
import jax
import jax.numpy as jnp

def _softmax(x, axis=-1):
    return jax.nn.softmax(x, axis=axis)

def _gelu(x):
    return jax.nn.gelu(x, approximate=True)

def _silu(x):
    return jax.nn.silu(x)

def _sigmoid(x):
    return jax.nn.sigmoid(x)

def _layernorm(x, axis=-1, eps=1e-05):
    m = jnp.mean(x, axis=axis, keepdims=True)
    v = jnp.var(x, axis=axis, keepdims=True)
    return (x - m) / jnp.sqrt(v + eps)

def _scatter_add(tgt, idx, src, axis=0):
    return tgt.at[idx].add(src)

def _segment_sum(src, seg, n):
    return jax.ops.segment_sum(src, seg, n)
kernel_name = 'mk_conv_preact_d4_conv_nchw64_r2_ce2bee'

def setup_inputs(seed: int=0):
    np.random.seed(seed)
    _w = jnp.asarray

    def _rec_inputs():
        import jax
        import jax.numpy as jnp
        _gk = jax.random.key(seed)
        x = 1.648e-05 + 1 * jax.random.normal(jax.random.fold_in(_gk, 1), (4, 32, 96, 96), jnp.float32)
        return x
    x = _rec_inputs()

    def _L0_conv_setup():
        import jax, jax.numpy as jnp
        import numpy as np
        BLOCK, HALO, HEADS = (8, 3, 4)
        WIN = BLOCK + 2 * HALO

        def _unfold_halo(t, nh, nw):
            B, C = (t.shape[0], t.shape[1])
            tp = jnp.pad(t, ((0, 0), (0, 0), (HALO, HALO), (HALO, HALO)))
            ri = (jnp.arange(nh) * BLOCK)[:, None] + jnp.arange(WIN)
            ci = (jnp.arange(nw) * BLOCK)[:, None] + jnp.arange(WIN)
            p = tp[:, :, ri, :]
            p = p[:, :, :, :, ci]
            p = p.transpose(0, 2, 4, 3, 5, 1)
            return p.reshape(B * nh * nw, WIN * WIN, C)
        key = jax.random.key(seed)
        k1, k2, k3, k4 = jax.random.split(key, 4)
        B, C, H, W = (4, 32, 96, 96)
        d = C // HEADS
        return {'x': jax.random.normal(k1, (B, C, H, W), dtype=jnp.float32), 'w_qkv': jax.random.normal(k2, (3 * C, C), dtype=jnp.float32) * 0.05, 'rel_h': jax.random.normal(k3, (1, WIN, 1, d // 2), dtype=jnp.float32), 'rel_w': jax.random.normal(k4, (1, 1, WIN, d // 2), dtype=jnp.float32)}
    _L0_conv_all = _L0_conv_setup()
    _L0_conv_in = {k: v for k, v in _L0_conv_all.items() if k in ('w_qkv', 'rel_h', 'rel_w')}
    del _L0_conv_all

    def _L1_conv_setup():
        import jax, jax.numpy as jnp
        import numpy as np
        K = 3
        STRIDE = 1
        PAD = 1

        def conv2d(x, w, b):
            y = jax.lax.conv_general_dilated(x, w, window_strides=(STRIDE, STRIDE), padding=[(PAD, PAD), (PAD, PAD)], dimension_numbers=('NCHW', 'OIHW', 'NCHW'))
            return y + b[None, :, None, None]

        def deform_conv2d(x, offset, mask, weight):
            B, C, H, W = x.shape
            K2 = K * K
            Ho, Wo = (offset.shape[2], offset.shape[3])
            off = offset.reshape(B, K2, 2, Ho, Wo)
            dy, dx = (off[:, :, 0], off[:, :, 1])
            ky, kx = jnp.meshgrid(jnp.arange(K), jnp.arange(K), indexing='ij')
            ky = ky.reshape(1, K2, 1, 1).astype(x.dtype)
            kx = kx.reshape(1, K2, 1, 1).astype(x.dtype)
            hs = (jnp.arange(Ho) * STRIDE - PAD).astype(x.dtype)[None, None, :, None]
            ws = (jnp.arange(Wo) * STRIDE - PAD).astype(x.dtype)[None, None, None, :]
            py = hs + ky + dy
            px = ws + kx + dx
            y0 = jnp.floor(py)
            x0 = jnp.floor(px)
            ly = py - y0
            lx = px - x0
            y0i = y0.astype(jnp.int32)
            x0i = x0.astype(jnp.int32)
            xt = jnp.transpose(x, (0, 2, 3, 1))
            b_idx = jnp.arange(B).reshape(B, 1, 1, 1)

            def gather(yi, xi):
                valid = (yi >= 0) & (yi < H) & (xi >= 0) & (xi < W)
                yc = jnp.clip(yi, 0, H - 1)
                xc = jnp.clip(xi, 0, W - 1)
                g = xt[b_idx, yc, xc]
                return g * valid[..., None].astype(x.dtype)
            w00 = ((1 - ly) * (1 - lx))[..., None]
            w01 = ((1 - ly) * lx)[..., None]
            w10 = (ly * (1 - lx))[..., None]
            w11 = (ly * lx)[..., None]
            val = gather(y0i, x0i) * w00 + gather(y0i, x0i + 1) * w01 + gather(y0i + 1, x0i) * w10 + gather(y0i + 1, x0i + 1) * w11
            w_r = weight.reshape(weight.shape[0], weight.shape[1], K2)
            out = jnp.einsum('bkhwc,bkhw,ock->bohw', val, mask, w_r)
            return out
        key = jax.random.key(seed)
        ks = jax.random.split(key, 6)
        B, Cin, Cout, H, W = (8, 32, 32, 64, 64)
        x = jax.random.normal(ks[0], (B, Cin, H, W), dtype=jnp.float32)
        offset_w = jax.random.normal(ks[1], (2 * K * K, Cin, K, K), dtype=jnp.float32) * 0.01
        offset_b = jax.random.normal(ks[2], (2 * K * K,), dtype=jnp.float32) * 0.01
        mask_w = jax.random.normal(ks[3], (K * K, Cin, K, K), dtype=jnp.float32) * 0.02
        mask_b = jax.random.normal(ks[4], (K * K,), dtype=jnp.float32) * 0.02
        dcn_w = jax.random.normal(ks[5], (Cout, Cin, K, K), dtype=jnp.float32) * (1.0 / np.sqrt(Cin * K * K))
        return {'x': x, 'offset_w': offset_w, 'offset_b': offset_b, 'mask_w': mask_w, 'mask_b': mask_b, 'dcn_w': dcn_w}
    _L1_conv_all = _L1_conv_setup()
    _L1_conv_in = {k: v for k, v in _L1_conv_all.items() if k in ('offset_w', 'offset_b', 'mask_w', 'mask_b', 'dcn_w')}
    del _L1_conv_all

    def _L2_conv_setup():
        import jax, jax.numpy as jnp
        import numpy as np
        L_SEG, M_CHEB, MODES1, MODES2 = (4, 8, 16, 16)

        def _cft(signals, t_coords, f_points, L, M):
            n = signals.shape[-1]
            seg_len = 1.0 / L
            starts = jnp.linspace(0.0, 1.0, L + 1)[:-1]
            k = jnp.arange(M, dtype=jnp.float32)
            nodes = -jnp.cos((2.0 * k + 1.0) * jnp.pi / (2.0 * M))
            T = jnp.cos(k[:, None] * jnp.arccos(nodes)[None, :])
            w_prime = f_points * (2.0 * jnp.pi * (seg_len / 2.0))
            angle = nodes[:, None] * w_prime[None, :]
            Wr = T @ jnp.cos(angle) * (seg_len / 2.0)
            Wi = T @ -jnp.sin(angle) * (seg_len / 2.0)
            t_seg = starts[:, None] + seg_len / 2.0 * (nodes[None, :] + 1.0)
            right = jnp.clip(jnp.searchsorted(t_coords, t_seg), 0, n - 1)
            left = jnp.clip(right - 1, 0, n - 1)
            tl, tr = (t_coords[left], t_coords[right])
            denom = jnp.where(tr - tl < 1e-08, 1.0, tr - tl)
            wr = (t_seg - tl) / denom
            wl = 1.0 - wr
            seg_sig = wl * signals[..., left] + wr * signals[..., right]
            Sr = jnp.einsum('nclm,mf->nclf', seg_sig, Wr)
            Si = jnp.einsum('nclm,mf->nclf', seg_sig, Wi)
            phase = -2.0 * jnp.pi * starts[:, None] * f_points[None, :]
            cr, ci = (jnp.cos(phase), jnp.sin(phase))
            real = jnp.sum(Sr * cr - Si * ci, axis=2)
            imag = jnp.sum(Sr * ci + Si * cr, axis=2)
            return (real, imag)

        def _cft2d(x, m1, m2, L, M):
            B, C, H, W = x.shape
            tw = jnp.linspace(0.0, 1.0, W)
            fw = jnp.fft.rfftfreq(W, d=1.0 / W)[:m2].astype(jnp.float32)
            xr = x.transpose(0, 2, 1, 3).reshape(B * H, C, W)
            r, i = _cft(xr, tw, fw, L, M)
            r = r.reshape(B, H, C, m2).transpose(0, 2, 1, 3)
            i = i.reshape(B, H, C, m2).transpose(0, 2, 1, 3)
            th = jnp.linspace(0.0, 1.0, H)
            fh = jnp.fft.fftfreq(H, d=1.0 / H).astype(jnp.float32)
            hidx = np.concatenate([np.arange(0, m1 // 2), np.arange(H - (m1 - m1 // 2), H)])
            fsel = fh[hidx]
            rh = r.transpose(0, 3, 1, 2).reshape(B * m2, C, H)
            ih = i.transpose(0, 3, 1, 2).reshape(B * m2, C, H)
            rr, ri = _cft(rh, th, fsel, L, M)
            ir, ii = _cft(ih, th, fsel, L, M)
            real = (rr - ii).reshape(B, m2, C, m1).transpose(0, 2, 3, 1)
            imag = (ri + ir).reshape(B, m2, C, m1).transpose(0, 2, 3, 1)
            return (real, imag)
        key = jax.random.key(seed)
        ks = jax.random.split(key, 6)
        B, C, O, H, W = (32, 32, 32, 64, 64)
        m1, m2 = (MODES1, MODES2)
        scale = 1.0 / (C * O)
        x = jax.random.normal(ks[0], (B, C, H, W), jnp.float32)
        w1 = scale * jax.random.uniform(ks[1], (C, O, m1, m2, 2), jnp.float32)
        w2 = scale * jax.random.uniform(ks[2], (C, O, m1, m2, 2), jnp.float32)
        d_in = C * (m1 // 4) * (m2 // 4) * 2
        hid = (C + O) * 2
        lin1_w = jax.random.normal(ks[3], (d_in, hid), jnp.float32) * 0.02
        lin1_b = jnp.zeros((hid,), jnp.float32)
        lin2_w = jax.random.normal(ks[4], (hid, O), jnp.float32) * 0.02
        lin2_b = jnp.zeros((O,), jnp.float32)
        return dict(x=x, w1=w1, w2=w2, lin1_w=lin1_w, lin1_b=lin1_b, lin2_w=lin2_w, lin2_b=lin2_b)
    _L2_conv_all = _L2_conv_setup()
    _L2_conv_in = {k: v for k, v in _L2_conv_all.items() if k in ('w1', 'w2', 'lin1_w', 'lin1_b', 'lin2_w', 'lin2_b')}
    del _L2_conv_all

    def _L3_conv_setup():
        import jax, jax.numpy as jnp
        import numpy as np
        from jax import lax
        PS = 8

        def _conv(x, w, groups=1, padding='VALID'):
            return lax.conv_general_dilated(x, w, window_strides=(1, 1), padding=padding, dimension_numbers=('NCHW', 'OIHW', 'NCHW'), feature_group_count=groups)
        key = jax.random.key(seed)
        ks = jax.random.split(key, 7)
        dim = 32
        B, H, W = (4, 128, 128)
        x = jax.random.normal(ks[0], (B, dim, H, W), dtype=jnp.float32)
        w_hidden = jax.random.normal(ks[1], (6 * dim, dim, 1, 1), dtype=jnp.float32) * 0.05
        b_hidden = jax.random.normal(ks[2], (6 * dim,), dtype=jnp.float32) * 0.01
        w_dw = jax.random.normal(ks[3], (6 * dim, 1, 3, 3), dtype=jnp.float32) * 0.05
        b_dw = jax.random.normal(ks[4], (6 * dim,), dtype=jnp.float32) * 0.01
        w_out = jax.random.normal(ks[5], (dim, 2 * dim, 1, 1), dtype=jnp.float32) * 0.05
        b_out = jax.random.normal(ks[6], (dim,), dtype=jnp.float32) * 0.01
        return {'x': x, 'w_hidden': w_hidden, 'b_hidden': b_hidden, 'w_dw': w_dw, 'b_dw': b_dw, 'w_out': w_out, 'b_out': b_out}
    _L3_conv_all = _L3_conv_setup()
    _L3_conv_in = {k: v for k, v in _L3_conv_all.items() if k in ('w_hidden', 'b_hidden', 'w_dw', 'b_dw', 'w_out', 'b_out')}
    del _L3_conv_all
    return {'x': x, 'L0_conv_w_qkv': _L0_conv_in['w_qkv'], 'L0_conv_rel_h': _L0_conv_in['rel_h'], 'L0_conv_rel_w': _L0_conv_in['rel_w'], 'L1_conv_offset_w': _L1_conv_in['offset_w'], 'L1_conv_offset_b': _L1_conv_in['offset_b'], 'L1_conv_mask_w': _L1_conv_in['mask_w'], 'L1_conv_mask_b': _L1_conv_in['mask_b'], 'L1_conv_dcn_w': _L1_conv_in['dcn_w'], 'L2_conv_w1': _L2_conv_in['w1'], 'L2_conv_w2': _L2_conv_in['w2'], 'L2_conv_lin1_w': _L2_conv_in['lin1_w'], 'L2_conv_lin1_b': _L2_conv_in['lin1_b'], 'L2_conv_lin2_w': _L2_conv_in['lin2_w'], 'L2_conv_lin2_b': _L2_conv_in['lin2_b'], 'L3_conv_w_hidden': _L3_conv_in['w_hidden'], 'L3_conv_b_hidden': _L3_conv_in['b_hidden'], 'L3_conv_w_dw': _L3_conv_in['w_dw'], 'L3_conv_b_dw': _L3_conv_in['b_dw'], 'L3_conv_w_out': _L3_conv_in['w_out'], 'L3_conv_b_out': _L3_conv_in['b_out']}

def reference(x, L0_conv_w_qkv, L0_conv_rel_h, L0_conv_rel_w, L1_conv_offset_w, L1_conv_offset_b, L1_conv_mask_w, L1_conv_mask_b, L1_conv_dcn_w, L2_conv_w1, L2_conv_w2, L2_conv_lin1_w, L2_conv_lin1_b, L2_conv_lin2_w, L2_conv_lin2_b, L3_conv_w_hidden, L3_conv_b_hidden, L3_conv_w_dw, L3_conv_b_dw, L3_conv_w_out, L3_conv_b_out):
    import jax
    import jax.numpy as jnp

    def _L0_conv_ref(x, w_qkv, rel_h, rel_w):
        import jax, jax.numpy as jnp
        import numpy as np
        BLOCK, HALO, HEADS = (8, 3, 4)
        WIN = BLOCK + 2 * HALO

        def _unfold_halo(t, nh, nw):
            B, C = (t.shape[0], t.shape[1])
            tp = jnp.pad(t, ((0, 0), (0, 0), (HALO, HALO), (HALO, HALO)))
            ri = (jnp.arange(nh) * BLOCK)[:, None] + jnp.arange(WIN)
            ci = (jnp.arange(nw) * BLOCK)[:, None] + jnp.arange(WIN)
            p = tp[:, :, ri, :]
            p = p[:, :, :, :, ci]
            p = p.transpose(0, 2, 4, 3, 5, 1)
            return p.reshape(B * nh * nw, WIN * WIN, C)
        B, C, H, W = x.shape
        d = C // HEADS
        nh, nw = (H // BLOCK, W // BLOCK)
        qkv = jnp.einsum('bchw,oc->bohw', x, w_qkv)
        q, k, v = jnp.split(qkv, 3, axis=1)
        q = q.reshape(B, C, nh, BLOCK, nw, BLOCK).transpose(0, 2, 4, 3, 5, 1)
        q = q.reshape(B * nh * nw, BLOCK * BLOCK, C) * d ** (-0.5)
        k = _unfold_halo(k, nh, nw)
        v = _unfold_halo(v, nh, nw)
        q = q.reshape(-1, BLOCK * BLOCK, HEADS, d).transpose(0, 2, 1, 3).reshape(-1, BLOCK * BLOCK, d)
        v = v.reshape(-1, WIN * WIN, HEADS, d).transpose(0, 2, 1, 3).reshape(-1, WIN * WIN, d)
        k = k.reshape(-1, WIN, WIN, HEADS, d).transpose(0, 3, 1, 2, 4).reshape(-1, WIN, WIN, d)
        kh, kw = (k[..., :d // 2], k[..., d // 2:])
        k = jnp.concatenate([kh + rel_h, kw + rel_w], axis=-1).reshape(-1, WIN * WIN, d)
        sim = jnp.einsum('bid,bjd->bij', q, k)
        attn = jax.nn.softmax(sim, axis=-1)
        out = jnp.einsum('bij,bjd->bid', attn, v)
        out = out.reshape(B, nh, nw, HEADS, BLOCK, BLOCK, d)
        out = out.transpose(0, 3, 6, 1, 4, 2, 5).reshape(B, HEADS * d, nh * BLOCK, nw * BLOCK)
        return out

    def _L1_conv_ref(x, offset_w, offset_b, mask_w, mask_b, dcn_w):
        import jax, jax.numpy as jnp
        import numpy as np
        K = 3
        STRIDE = 1
        PAD = 1

        def conv2d(x, w, b):
            y = jax.lax.conv_general_dilated(x, w, window_strides=(STRIDE, STRIDE), padding=[(PAD, PAD), (PAD, PAD)], dimension_numbers=('NCHW', 'OIHW', 'NCHW'))
            return y + b[None, :, None, None]

        def deform_conv2d(x, offset, mask, weight):
            B, C, H, W = x.shape
            K2 = K * K
            Ho, Wo = (offset.shape[2], offset.shape[3])
            off = offset.reshape(B, K2, 2, Ho, Wo)
            dy, dx = (off[:, :, 0], off[:, :, 1])
            ky, kx = jnp.meshgrid(jnp.arange(K), jnp.arange(K), indexing='ij')
            ky = ky.reshape(1, K2, 1, 1).astype(x.dtype)
            kx = kx.reshape(1, K2, 1, 1).astype(x.dtype)
            hs = (jnp.arange(Ho) * STRIDE - PAD).astype(x.dtype)[None, None, :, None]
            ws = (jnp.arange(Wo) * STRIDE - PAD).astype(x.dtype)[None, None, None, :]
            py = hs + ky + dy
            px = ws + kx + dx
            y0 = jnp.floor(py)
            x0 = jnp.floor(px)
            ly = py - y0
            lx = px - x0
            y0i = y0.astype(jnp.int32)
            x0i = x0.astype(jnp.int32)
            xt = jnp.transpose(x, (0, 2, 3, 1))
            b_idx = jnp.arange(B).reshape(B, 1, 1, 1)

            def gather(yi, xi):
                valid = (yi >= 0) & (yi < H) & (xi >= 0) & (xi < W)
                yc = jnp.clip(yi, 0, H - 1)
                xc = jnp.clip(xi, 0, W - 1)
                g = xt[b_idx, yc, xc]
                return g * valid[..., None].astype(x.dtype)
            w00 = ((1 - ly) * (1 - lx))[..., None]
            w01 = ((1 - ly) * lx)[..., None]
            w10 = (ly * (1 - lx))[..., None]
            w11 = (ly * lx)[..., None]
            val = gather(y0i, x0i) * w00 + gather(y0i, x0i + 1) * w01 + gather(y0i + 1, x0i) * w10 + gather(y0i + 1, x0i + 1) * w11
            w_r = weight.reshape(weight.shape[0], weight.shape[1], K2)
            out = jnp.einsum('bkhwc,bkhw,ock->bohw', val, mask, w_r)
            return out
        offset = conv2d(x, offset_w, offset_b)
        mask = jax.nn.sigmoid(conv2d(x, mask_w, mask_b))
        return deform_conv2d(x, offset, mask, dcn_w)

    def _L2_conv_ref(x, w1, w2, lin1_w, lin1_b, lin2_w, lin2_b):
        import jax, jax.numpy as jnp
        import numpy as np
        L_SEG, M_CHEB, MODES1, MODES2 = (4, 8, 16, 16)

        def _cft(signals, t_coords, f_points, L, M):
            n = signals.shape[-1]
            seg_len = 1.0 / L
            starts = jnp.linspace(0.0, 1.0, L + 1)[:-1]
            k = jnp.arange(M, dtype=jnp.float32)
            nodes = -jnp.cos((2.0 * k + 1.0) * jnp.pi / (2.0 * M))
            T = jnp.cos(k[:, None] * jnp.arccos(nodes)[None, :])
            w_prime = f_points * (2.0 * jnp.pi * (seg_len / 2.0))
            angle = nodes[:, None] * w_prime[None, :]
            Wr = T @ jnp.cos(angle) * (seg_len / 2.0)
            Wi = T @ -jnp.sin(angle) * (seg_len / 2.0)
            t_seg = starts[:, None] + seg_len / 2.0 * (nodes[None, :] + 1.0)
            right = jnp.clip(jnp.searchsorted(t_coords, t_seg), 0, n - 1)
            left = jnp.clip(right - 1, 0, n - 1)
            tl, tr = (t_coords[left], t_coords[right])
            denom = jnp.where(tr - tl < 1e-08, 1.0, tr - tl)
            wr = (t_seg - tl) / denom
            wl = 1.0 - wr
            seg_sig = wl * signals[..., left] + wr * signals[..., right]
            Sr = jnp.einsum('nclm,mf->nclf', seg_sig, Wr)
            Si = jnp.einsum('nclm,mf->nclf', seg_sig, Wi)
            phase = -2.0 * jnp.pi * starts[:, None] * f_points[None, :]
            cr, ci = (jnp.cos(phase), jnp.sin(phase))
            real = jnp.sum(Sr * cr - Si * ci, axis=2)
            imag = jnp.sum(Sr * ci + Si * cr, axis=2)
            return (real, imag)

        def _cft2d(x, m1, m2, L, M):
            B, C, H, W = x.shape
            tw = jnp.linspace(0.0, 1.0, W)
            fw = jnp.fft.rfftfreq(W, d=1.0 / W)[:m2].astype(jnp.float32)
            xr = x.transpose(0, 2, 1, 3).reshape(B * H, C, W)
            r, i = _cft(xr, tw, fw, L, M)
            r = r.reshape(B, H, C, m2).transpose(0, 2, 1, 3)
            i = i.reshape(B, H, C, m2).transpose(0, 2, 1, 3)
            th = jnp.linspace(0.0, 1.0, H)
            fh = jnp.fft.fftfreq(H, d=1.0 / H).astype(jnp.float32)
            hidx = np.concatenate([np.arange(0, m1 // 2), np.arange(H - (m1 - m1 // 2), H)])
            fsel = fh[hidx]
            rh = r.transpose(0, 3, 1, 2).reshape(B * m2, C, H)
            ih = i.transpose(0, 3, 1, 2).reshape(B * m2, C, H)
            rr, ri = _cft(rh, th, fsel, L, M)
            ir, ii = _cft(ih, th, fsel, L, M)
            real = (rr - ii).reshape(B, m2, C, m1).transpose(0, 2, 3, 1)
            imag = (ri + ir).reshape(B, m2, C, m1).transpose(0, 2, 3, 1)
            return (real, imag)
        m1, m2 = (MODES1, MODES2)
        B, C, H, W = x.shape
        O = w1.shape[1]
        xf = jnp.fft.rfft2(x)
        w1c = w1[..., 0] + 1j * w1[..., 1]
        w2c = w2[..., 0] + 1j * w2[..., 1]
        out_ft = jnp.zeros((B, O, H, W // 2 + 1), jnp.complex64)
        out_ft = out_ft.at[:, :, :m1, :m2].set(jnp.einsum('bixy,ioxy->boxy', xf[:, :, :m1, :m2], w1c))
        out_ft = out_ft.at[:, :, H - m1:, :m2].set(jnp.einsum('bixy,ioxy->boxy', xf[:, :, H - m1:, :m2], w2c))
        x_fno = jnp.fft.irfft2(out_ft, s=(H, W))
        cr, ci = _cft2d(x, m1 // 4, m2 // 4, L_SEG, M_CHEB)
        flat = jnp.stack([cr, ci], axis=-1).reshape(B, -1)
        h = jax.nn.gelu(flat @ lin1_w + lin1_b, approximate=False)
        corr = h @ lin2_w + lin2_b
        return x_fno + corr[:, :, None, None]

    def _L3_conv_ref(x, w_hidden, b_hidden, w_dw, b_dw, w_out, b_out):
        import jax, jax.numpy as jnp
        import numpy as np
        from jax import lax
        PS = 8

        def _conv(x, w, groups=1, padding='VALID'):
            return lax.conv_general_dilated(x, w, window_strides=(1, 1), padding=padding, dimension_numbers=('NCHW', 'OIHW', 'NCHW'), feature_group_count=groups)
        hidden = _conv(x, w_hidden) + b_hidden[None, :, None, None]
        dw = _conv(hidden, w_dw, groups=w_dw.shape[0], padding='SAME') + b_dw[None, :, None, None]
        q, k, v = jnp.split(dw, 3, axis=1)
        B, C, H, W = q.shape
        q_patch = q.reshape(B, C, H // PS, W // PS, PS, PS)
        k_patch = k.reshape(B, C, H // PS, W // PS, PS, PS)
        q_fft = jnp.fft.rfft2(q_patch)
        k_fft = jnp.fft.rfft2(k_patch)
        out = jnp.fft.irfft2(q_fft * k_fft, s=(PS, PS))
        out = out.reshape(B, C, H // PS * PS, W // PS * PS)
        output = v * out
        output = _conv(output, w_out) + b_out[None, :, None, None]
        return output

    def _gn(v, G=32, eps=1e-05):
        B_, C_, H_, W_ = v.shape
        g = v.reshape(B_, G, C_ // G, H_, W_)
        m = jnp.mean(g, axis=(2, 3, 4), keepdims=True)
        s = jnp.var(g, axis=(2, 3, 4), keepdims=True)
        return ((g - m) / jnp.sqrt(s + eps)).reshape(v.shape)

    def _ln_c(v, eps=1e-06):
        m = jnp.mean(v, axis=1, keepdims=True)
        s = jnp.var(v, axis=1, keepdims=True)
        return (v - m) / jnp.sqrt(s + eps)

    def _ln_t(v, eps=1e-05):
        m = jnp.mean(v, axis=-1, keepdims=True)
        s = jnp.var(v, axis=-1, keepdims=True)
        return (v - m) / jnp.sqrt(s + eps)

    def _to_tokens(v):
        B_, C_, H_, W_ = v.shape
        return v.reshape(B_, C_, H_ * W_).transpose(0, 2, 1)

    def _from_tokens(t, like):
        B_, C_, H_, W_ = like.shape
        return t.transpose(0, 2, 1).reshape(B_, C_, H_, W_)
    x = x + _L0_conv_ref(_gn(x), L0_conv_w_qkv, L0_conv_rel_h, L0_conv_rel_w)
    x = x + _L1_conv_ref(_gn(x), L1_conv_offset_w, L1_conv_offset_b, L1_conv_mask_w, L1_conv_mask_b, L1_conv_dcn_w)
    x = x + _L2_conv_ref(_gn(x), L2_conv_w1, L2_conv_w2, L2_conv_lin1_w, L2_conv_lin1_b, L2_conv_lin2_w, L2_conv_lin2_b)
    x = x + _L3_conv_ref(_gn(x), L3_conv_w_hidden, L3_conv_b_hidden, L3_conv_w_dw, L3_conv_b_dw, L3_conv_w_out, L3_conv_b_out)
    return x

_drawn_inputs = setup_inputs


def setup_inputs(seed=0):
    import zlib

    import numpy as np

    out = dict(_drawn_inputs(seed))
    spreads = {'L2_conv_lin1_b': (0.0, 2.0), 'L2_conv_lin2_b': (0.0, 2.0)}
    factors = {'L0_conv_rel_h': 8.0,
     'L0_conv_rel_w': 8.0,
     'L1_conv_offset_b': 8.0,
     'L2_conv_w1': 64.0,
     'L2_conv_w2': 64.0,
     'L3_conv_w_hidden': 8.0,
     'L3_conv_b_hidden': 8.0,
     'L3_conv_w_dw': 8.0,
     'L3_conv_b_dw': 8.0,
     'L3_conv_w_out': 8.0,
     'L3_conv_b_out': 200.0,
     'L2_conv_lin1_w': 26.084,
     'L2_conv_lin2_w': 8.0}
    for name, (base, spread) in spreads.items():
        noise = np.random.default_rng([zlib.crc32(name.encode()), seed]).standard_normal(out[name].shape)
        drawn = base * np.exp(spread * noise) if base else spread * noise
        out[name] = jnp.asarray(drawn.astype(out[name].dtype))
    for name, factor in factors.items():
        out[name] = (out[name] * factor).astype(out[name].dtype)
    return out
```

```python
from contextlib import ExitStack

import numpy as np

import concourse.bass as bass
from concourse import mybir

F=mybir.dt.float32; ALU=mybir.AluOpType; ACT=mybir.ActivationFunctionType; AX=mybir.AxisListType
B, C, H, W = 4, 32, 96, 96
P = B * C
NPIX = H * W
ds = bass.ds


def stage_norm(nc, name, x_sb, xpad, pad):
    wide = xpad.shape[2]
    with ExitStack() as ctx:
        stats = ctx.enter_context(nc.sbuf_tensor(name + "_stats", [P, 18, 6], F))
        agg = ctx.enter_context(nc.sbuf_tensor(name + "_agg", [P, 8], F))
        stats_done = ctx.enter_context(nc.semaphore(name + "_stats_done"))
        var_ready = ctx.enter_context(nc.semaphore(name + "_var_ready"))
        root_ready = ctx.enter_context(nc.semaphore(name + "_root_ready"))
        step_done = ctx.enter_context(nc.semaphore(name + "_step_done"))
        border_done = ctx.enter_context(nc.semaphore(name + "_border_done"))
        block = ctx.enter_context(nc.Block())
        mean, var, std, rstd, t = (agg[:, k:k + 1] for k in range(5))

        @block.gpsimd
        def _(pool):
            nc.gpsimd.memset(xpad[:, 0:pad, :], 0.0)
            nc.gpsimd.memset(xpad[:, H + pad:H + 2 * pad, :], 0.0)
            nc.gpsimd.memset(xpad[:, pad:H + pad, 0:pad], 0.0)
            nc.gpsimd.memset(xpad[:, pad:H + pad, W + pad:wide], 0.0).then_inc(border_done, 1)

        @block.vector
        def _(dve):
            for k in range(18):
                nc.vector.bn_stats(stats[:, k, :], x_sb[:, k * 512:(k + 1) * 512]).then_inc(stats_done, 1)
            dve.wait_ge(stats_done, 18)
            nc.vector.bn_aggr(agg[:, 0:2], stats[:, :, :]).then_inc(step_done, 1)
            dve.wait_ge(step_done, 1)
            nc.vector.tensor_scalar(var, var, 1e-5, None, ALU.add).then_inc(var_ready, 1)
            dve.wait_ge(root_ready, 1)
            nc.vector.reciprocal(rstd, std).then_inc(step_done, 1)
            dve.wait_ge(step_done, 2)
            nc.vector.tensor_tensor(t, rstd, rstd, ALU.mult).then_inc(step_done, 1)
            dve.wait_ge(step_done, 3)
            nc.vector.tensor_tensor(t, t, var, ALU.mult).then_inc(step_done, 1)
            dve.wait_ge(step_done, 4)
            nc.vector.tensor_scalar(t, t, -0.5, 1.5, ALU.mult, ALU.add).then_inc(step_done, 1)
            dve.wait_ge(step_done, 5)
            nc.vector.tensor_tensor(rstd, rstd, t, ALU.mult).then_inc(step_done, 1)
            dve.wait_ge(step_done, 6)
            nc.vector.tensor_scalar(xpad[:, pad:H + pad, pad:W + pad],
                                    x_sb[:, :].rearrange("p (h w) -> p h w", h=H),
                                    mean, rstd, ALU.subtract, ALU.mult)

        @block.scalar
        def _(act):
            act.wait_ge(var_ready, 1)
            nc.scalar.activation(std, var, ACT.Sqrt).then_inc(root_ready, 1)


BLK, HALO, HEADS = 8, 3, 4
D = C // HEADS
WIN = BLK + 2 * HALO
NK = WIN * WIN
HK = NK // 2
NWIN = (H // BLK) * (W // BLK)
Q64 = BLK * BLK


def stage_attention(nc, x_sb, wqkvT, rel, halves, headmask, ident_d):
    PADDED = H + 2 * HALO
    NW = W // BLK
    with ExitStack() as outer:
        sb = lambda n, s, dt=F: outer.enter_context(nc.sbuf_tensor("at_" + n, s, dt))
        xp = sb("xp", [P, PADDED, PADDED])
        stage_norm(nc, "gn0", x_sb, xp, HALO)
        kp = sb("kp", [P, PADDED, PADDED])
        qs = sb("qs", [P, NWIN, Q64])
        wbd = sb("wbd", [P, 3, P])
        relc = sb("relc", [P, WIN])
        relhw = sb("relhw", [P, WIN, WIN])
        half = sb("half", [P, 2])
        hm = sb("hm", [P, HEADS])
        ident = sb("ident", [P, P])
        kw = [sb(f"kw{i}", [P, NK]) for i in range(2)]
        qw = [sb(f"qw{i}", [P, HEADS, Q64]) for i in range(2)]
        xw = [sb(f"xw{i}", [P, NK]) for i in range(2)]
        vs = [sb(f"vs{i}", [HK, 2, P]) for i in range(2)]
        nmx = sb("nmx", [P, B, 2])
        sums = sb("sums", [P, B, 2])
        rs = sb("rs", [P, B, 2])
        probs = [sb(f"probs{b}", [P, 2, NK]) for b in range(B)]
        pts = [sb(f"pts{i}", [HK, 2, 2, P]) for i in range(2)]
        with ExitStack() as ctx:
            sem = lambda n: ctx.enter_context(nc.semaphore("ap_" + n))
            ps = [ctx.enter_context(nc.psum_tensor(f"ap_ps{i}", [P, 512], F)) for i in range(4)]
            zeroed, loaded, rel_step = sem("zeroed"), sem("loaded"), sem("rel_step")
            proj_done, evac_done = sem("proj_done"), sem("evac_done")
            block = ctx.enter_context(nc.Block())

            @block.gpsimd
            def _(pool):
                nc.gpsimd.memset(wbd[:, :, :], 0.0).then_inc(zeroed, 1)

            @block.sync
            def _(sp):
                sp.dma_start(relc[:, :], rel).then_inc(loaded, 16)
                sp.dma_start(half[:, :], halves).then_inc(loaded, 16)
                sp.dma_start(hm[:, :], headmask).then_inc(loaded, 16)
                sp.dma_start(ident[:, :], ident_d).then_inc(loaded, 16)
                sp.wait_ge(zeroed, 1)
                for b in range(B):
                    sp.dma_start(wbd[C * b:C * b + C, :, C * b:C * b + C], wqkvT).then_inc(loaded, 16)

            @block.vector
            def _(dve):
                dve.wait_ge(loaded, 16 * 8)
                nc.vector.tensor_scalar(relhw[:, :, :], relc[:, :].unsqueeze(2).broadcast_to([P, WIN, WIN]),
                                        half[:, 0:1], None, ALU.mult).then_inc(rel_step, 1)
                dve.wait_ge(rel_step, 1)
                nc.vector.scalar_tensor_tensor(relhw[:, :, :], relc[:, :].unsqueeze(1).broadcast_to([P, WIN, WIN]),
                                               half[:, 1:2], relhw[:, :, :], ALU.mult, ALU.add)
                with dve.Fori(0, 17) as i:
                    for s in range(2):
                        dve.wait_ge(proj_done, i * 2 + s + 1)
                        nc.vector.tensor_copy(kp[:, ds(i * 6 + 3 * s, 3), :],
                                              ps[s][:, 0:306].rearrange("p (r c) -> p r c", r=3)).then_inc(evac_done, 1)

            @block.scalar
            def _(act):
                with act.Fori(0, 12) as i:
                    for s in range(2):
                        act.wait_ge(proj_done, i * 2 + (34 + s + 1))
                        nc.scalar.activation(
                            qs[:, ds(i * 12, 12), 32 * s:32 * s + 32].rearrange("p x (r c) -> p x r c", r=4),
                            ps[2 + s][:, 0:384].rearrange("p (r x c) -> p x r c", r=4, x=12),
                            ACT.Copy, scale=D ** -0.5).then_inc(evac_done, 1)

            @block.tensor
            def _(pe):
                pe.wait_ge(loaded, 16 * 8)
                def key_rows(i, s):
                    nc.tensor.matmul(ps[s][:, 0:306], wbd[:, 1, :], xp[:, ds(i * 6 + 3 * s, 3), :],
                                     start=True, stop=True).then_inc(proj_done, 1)
                for s in range(2):
                    key_rows(0, s)
                with pe.Fori(1, 17) as i:
                    for s in range(2):
                        pe.wait_ge(evac_done, i * 2 + (s - 1))
                        key_rows(i, s)

                def query_rows(i, s):
                    nc.tensor.matmul(ps[2 + s][:, 0:384], wbd[:, 0, :],
                                     xp[:, ds(i * 8 + (HALO + 4 * s), 4), HALO:HALO + W],
                                     start=True, stop=True).then_inc(proj_done, 1)
                pe.wait_ge(evac_done, 34)
                for s in range(2):
                    query_rows(0, s)
                with pe.Fori(1, 12) as i:
                    for s in range(2):
                        pe.wait_ge(evac_done, i * 2 + (34 + s - 1))
                        query_rows(i, s)

        with ExitStack() as ctx:
            sem = lambda n: ctx.enter_context(nc.semaphore("at_" + n))
            sc = [ctx.enter_context(nc.psum_tensor(f"at_sc{b}", [P, 512], F)) for b in range(B)]
            pt = [ctx.enter_context(nc.psum_tensor(f"at_pt{i}", [P, 512], F)) for i in range(2)]
            ov = [ctx.enter_context(nc.psum_tensor(f"at_ov{i}", [P, 512], F)) for i in range(2)]
            scores_ready, max_ready, exp_done, inv_ready = sem("scores_ready"), sem("max_ready"), sem("exp_done"), sem("inv_ready")
            normed, pt_ready, pts_ready = sem("normed"), sem("pt_ready"), sem("pts_ready")
            pv_done, v_ready, vs_ready = sem("pv_done"), sem("v_ready"), sem("vs_ready")
            keys_ready, q_ready, xw_ready, res_step = sem("keys_ready"), sem("q_ready"), sem("xw_ready"), sem("res_step")
            block = ctx.enter_context(nc.Block())

            def wait(eng, s, w, k, c):
                if isinstance(w, int):
                    if k * w + c > 0:
                        eng.wait_ge(s, k * w + c)
                else:
                    eng.wait_ge(s, w * k + c)

            def windows(eng, first, body, last):
                body(0, 0)
                body(1, 1)
                with eng.Fori(1, NWIN // 2) as g:
                    body(g * 2, 0)
                    body(g * 2 + 1, 1)

            def walk(eng, body):
                for x in range(0, NW, 2):
                    pass

            @block.gpsimd
            def _(pool):
                def spread(w, s):
                    wait(pool, scores_ready, w, B, B * (-1))
                    nc.gpsimd.tensor_tensor(qw[s][:, :, :], qs[:, ds(w, 1), :].broadcast_to([P, HEADS, Q64]),
                                            hm[:, :].unsqueeze(2).broadcast_to([P, HEADS, Q64]), ALU.mult).then_inc(q_ready, 1)
                def norm(w, s):
                    for b in range(B):
                        wait(pool, inv_ready, w, B, b + 1)
                        nc.gpsimd.tensor_tensor(probs[b][:, :, :], probs[b][:, :, :],
                                                rs[:, b, :].unsqueeze(2).broadcast_to([P, 2, NK]), ALU.mult).then_inc(normed, 1)
                spread(0, 0)
                spread(1, 1)
                norm(0, 0)
                def body(w, s):
                    spread(w + 1, 1 - s)
                    norm(w, s)
                body(1, 1)
                with pool.Fori(1, NWIN // 2 - 1) as g:
                    body(g * 2, 0)
                    body(g * 2 + 1, 1)
                body(NWIN - 2, 0)
                norm(NWIN - 1, 1)

            YX = [(y, x) for y in range(12) for x in range(12)]
            return_hook = None

            @block.vector
            def _(dve):
                def keys(w, y, x, s):
                    wait(dve, scores_ready, w, B, -B)
                    nc.vector.tensor_tensor(kw[s][:, :].rearrange("p (r c) -> p r c", r=WIN),
                                            kp[:, ds(y, WIN), ds(x, WIN)], relhw[:, :, :], ALU.add).then_inc(keys_ready, 1)
                def maxes(w, b):
                    wait(dve, scores_ready, w, B, b + 1)
                    nc.vector.tensor_reduce(nmx[:, b, :], sc[b][:, 0:2 * NK].rearrange("p (j k) -> p j k", j=2),
                                            AX.X, ALU.max, negate=True).then_inc(max_ready, 1)
                def inverse(w, b):
                    wait(dve, exp_done, w, 2 * B, 2 * b + 2)
                    nc.vector.reciprocal(rs[:, b, :], sums[:, b, :]).then_inc(inv_ready, 1)
                def evac(w, b):
                    wait(dve, pt_ready, w, B, b + 1)
                    wait(dve, pv_done, w, B, b - 1)
                    nc.vector.tensor_copy(pts[b % 2][:, :, :, :],
                                          pt[b % 2][0:HK, :].rearrange("p (c j q) -> p c j q", c=2, j=2)).then_inc(pts_ready, 1)
                def residual(w, y, x, s):
                    wait(dve, pv_done, w, B, B)
                    xv = x_sb[:, :].rearrange("p (h w) -> p h w", h=H)[:, ds(y, BLK), ds(x, BLK)]
                    for h in range(HEADS):
                        if h:
                            wait(dve, res_step, w, HEADS, h)
                        nc.vector.scalar_tensor_tensor(
                            xv, ov[s][:, Q64 * h:Q64 * h + Q64].rearrange("p (r c) -> p r c", r=BLK),
                            hm[:, h:h + 1], xv, ALU.mult, ALU.add).then_inc(res_step, 1)
                def window(w, y, x, yn, xn, s, last=False):
                    if not last:
                        keys(w + 1, yn, xn, 1 - s)
                    for b in range(B):
                        maxes(w, b)
                        if b >= 1:
                            inverse(w, b - 1)
                        if b >= 2:
                            evac(w, b - 2)
                    inverse(w, 3)
                    evac(w, 2)
                    evac(w, 3)
                    residual(w, y, x, s)
                keys(0, 0, 0, 0)
                def row(gy, lastrow):
                    y0 = gy * BLK
                    y1 = gy * BLK + BLK
                    for x in range(NW):
                        lastw = lastrow and x == NW - 1
                        yn, xn = (y0, (x + 1) * BLK) if x < NW - 1 else (y1, 0)
                        window(gy * NW + x, y0, x * BLK, yn, xn, x % 2, lastw)
                row(0, False)
                with dve.Fori(1, 11) as gy:
                    row(gy, False)
                row(11, True)

            @block.scalar
            def _(act):
                def crop(w, y, x, s):
                    wait(act, v_ready, w, 1, -1)
                    nc.scalar.copy(xw[s][:, :].rearrange("p (r c) -> p r c", r=WIN),
                                   xp[:, ds(y, WIN), ds(x, WIN)]).then_inc(xw_ready, 1)
                def values(w, s):
                    wait(act, v_ready, w, 1, 1)
                    wait(act, pv_done, w, B, -B)
                    nc.scalar.copy(vs[s][:, :, :], ov[s][0:HK, 256:512].rearrange("p (c o) -> p c o", c=2)).then_inc(vs_ready, 1)
                def exps(w, b):
                    wait(act, max_ready, w, B, b + 1)
                    wait(act, pt_ready, w, B, b + 1 - B)
                    wait(act, inv_ready, w, B, b + 1 - B)
                    for j in range(2):
                        nc.scalar.activation(probs[b][:, j, :], sc[b][:, NK * j:NK * j + NK], ACT.Exp,
                                             bias=nmx[:, b, j:j + 1], accum_out=sums[:, b, j:j + 1]).then_inc(exp_done, 1)
                crop(0, 0, 0, 0)
                def row(gy, lastrow):
                    for x in range(NW):
                        w = gy * NW + x
                        s = x % 2
                        if not (lastrow and x == NW - 1):
                            if x < NW - 1:
                                crop(w + 1, gy * BLK, (x + 1) * BLK, 1 - s)
                            else:
                                crop(w + 1, gy * BLK + BLK, 0, 1 - s)
                        exps(w, 0)
                        exps(w, 1)
                        values(w, s)
                        exps(w, 2)
                        exps(w, 3)
                row(0, False)
                with act.Fori(1, 11) as gy:
                    row(gy, False)
                row(11, True)

            @block.tensor
            def _(pe):
                def score(w, b, s):
                    if b == 0:
                        wait(pe, keys_ready, w, 1, 1)
                        wait(pe, q_ready, w, 1, 1)
                    wait(pe, exp_done, w, 2 * B, 2 * b + 2 - 2 * B)
                    for j in range(2):
                        mm = nc.tensor.matmul(sc[b][:, NK * j:NK * j + NK], qw[s][C * b:C * b + C, 2 * j:2 * j + 2, :],
                                              kw[s][C * b:C * b + C, :], start=True, stop=True)
                    mm.then_inc(scores_ready, 1)
                def value(w, s):
                    wait(pe, xw_ready, w, 1, 1)
                    wait(pe, res_step, w, HEADS, -2 * HEADS + HEADS)
                    for c in range(2):
                        mm = nc.tensor.matmul(ov[s][0:HK, 256 + P * c:256 + P * c + P], xw[s][:, HK * c:HK * c + HK],
                                              wbd[:, 2, :], start=True, stop=True)
                    mm.then_inc(v_ready, 1)
                def transposed(w, b):
                    wait(pe, normed, w, B, b + 1)
                    wait(pe, pts_ready, w, B, b - 1)
                    for c in range(2):
                        for j in range(2):
                            o = (2 * c + j) * P
                            mm = nc.tensor.transpose(pt[b % 2][0:HK, o:o + P], probs[b][:, j, HK * c:HK * c + HK], ident[:, :])
                    mm.then_inc(pt_ready, 1)
                def weigh(w, b, s):
                    if b == 0:
                        wait(pe, vs_ready, w, 1, 1)
                    wait(pe, pts_ready, w, B, b + 1)
                    for c in range(2):
                        mm = nc.tensor.matmul(ov[s][C * b:C * b + C, 0:256], vs[s][:, c, C * b:C * b + C],
                                              pts[b % 2][:, c, :, :], start=(c == 0), stop=(c == 1))
                    mm.then_inc(pv_done, 1)
                value(0, 0)
                for b in range(B):
                    score(0, b, 0)
                def window(w, s, last=False):
                    if not last:
                        value(w + 1, 1 - s)
                    for b in range(B):
                        transposed(w, b)
                        if not last:
                            score(w + 1, b, 1 - s)
                        if b:
                            weigh(w, b - 1, s)
                    weigh(w, B - 1, s)
                window(0, 0)
                window(1, 1)
                with pe.Fori(1, NWIN // 2 - 1) as g:
                    window(g * 2, 0)
                    window(g * 2 + 1, 1)
                window(NWIN - 2, 0)
                window(NWIN - 1, 1, True)


def host_consts():
    p = np.arange(P)
    return dict(
        halves=np.stack([(p % D < D // 2), (p % D >= D // 2)], 1).astype(np.float32),
        headmask=((p % C)[:, None] // D == np.arange(HEADS)[None]).astype(np.float32),
        ident=np.eye(P, dtype=np.float32))



def wait(eng, s, w, k, c):
    if isinstance(w, int):
        if k * w + c > 0:
            eng.wait_ge(s, k * w + c)
    else:
        eng.wait_ge(s, w * k + c)



I32 = mybir.dt.int32
U32 = mybir.dt.uint32
TAPS = 9
TR = 8
NSTRIP, TPS = H // TR, TR * W // P
UNITS = TPS * B
EDGE = 2
TY, TX = H + 2 * EDGE, 112
TROWS = TY - 1
ENTRY = 4 * C
GROWS = 9
RING = 4


def stage_deform(nc, x_sb, convw, biasr, coord, base_ix, dcn, ident_d, xn_d, table):
    LOADS = 16 * 3 * B
    with ExitStack() as outer:
        sb = lambda n, s, dt=F: outer.enter_context(nc.sbuf_tensor("df_" + n, s, dt))
        ident = sb("ident", [P, P])
        wc = sb("wc", [3 * C, 3, 27])
        wd = sb("wd", [P, TAPS, C])
        base = sb("base", [P, UNITS, 2, TAPS])
        bias = sb("bias", [P, 27])
        ixb = sb("ixb", [P, UNITS, TAPS])
        with ExitStack() as ctx:
            xp = ctx.enter_context(nc.sbuf_tensor("df_xp", [P, TY, TX], F))
            stage_norm(nc, "gn1", x_sb, xp, EDGE)
            sem = lambda n: ctx.enter_context(nc.semaphore("dt_" + n))
            rows = [ctx.enter_context(nc.sbuf_tensor(f"dt_rows{i}", [P, GROWS + 1, TX], F)) for i in range(2)]
            stage = [ctx.enter_context(nc.sbuf_tensor(f"dt_stage{i}", [TX, GROWS, B, 2, C], F)) for i in range(2)]
            zeros = ctx.enter_context(nc.sbuf_tensor("dt_zeros", [1, 64], F))
            ps = [ctx.enter_context(nc.psum_tensor(f"dt_ps{i}", [P, 4, 512], F)) for i in range(2)]
            zeros_ready, lower, filled, loaded, written = sem("zeros_ready"), sem("lower"), sem("filled"), sem("loaded"), sem("written")
            rows_ready, turned, staged, stored = sem("rows_ready"), sem("turned"), sem("staged"), [sem("stored0"), sem("stored1")]
            block = ctx.enter_context(nc.Block())
            NG = (TY - 1) // GROWS
            assert NG * GROWS == TY - 1 and NG % 2 == 1

            @block.sync
            def _(sp):
                for dst, src in ((ident[:, :], ident_d), (wc[:, :, :], convw), (wd[:, :, :], dcn),
                                 (base[:, :, :, :], coord), (bias[:, :], biasr), (ixb[:, :, :], base_ix)):
                    sp.dma_start(dst, src).then_inc(loaded, 16)
                sp.dma_start(xn_d, xp[:, :, 0:TY]).then_inc(written, 16)

                sp.wait_ge(zeros_ready, 1)
                sp.dma_start(table[0:1, 0:64], zeros[0:1, :]).then_inc(written, 16)
                sp.dma_start(table[B * TROWS * TX:B * TROWS * TX + 1, 64:128], zeros[0:1, :]).then_inc(written, 16)

                def store(g, s, n):
                    wait(sp, lower, g, 1, 1)
                    wait(sp, staged, g, 1, 1)
                    for b in range(B):
                        for half in range(2):
                            dst = table[ds(g * (GROWS * TX) + (1 - half + b * TROWS * TX), GROWS * TX), 64 * half:64 * half + 64]
                            sp.dma_start(dst.rearrange("(y x) c -> x y c", x=TX),
                                         stage[s][:, :, b, :, :].rearrange("x y r c -> x y (r c)")).then_inc(stored[s], 16)
                store(0, 0, 0)
                with sp.Fori(0, NG // 2) as h:
                    store(h * 2 + 1, 1, 0)
                    store(h * 2 + 2, 0, 0)
                sp.wait_ge(written, 48)
                sp.wait_ge(loaded, 16 * 6)
                sp.wait_ge(stored[0], 128 * (NG // 2 + 1))
                sp.wait_ge(stored[1], 128 * (NG // 2))

            @block.gpsimd
            def _(pool):
                nc.gpsimd.memset(zeros[:, :], 0.0).then_inc(zeros_ready, 1)
                pool.wait_ge(loaded, 16 * 6)
                nc.gpsimd.tensor_tensor(base[:, :, :, :].rearrange("p u a k -> p u (a k)"), base[:, :, :, :].rearrange("p u a k -> p u (a k)"),
                                        bias[:, 0:18].unsqueeze(1).broadcast_to([P, UNITS, 18]), ALU.add).then_inc(filled, 1)

            @block.scalar
            def _(act):
                def take(g, s, j):
                    wait(act, turned, g, 1, -1)
                    nc.scalar.copy(rows[s][:, :, :], xp[:, ds(g * GROWS, GROWS + 1), :]).then_inc(rows_ready, 1)

                def put(g, s, j):
                    wait(act, lower, g, 1, 1)
                    if j is not None:
                        wait(act, stored[s], j, 128, 0)
                    nc.scalar.copy(stage[s][:, :, :, 0, :],
                                   ps[s][0:TX, :, :].rearrange("p k n -> p (k n)")[:, 0:GROWS * P].rearrange("p (y b c) -> p y b c", y=GROWS, b=B)).then_inc(staged, 1)
                take(0, 0, 0)
                take(1, 1, 0)
                put(0, 0, None)
                take(2, 0, 0)
                put(1, 1, None)
                with act.Fori(1, NG // 2) as h:
                    take(h * 2 + 1, 1, 0)
                    put(h * 2, 0, h)
                    take(h * 2 + 2, 0, 0)
                    put(h * 2 + 1, 1, h)
                put(NG - 1, 0, NG // 2)

            @block.vector
            def _(dve):
                def put(g, s, j):
                    wait(dve, turned, g, 1, 1)
                    if j is not None:
                        wait(dve, stored[s], j, 128, 0)
                    nc.vector.tensor_copy(stage[s][:, :, :, 1, :],
                                          ps[s][0:TX, :, :].rearrange("p k n -> p (k n)")[:, P:(GROWS + 1) * P].rearrange("p (y b c) -> p y b c", y=GROWS, b=B)).then_inc(lower, 1)
                put(0, 0, None)
                put(1, 1, None)
                with dve.Fori(1, NG // 2) as h:
                    put(h * 2, 0, h)
                    put(h * 2 + 1, 1, h)
                put(NG - 1, 0, NG // 2)

            @block.tensor
            def _(pe):
                pe.wait_ge(loaded, 16 * 6)
                def turn(g, s):
                    wait(pe, rows_ready, g, 1, 1)
                    wait(pe, staged, g, 1, -1)
                    for y in range(GROWS + 1):
                        o = y * P
                        mm = nc.tensor.transpose(ps[s][0:TX, o // 512, o % 512:o % 512 + P], rows[s][:, y, :], ident[:, :])
                    mm.then_inc(turned, 1)
                turn(0, 0)
                turn(1, 1)
                with pe.Fori(1, NG // 2) as h:
                    turn(h * 2, 0)
                    turn(h * 2 + 1, 1)
                turn(NG - 1, 0)

        with ExitStack() as ctx:
            sem = lambda n: ctx.enter_context(nc.semaphore("df_" + n))
            sbc = lambda n, s, dt=F: ctx.enter_context(nc.sbuf_tensor("df_" + n, s, dt))
            psum = lambda n, s: ctx.enter_context(nc.psum_tensor("df_" + n, s, F))
            xs = [sbc(f"xs{i}", [3 * C, B, TR + 2, W]) for i in range(2)]
            pos = sbc("pos", [P, UNITS, 2, TAPS])
            logit = sbc("logit", [P, UNITS, TAPS])
            msk = sbc("msk", [P, UNITS, TAPS])
            ii = sbc("ii", [P, UNITS, 2, TAPS], I32)
            fl = sbc("fl", [P, UNITS, 2, TAPS])
            lt = sbc("lt", [P, UNITS, 2, TAPS])
            ixf = sbc("ixf", [P, UNITS, TAPS])
            gy = sbc("gy", [P, 2, UNITS, TAPS])
            ixu = [sbc(f"ixu{i}", [P, UNITS, TAPS], U32) for i in range(2)]
            wt = [sbc(f"wt{i}", [P, UNITS, TAPS, 4]) for i in range(2)]
            gat = [sbc(f"gat{i}", [P, TAPS, 4, C]) for i in range(RING)]
            gts = [sbc(f"gts{i}", [P, TAPS, P]) for i in range(2)]
            cps = [psum(f"cps{i}", [P, 512]) for i in range(2)]
            tps = psum("tps", [P, 3, 512])
            ops = [psum(f"ops{i}", [P, 512]) for i in range(2)]
            strip_in = [sem("strip_in0"), sem("strip_in1")]
            conv_done, conv_read, logit_ready, mask_ready, chain = sem("conv_done"), sem("conv_read"), sem("logit_ready"), sem("mask_ready"), sem("chain")
            coords_ready, slot_free = sem("coords_ready"), sem("slot_free")
            gathered = [sem(f"gathered{i}") for i in range(RING)]
            weighted, turned, turned_sb, mixed, added = sem("weighted"), sem("turned"), sem("turned_sb"), sem("mixed"), sem("added")
            block = ctx.enter_context(nc.Block())

            def strips(eng, body):
                body(0, 0, True, False)
                with eng.Fori(0, NSTRIP // 2 - 1) as h:
                    body(h * 2 + 1, 1, False, False)
                    body(h * 2 + 2, 0, False, False)
                body(NSTRIP - 1, 1, False, True)

            @block.sync
            def _(sp):
                def load(s, i, first, last):
                    wait(sp, conv_done, s, 1, -1)
                    for dx in range(3):
                        for b in range(B):
                            sp.dma_start(xs[i][C * dx:C * dx + C, b, :, :],
                                         xn_d[C * b:C * b + C, ds(s * TR + EDGE - 1, TR + 2), EDGE - 1 + dx:EDGE - 1 + dx + W]
                                         ).then_inc(strip_in[i], 16)
                strips(sp, load)

            @block.tensor
            def _(pe):
                def conv_strip(s, i, half):
                    wait(pe, strip_in[i], half, LOADS, LOADS)
                    wait(pe, conv_read, s, 4, 0)
                    for t in range(TPS):
                        for b in range(B):
                            u = t * B + b
                            for dy in range(3):
                                mm = nc.tensor.matmul(cps[u // 12][:, 27 * (u % 12):27 * (u % 12) + 27],
                                                      xs[i][:, b, :, :].rearrange("p r c -> p (r c)")[:, dy * W + P * t:dy * W + P * t + P], wc[:, dy, :],
                                                      start=(dy == 0), stop=(dy == 2))
                    mm.then_inc(conv_done, 1)

                def turn(s, u):
                    wait(pe, weighted, s, UNITS, u + 1)
                    wait(pe, turned_sb, s, UNITS, u)
                    for k in range(TAPS):
                        mm = nc.tensor.transpose(tps[:, k // 4, P * (k % 4):P * (k % 4) + P], gat[u % RING][:, k, :, :], ident[:, :])
                    mm.then_inc(turned, 1)

                def mix(s, u):
                    t, b = u // B, u % B
                    wait(pe, turned_sb, s, UNITS, u + 1)
                    if b == 0:
                        wait(pe, added, s, TPS, t - 1)
                    for k in range(TAPS):
                        mm = nc.tensor.matmul(ops[t % 2][C * b:C * b + C, 0:P], wd[:, k, :], gts[u % 2][:, k, :],
                                              start=(k == 0), stop=(k == TAPS - 1))
                    mm.then_inc(mixed, 1)

                def strip(s, i, half, last):
                    if not last:
                        conv_strip(s + 1, 1 - i, half)
                    for u in range(UNITS):
                        turn(s, u)
                        mix(s, u)
                conv_strip(0, 0, 0)
                strip(0, 0, 0, False)
                with pe.Fori(0, NSTRIP // 2 - 1) as h:
                    strip(h * 2 + 1, 1, h + 1, False)
                    strip(h * 2 + 2, 0, h + 1, False)
                strip(NSTRIP - 1, 1, 0, True)

            @block.scalar
            def _(act):
                def sigmoid(s):
                    wait(act, logit_ready, s, 1, 1)
                    nc.scalar.activation(msk[:, :, :], logit[:, :, :], ACT.Sigmoid).then_inc(mask_ready, 1)

                def strip(s, i, first, last):
                    if not last:
                        sigmoid(s + 1)
                    for u in range(UNITS):
                        wait(act, turned, s, UNITS, u + 1)
                        wait(act, mixed, s, UNITS, u - 1)
                        nc.scalar.copy(gts[u % 2][:, :, :].rearrange("p k n -> p (k n)"),
                                       tps[:, :, :].rearrange("p k n -> p (k n)")[:, 0:TAPS * P]).then_inc(turned_sb, 1)
                sigmoid(0)
                strips(act, strip)

            @block.gpsimd
            def _(pool):
                def strip(s, i, first, last):
                    wait(pool, coords_ready, s, 1, 1)
                    for u in range(UNITS):
                        wait(pool, turned, s, UNITS, u + 1 - RING)
                        pool.sem_inc(slot_free, 1)
                        for k in range(TAPS):
                            pool.indirect_dma_start(gat[u % RING][:, k, :, :].rearrange("p a c -> p (a c)"), None, table,
                                                    bass.IndirectOffsetOnAxis(ap=ixu[i][:, u, k:k + 1], axis=0)
                                                    ).then_inc(gathered[u % RING], 16)
                strips(pool, strip)

            @block.vector
            def _(dve):
                STEPS = 13

                def coords(s, i):
                    n = [0]

                    def link(ins):
                        n[0] += 1
                        ins.then_inc(chain, 1)
                        wait(dve, chain, s, STEPS, n[0])
                    wait(dve, conv_done, s, 1, 1)
                    wait(dve, mask_ready, s, 1, 0)
                    for h in range(2):
                        u0 = 12 * h
                        conv = cps[h][:, 0:324].rearrange("p (u o) -> p u o", u=12)
                        nc.vector.tensor_tensor(pos[:, u0:u0 + 12, :, :].rearrange("p u a k -> p u (a k)"), conv[:, :, 0:18],
                                                base[:, u0:u0 + 12, :, :].rearrange("p u a k -> p u (a k)"), ALU.add).then_inc(conv_read, 1)
                        nc.vector.tensor_tensor(logit[:, u0:u0 + 12, :], conv[:, :, 18:27],
                                                bias[:, 18:27].unsqueeze(1).broadcast_to([P, 12, 9]), ALU.add).then_inc(conv_read, 1)
                    wait(dve, conv_read, s, 4, 4)
                    nc.vector.tensor_scalar(base[:, :, 0, :], base[:, :, 0, :], float(TR), None, ALU.add).then_inc(logit_ready, 1)
                    link(nc.vector.tensor_scalar(pos[:, :, :, :], pos[:, :, :, :], -float(EDGE), float(H), ALU.max, ALU.min))
                    link(nc.vector.tensor_copy(ii[:, :, :, :], pos[:, :, :, :]))
                    link(nc.vector.tensor_copy(fl[:, :, :, :], ii[:, :, :, :]))
                    link(nc.vector.tensor_tensor(lt[:, :, :, :], pos[:, :, :, :], fl[:, :, :, :], ALU.is_lt))
                    link(nc.vector.tensor_tensor(fl[:, :, :, :], fl[:, :, :, :], lt[:, :, :, :], ALU.subtract))
                    link(nc.vector.tensor_tensor(pos[:, :, :, :], pos[:, :, :, :], fl[:, :, :, :], ALU.subtract))
                    link(nc.vector.scalar_tensor_tensor(ixf[:, :, :], fl[:, :, 0, :], float(TX), fl[:, :, 1, :], ALU.mult, ALU.add))
                    wait(dve, mask_ready, s, 1, 1)
                    link(nc.vector.tensor_tensor(ixu[i][:, :, :], ixf[:, :, :], ixb[:, :, :], ALU.add))
                    link(nc.vector.tensor_tensor(gy[:, 1, :, :], pos[:, :, 0, :], msk[:, :, :], ALU.mult))
                    link(nc.vector.tensor_tensor(gy[:, 0, :, :], msk[:, :, :], gy[:, 1, :, :], ALU.subtract))
                    link(nc.vector.tensor_tensor(wt[i][:, :, :, 3], gy[:, 1, :, :], pos[:, :, 1, :], ALU.mult))
                    link(nc.vector.tensor_tensor(wt[i][:, :, :, 2], gy[:, 0, :, :], pos[:, :, 1, :], ALU.mult))
                    link(nc.vector.tensor_tensor(wt[i][:, :, :, 1], gy[:, 1, :, :], wt[i][:, :, :, 3], ALU.subtract))
                    assert n[0] == STEPS
                    nc.vector.tensor_tensor(wt[i][:, :, :, 0], gy[:, 0, :, :], wt[i][:, :, :, 2], ALU.subtract).then_inc(coords_ready, 1)

                def strip(s, i, first, last):
                    wait(dve, coords_ready, s, 1, 1)
                    if not last:
                        coords(s + 1, 1 - i)
                    for u in range(UNITS):
                        wait(dve, gathered[u % RING], s, 16 * TAPS * (UNITS // RING), 16 * TAPS * (u // RING + 1))
                        nc.vector.tensor_tensor(gat[u % RING][:, :, :, :], gat[u % RING][:, :, :, :],
                                                wt[i][:, u, :, :].unsqueeze(3).broadcast_to([P, TAPS, 4, C]), ALU.mult).then_inc(weighted, 1)
                        if u % B == 1 and u > B:
                            residual(s, u // B - 1)
                    residual(s, TPS - 1)

                def residual(s, t):
                    wait(dve, mixed, s, UNITS, B * t + B)
                    xv = x_sb[:, ds(s * (TR * W) + P * t, P)]
                    nc.vector.tensor_tensor(xv, xv, ops[t % 2][:, 0:P], ALU.add).then_inc(added, 1)
                coords(0, 0)
                strips(dve, strip)


def host_l1(ow, ob, mw, mb, dw):
    wk = np.concatenate([ow[0::2], ow[1::2], mw], 0)
    convw = np.ascontiguousarray(wk.transpose(3, 1, 2, 0).reshape(3 * C, 3, 27))
    bias = np.tile(np.concatenate([ob[0::2], ob[1::2], mb]), (P, 1))
    dcn = np.tile(dw.reshape(C, C, 9).transpose(1, 2, 0), (4, 1, 1))
    p = np.arange(P)
    k = np.arange(9)
    u = np.arange(UNITS)
    px = P * (u // B)[None, :] + p[:, None]
    r, c = px // W, px % W
    coord = np.zeros((P, UNITS, 2, 9), np.float32)
    coord[:, :, 0, :] = r[:, :, None] - 1 + (k // 3)[None, None]
    coord[:, :, 1, :] = c[:, :, None] - 1 + (k % 3)[None, None]
    ixb = np.zeros((P, UNITS, 9), np.float32)
    ixb[:] = (1 + (u % B) * TROWS * TX + EDGE * TX + EDGE)[None, :, None]
    return dict(convw=convw, bias=np.ascontiguousarray(bias), coord=coord, ixb=ixb, dcn=np.ascontiguousarray(dcn))


KX, KY = 32, 16
M1 = M2 = 4
L1_IN, HIDN = C * M1 * M2 * 2, 128
FW = 2 * KY + 2 * M2
NG = 4
GX = KX // NG
MODES = GX * KY
ZN = KX * KY * 2
LRows = 8


def stage_fourier(nc, x_sb, fw_d, fh_d, ch_d, ih_d, iw_d, w1, w2, lin1, b1, lin2, b2, ident_d):
    with ExitStack() as outer:
        sb = lambda n, s, dt=F: outer.enter_context(nc.sbuf_tensor("fo_" + n, s, dt))
        ident = sb("ident", [P, P])
        fw = sb("fw", [W, FW])
        fh = sb("fh", [H, 2, 2 * KX])
        ch = sb("ch", [H, 2, 2 * M1])
        ih = sb("ih", [2 * KX, 2 * H])
        iw = sb("iw", [P, 4, W])
        wts = sb("wts", [P, C, GX, KY * 2])
        l1w = sb("l1w", [C, 2 * M1 * M2, HIDN])
        b1s = sb("b1s", [HIDN, 1])
        l2w = sb("l2w", [HIDN, C])
        b2s = sb("b2s", [P, 1])
        y = sb("y", [P, FW, H])
        yt = sb("yt", [H, FW, P])
        z = sb("z", [P, KX, KY, 2])
        zi = sb("zi", [P, B, GX, KY * 2])
        flat = sb("flat", [P, M1, M2, 2])
        fl = sb("fl", [C, B, 2 * M1 * M2])
        corr = sb("corr", [P, 1])
        with ExitStack() as ctx:
            sem = lambda n: ctx.enter_context(nc.semaphore("ff_" + n))
            sbc = lambda n, s, dt=F: ctx.enter_context(nc.sbuf_tensor("ff_" + n, s, dt))
            psum = lambda n, s: ctx.enter_context(nc.psum_tensor("ff_" + n, s, F))
            stats = sbc("stats", [P, 18, 6])
            agg = sbc("agg", [P, 8])
            rows = [sbc(f"rows{i}", [P, LRows, W]) for i in range(2)]
            xt = [sbc(f"xt{i}", [W, LRows, P]) for i in range(2)]
            tps = [psum(f"tps{i}", [P, 2, 512]) for i in range(2)]
            yps = [psum(f"yps{i}", [P, 512]) for i in range(2)]
            zps = [psum(f"zps{i}", [P, 512]) for i in range(2)]
            loaded, moved, root_ready, var_ready, step = sem("loaded"), sem("moved"), sem("root_ready"), sem("var_ready"), sem("step")
            stats_done = sem("stats_done")
            rows_ready, turned, xt_ready, y_done, y_sb = sem("rows_ready"), sem("turned"), sem("xt_ready"), sem("y_done"), sem("y_sb")
            yturned, yt_sb, z_done, z_sb = sem("yturned"), sem("yt_sb"), sem("z_done"), sem("z_sb")
            block = ctx.enter_context(nc.Block())
            mean, var, std, rstd, t = (agg[:, k:k + 1] for k in range(5))
            G8 = H // LRows

            @block.sync
            def _(sp):
                loads = [(ident[:, :], ident_d), (fw[:, :], fw_d), (fh[:, :, :], fh_d), (ch[:, :, :], ch_d), (ih[:, :], ih_d),
                         (iw[:, :, :], iw_d), (l1w[:, :, :], lin1.rearrange("(c j) n -> c j n", c=C)), (b1s[:, :], b1), (l2w[:, :], lin2), (b2s[:, :], b2)]
                for dst, src in loads:
                    sp.dma_start(dst, src).then_inc(loaded, 16)
                for g in range(NG):
                    w = (w1, w2)[g // 2]
                    k0 = GX * (g % 2)
                    sp.dma_start(wts[C * g:C * g + C, :, :, :].rearrange("i o k y -> i o (k y)"),
                                 w[:, :, k0:k0 + GX, :, :].rearrange("i o k y r -> i o (k y r)")).then_inc(loaded, 16)
                sp.wait_ge(loaded, 224)
                sp.wait_ge(z_sb, 3)
                for b in range(B):
                    for g in range(NG):
                        sp.dma_start(zi[C * g:C * g + C, b, :, :].rearrange("i k y -> i (k y)"),
                                     z[C * b:C * b + C, GX * g:GX * g + GX, :, :].rearrange("i k y r -> i (k y r)")).then_inc(moved, 16)
                    sp.dma_start(fl[:, b, :], flat[C * b:C * b + C, :, :, :].rearrange("c a b r -> c (a b r)")).then_inc(moved, 16)
                sp.wait_ge(moved, 16 * B * (NG + 1))

            @block.vector
            def _(dve):
                for k in range(18):
                    nc.vector.bn_stats(stats[:, k, :], x_sb[:, k * 512:(k + 1) * 512]).then_inc(stats_done, 1)
                dve.wait_ge(stats_done, 18)
                nc.vector.bn_aggr(agg[:, 0:2], stats[:, :, :]).then_inc(step, 1)
                dve.wait_ge(step, 1)
                nc.vector.tensor_scalar(var, var, 1e-5, None, ALU.add).then_inc(var_ready, 1)
                dve.wait_ge(root_ready, 1)
                nc.vector.reciprocal(rstd, std).then_inc(step, 1)
                dve.wait_ge(step, 2)
                nc.vector.tensor_tensor(t, rstd, rstd, ALU.mult).then_inc(step, 1)
                dve.wait_ge(step, 3)
                nc.vector.tensor_tensor(t, t, var, ALU.mult).then_inc(step, 1)
                dve.wait_ge(step, 4)
                nc.vector.tensor_scalar(t, t, -0.5, 1.5, ALU.mult, ALU.add).then_inc(step, 1)
                dve.wait_ge(step, 5)
                nc.vector.tensor_tensor(rstd, rstd, t, ALU.mult).then_inc(step, 1)
                dve.wait_ge(step, 6)

                def normalise(g, s):
                    wait(dve, turned, g, 1, -1)
                    nc.vector.tensor_scalar(rows[s][:, :, :].rearrange("p r c -> p (r c)"), x_sb[:, ds(g * (LRows * W), LRows * W)],
                                            mean, rstd, ALU.subtract, ALU.mult).then_inc(rows_ready, 1)

                def keep(g, s):
                    wait(dve, turned, g, 1, 1)
                    wait(dve, y_done, g, 1, -1)
                    nc.vector.tensor_copy(xt[s][:, :, :].rearrange("p r n -> p (r n)"), tps[s][0:W, :, :].rearrange("p k n -> p (k n)")).then_inc(xt_ready, 1)
                normalise(0, 0)
                normalise(1, 1)
                keep(0, 0)
                with dve.Fori(0, G8 // 2 - 1) as h:
                    normalise(h * 2 + 2, 0)
                    keep(h * 2 + 1, 1)
                    normalise(h * 2 + 3, 1)
                    keep(h * 2 + 2, 0)
                keep(G8 - 1, 1)
                for q in range(FW // 4):
                    dve.wait_ge(yturned, q + 1)
                    nc.vector.tensor_copy(yt[:, 4 * q:4 * q + 4, :].rearrange("p f n -> p (f n)"), tps[q % 2][0:H, 0, :]).then_inc(yt_sb, 1)

            @block.scalar
            def _(act):
                act.wait_ge(var_ready, 1)
                nc.scalar.activation(std, var, ACT.Sqrt).then_inc(root_ready, 1)

                def keep(g, s):
                    wait(act, y_done, g, 1, 1)
                    nc.scalar.copy(y[:, :, ds(g * LRows, LRows)], yps[s][:, 0:LRows * FW].rearrange("p (r f) -> p f r", r=LRows)).then_inc(y_sb, 1)
                with act.Fori(0, G8 // 2) as h:
                    keep(h * 2, 0)
                    keep(h * 2 + 1, 1)
                for k in range(2):
                    act.wait_ge(z_done, k + 1)
                    nc.scalar.copy(z[:, :, 8 * k:8 * k + 8, :], zps[k][:, :].rearrange("p (y k r) -> p k y r", y=8, r=2)).then_inc(z_sb, 1)
                act.wait_ge(z_done, 3)
                nc.scalar.copy(flat[:, :, :, :], yps[0][:, 0:2 * M1 * M2].rearrange("p (b a r) -> p a b r", b=M2, r=2)).then_inc(z_sb, 1)

            @block.tensor
            def _(pe):
                pe.wait_ge(loaded, 224)

                def turn(g, s):
                    wait(pe, rows_ready, g, 1, 1)
                    wait(pe, xt_ready, g, 1, -1)
                    for r in range(LRows):
                        mm = nc.tensor.transpose(tps[s][0:W, r // 4, P * (r % 4):P * (r % 4) + P], rows[s][:, r, :], ident[:, :])
                    mm.then_inc(turned, 1)

                def along_width(g, s):
                    wait(pe, xt_ready, g, 1, 1)
                    wait(pe, y_sb, g, 1, -1)
                    for r in range(LRows):
                        mm = nc.tensor.matmul(yps[s][:, FW * r:FW * r + FW], xt[s][:, r, :], fw[:, :], start=True, stop=True)
                    mm.then_inc(y_done, 1)
                turn(0, 0)
                turn(1, 1)
                along_width(0, 0)
                with pe.Fori(0, G8 // 2 - 1) as h:
                    turn(h * 2 + 2, 0)
                    along_width(h * 2 + 1, 1)
                    turn(h * 2 + 3, 1)
                    along_width(h * 2 + 2, 0)
                along_width(G8 - 1, 1)
                pe.wait_ge(y_sb, G8)
                for q in range(FW // 4):
                    if q == 0:
                        pe.wait_ge(xt_ready, G8)
                    if q >= 2:
                        pe.wait_ge(yt_sb, q - 1)
                    for f in range(4):
                        mm = nc.tensor.transpose(tps[q % 2][0:H, 0, P * f:P * f + P], y[:, 4 * q + f, :], ident[:, :])
                    mm.then_inc(yturned, 1)
                for k in range(KY):
                    pe.wait_ge(yt_sb, (2 * k + 1) // 4 + 1)
                    for part in range(2):
                        mm = nc.tensor.matmul(zps[k // 8][:, 64 * (k % 8):64 * (k % 8) + 64], yt[:, 2 * k + part, :], fh[:, part, :],
                                              start=(part == 0), stop=(part == 1))
                    if k % 8 == 7:
                        mm.then_inc(z_done, 1)
                pe.wait_ge(yt_sb, FW // 4)
                for k in range(M2):
                    for part in range(2):
                        mm = nc.tensor.matmul(yps[0][:, 8 * k:8 * k + 8], yt[:, 2 * KY + M2 * part + k, :], ch[:, part, :],
                                              start=(part == 0), stop=(part == 1))
                mm.then_inc(z_done, 1)

        with ExitStack() as ctx:
            sem = lambda n: ctx.enter_context(nc.semaphore("fb_" + n))
            sbc = lambda n, s, dt=F: ctx.enter_context(nc.sbuf_tensor("fb_" + n, s, dt))
            psum = lambda n, s: ctx.enter_context(nc.psum_tensor("fb_" + n, s, F))
            wst = [sbc(f"wst{i}", [P, C, KY, 2]) for i in range(2)]
            zst = [sbc(f"zst{i}", [P, 2, B, KY, 2]) for i in range(2)]
            o = sbc("o", [P, B, GX, KY * 2])
            hb = sbc("hb", [HIDN, B])
            g = sbc("g", [P, H, KY, 2])
            z2 = sbc("z2", [P, KY, 2, KX])
            ot = sbc("ot", [2 * KX, KY, P])
            gt = [sbc(f"gt{i}", [P, 4, P]) for i in range(2)]
            mps = [psum(f"mps{i}", [P, 512]) for i in range(2)]
            hps = psum("hps", [P, 512])
            cps = psum("cps", [P, 512])
            tps = [psum(f"tps{i}", [P, 512]) for i in range(2)]
            ops = [psum(f"ops{i}", [P, 512]) for i in range(2)]
            staged, mixed, o_sb, moved = sem("staged"), sem("mixed"), sem("o_sb"), sem("moved")
            h_done, h_ready, c_done, c_ready = (sem(n) for n in ("h_done", "h_ready", "c_done", "c_ready"))
            sorted_, oturned, ot_sb, g_done, g_sb = sem("sorted"), sem("oturned"), sem("ot_sb"), sem("g_done"), sem("g_sb")
            gturned, gt_sb, back, added = sem("gturned"), sem("gt_sb"), sem("back"), sem("added")
            zstaged, mix_begun = sem("zstaged"), sem("mix_begun")
            block = ctx.enter_context(nc.Block())

            @block.sync
            def _(sp):
                sp.wait_ge(o_sb, GX)
                for b in range(B):
                    for q in range(NG):
                        sp.dma_start(z[C * b:C * b + C, GX * q:GX * q + GX, :, :].rearrange("i k y r -> i (k y r)"),
                                     o[C * q:C * q + C, b, :, :].rearrange("i k y -> i (k y)")).then_inc(moved, 16)
                sp.wait_ge(moved, 256)

            @block.gpsimd
            def _(pool):
                pass

            @block.scalar
            def _(act):
                def stage(k, s):
                    wait(act, mixed, k, 1, -1)
                    nc.scalar.copy(wst[s][:, :, :, :].rearrange("p o y r -> p o (y r)"), wts[:, :, ds(k, 1), :].rearrange("p o k y -> p o (k y)")).then_inc(staged, 1)
                stage(0, 0)
                stage(1, 1)
                with act.Fori(1, GX // 2) as h:
                    stage(h * 2, 0)
                    stage(h * 2 + 1, 1)
                act.wait_ge(h_done, 1)
                nc.scalar.activation(hb[:, :], hps[:, 0:B], ACT.Gelu, bias=b1s[:, 0:1]).then_inc(h_ready, 1)
                act.wait_ge(moved, 256)
                nc.scalar.copy(z2[:, :, :, :], z[:, :, :, :].rearrange("p k y r -> p y r k")).then_inc(sorted_, 1)
                for q in range(KY // 2):
                    act.wait_ge(g_done, q + 1)
                    nc.scalar.copy(g[:, :, 2 * q:2 * q + 2, :],
                                   ops[q % 2][:, 0:4 * H].rearrange("p (y r h) -> p h y r", y=2, r=2)).then_inc(g_sb, 1)
                for q in range(H // 4):
                    act.wait_ge(gturned, q + 1)
                    if q >= 2:
                        act.wait_ge(back, q - 1)
                    nc.scalar.copy(gt[q % 2][:, 0, :], tps[q % 2][:, 0:P]).then_inc(gt_sb, 1)

            @block.vector
            def _(dve):
                def stage(k, s):
                    wait(dve, mixed, k, 1, -1)
                    v = zi[:, :, ds(k, 1), :].rearrange("p b k (y r) -> p (b k) y r", r=2)
                    nc.vector.tensor_copy(zst[s][:, 0, :, :, :], v).then_inc(zstaged, 1)
                    nc.vector.tensor_scalar(zst[s][:, 1, :, :, 0], v[:, :, :, 1], -1.0, None, ALU.mult).then_inc(zstaged, 1)
                    nc.vector.tensor_copy(zst[s][:, 1, :, :, 1], v[:, :, :, 0]).then_inc(zstaged, 1)

                def keep(k, s):
                    wait(dve, mixed, k, 1, 1)
                    nc.vector.tensor_copy(o[:, :, ds(k, 1), :].rearrange("p b k (y r) -> p (b k) y r", r=2),
                                          mps[s][:, 0:KY * 2 * B].rearrange("p (y b r) -> p b y r", y=KY, r=2)).then_inc(o_sb, 1)
                stage(0, 0)
                stage(1, 1)
                keep(0, 0)
                with dve.Fori(0, GX // 2 - 1) as h:
                    stage(h * 2 + 2, 0)
                    keep(h * 2 + 1, 1)
                    stage(h * 2 + 3, 1)
                    keep(h * 2 + 2, 0)
                keep(GX - 1, 1)
                dve.wait_ge(c_done, 1)
                nc.vector.tensor_tensor(corr[:, :], cps[:, 0:1], b2s[:, :], ALU.add).then_inc(c_ready, 1)
                for q in range(KY // 4):
                    dve.wait_ge(oturned, q + 1)
                    nc.vector.tensor_copy(ot[:, 4 * q:4 * q + 4, :].rearrange("p y n -> p (y n)"), tps[q % 2][0:2 * KX, :]).then_inc(ot_sb, 1)
                dve.wait_ge(c_ready, 1)
                for q in range(H // 4):
                    dve.wait_ge(back, q + 1)
                    xv = x_sb[:, 4 * W * q:4 * W * q + 4 * W]
                    nc.vector.scalar_tensor_tensor(xv, ops[q % 2][:, 0:4 * W], corr[:, 0:1], xv, ALU.add, ALU.add).then_inc(added, 1)

            @block.tensor
            def _(pe):
                def mix(k, s):
                    wait(pe, staged, k, 1, 1)
                    wait(pe, zstaged, k, 3, 3)
                    wait(pe, o_sb, k, 1, -1)
                    pe.sem_inc(mix_begun, 1)
                    for m in range(KY):
                        for part in range(2):
                            for q in range(NG):
                                r = slice(C * q, C * q + C)
                                mm = nc.tensor.matmul(mps[s][r, 2 * B * m:2 * B * m + 2 * B], wst[s][r, :, m, part],
                                                      zst[s][r, part, :, m, :], start=(part == 0), stop=(part == 1))
                    mm.then_inc(mixed, 1)
                mix(0, 0)
                mix(1, 1)
                with pe.Fori(1, GX // 2) as h:
                    mix(h * 2, 0)
                    mix(h * 2 + 1, 1)
                for j in range(2 * M1 * M2):
                    mm = nc.tensor.matmul(hps[:, 0:B], l1w[:, j, :], fl[:, :, j], start=(j == 0), stop=(j == 2 * M1 * M2 - 1))
                mm.then_inc(h_done, 1)
                pe.wait_ge(h_ready, 1)
                for b in range(B):
                    mm = nc.tensor.matmul(cps[C * b:C * b + C, 0:1], l2w[:, :], hb[:, b:b + 1], start=True, stop=True)
                mm.then_inc(c_done, 1)
                pe.wait_ge(sorted_, 1)
                for q in range(KY // 4):
                    if q >= 2:
                        pe.wait_ge(ot_sb, q - 1)
                    for j in range(4):
                        mm = nc.tensor.transpose(tps[q % 2][0:2 * KX, P * j:P * j + P], z2[:, 4 * q + j, :, :].rearrange("p r k -> p (r k)"), ident[:, :])
                    mm.then_inc(oturned, 1)
                for q in range(KY // 2):
                    pe.wait_ge(ot_sb, q // 2 + 1)
                    if q >= 2:
                        pe.wait_ge(g_sb, q - 1)
                    for j in range(2):
                        mm = nc.tensor.matmul(ops[q % 2][:, 2 * H * j:2 * H * j + 2 * H], ot[:, 2 * q + j, :], ih[:, :], start=True, stop=True)
                    mm.then_inc(g_done, 1)
                pe.wait_ge(g_sb, KY // 2)
                pe.wait_ge(ot_sb, KY // 4)

                def turn(q):
                    if q >= 2:
                        pe.wait_ge(gt_sb, q - 1)
                    nc.tensor.transpose(tps[q % 2][:, 0:P], g[:, 4 * q:4 * q + 4, :, :].rearrange("p h y r -> p (h y r)"), ident[:, :]).then_inc(gturned, 1)

                def along_width(q):
                    pe.wait_ge(gt_sb, q + 1)
                    if q >= 2:
                        pe.wait_ge(added, q - 1)
                    nc.tensor.matmul(ops[q % 2][:, 0:4 * W], gt[q % 2][:, 0, :], iw[:, :, :].rearrange("p a w -> p (a w)"), start=True, stop=True).then_inc(back, 1)
                turn(0)
                for q in range(H // 4):
                    if q + 1 < H // 4:
                        turn(q + 1)
                    along_width(q)


def host_l2():
    f8 = np.float64
    def cft(n, f):
        L, M = 4, 8
        seg = 1.0 / L
        starts = np.arange(L) / L
        k = np.arange(M)
        nodes = -np.cos((2 * k + 1) * np.pi / (2 * M))
        T = np.cos(k[:, None] * np.arccos(nodes)[None])
        ang = nodes[:, None] * (f * 2 * np.pi * seg / 2)[None]
        Wc = (T @ np.cos(ang) - 1j * (T @ np.sin(ang))) * (seg / 2)
        tc = np.linspace(0, 1, n)
        ts = starts[:, None] + seg / 2 * (nodes[None] + 1)
        right = np.clip(np.searchsorted(tc, ts), 0, n - 1)
        left = np.clip(right - 1, 0, n - 1)
        wr = (ts - tc[left]) / (tc[right] - tc[left])
        ph = np.exp(-2j * np.pi * starts[:, None] * f[None])
        out = np.zeros((n, len(f)), complex)
        for l in range(L):
            for m in range(M):
                v = Wc[m] * ph[l]
                out[left[l, m]] += (1 - wr[l, m]) * v
                out[right[l, m]] += wr[l, m] * v
        return out
    w = np.arange(W)
    ky = np.arange(KY)
    th = 2 * np.pi * w[:, None] * ky[None] / W
    fw = np.zeros((W, FW))
    fw[:, 0:2 * KY:2], fw[:, 1:2 * KY:2] = np.cos(th), -np.sin(th)
    cw = cft(W, np.arange(M2).astype(f8))
    fw[:, 2 * KY:2 * KY + M2], fw[:, 2 * KY + M2:] = cw.real, cw.imag
    kx = np.concatenate([np.arange(16), np.arange(H - 16, H)])
    h = np.arange(H)
    t = 2 * np.pi * ((h[:, None] * kx[None]) % H) / H
    fh = np.zeros((H, 2, KX, 2))
    fh[:, 0, :, 0], fh[:, 0, :, 1] = np.cos(t), -np.sin(t)
    fh[:, 1, :, 0], fh[:, 1, :, 1] = np.sin(t), np.cos(t)
    cc = cft(H, np.array([0., 1., -2., -1.]))
    ch = np.zeros((H, 2, M1, 2))
    ch[:, 0, :, 0], ch[:, 0, :, 1] = cc.real, cc.imag
    ch[:, 1, :, 0], ch[:, 1, :, 1] = -cc.imag, cc.real
    ih = np.zeros((2, KX, 2, H))
    ih[0, :, 0], ih[0, :, 1] = np.cos(t).T, np.sin(t).T
    ih[1, :, 0], ih[1, :, 1] = -np.sin(t).T, np.cos(t).T
    ih /= H
    c = np.where(ky == 0, 1.0, 2.0) / W
    i1 = np.zeros((KY, 2, W))
    i1[:, 0], i1[:, 1] = c[:, None] * np.cos(th).T, -c[:, None] * np.sin(th).T
    iw = np.zeros((4, KY * 2, 4, W))
    for a in range(4):
        iw[a, :, a] = i1.reshape(KY * 2, W)
    r = dict(fw=fw, fh=fh.reshape(H, 2, 2 * KX), ch=ch.reshape(H, 2, 2 * M1), ih=ih.reshape(2 * KX, 2 * H), iw=iw.reshape(P, 4, W))
    return {k: np.ascontiguousarray(v).astype(np.float32) for k, v in r.items()}


EDGE1 = 1
HID = 2 * C
KS = 3 * C + 3
STRIP = TR * W
NPP = STRIP // P
HALF = STRIP // 2


def stage_fftconv(nc, x_sb, whid, wdw, bdw, wout, bout, ones_d, dft_d, xn_d, out):
    with ExitStack() as outer:
        sb = lambda n, s, dt=F: outer.enter_context(nc.sbuf_tensor("fc_" + n, s, dt))
        wk = sb("wk", [KS, 3, 3 * HID])
        wtmp = sb("wtmp", [KS, 3 * HID])
        bd = sb("bd", [KS, 3 * HID])
        wo = sb("wo", [P, 2, P])
        bo = sb("bo", [P, 1])
        dft = sb("dft", [P, 4, P])
        with ExitStack() as ctx:
            xp = ctx.enter_context(nc.sbuf_tensor("fc_xp", [P, H + 2, W + 2], F))
            stage_norm(nc, "gn3", x_sb, xp, 1)
            sem = lambda n: ctx.enter_context(nc.semaphore("fl_" + n))
            loaded, zeroed, stepped = sem("loaded"), sem("zeroed"), sem("stepped")
            block = ctx.enter_context(nc.Block())

            @block.gpsimd
            def _(pool):
                nc.gpsimd.memset(wo[:, :, :], 0.0).then_inc(zeroed, 1)

            @block.sync
            def _(sp):
                sp.dma_start(xn_d, xp[:, :, :]).then_inc(loaded, 16)
                for dst, src in ((wk[:, :, :], wdw), (wtmp[:, :], whid), (bd[:, :], bdw), (bo[:, :], bout), (dft[:, :, :], dft_d)):
                    sp.dma_start(dst, src).then_inc(loaded, 16)
                sp.wait_ge(zeroed, 1)
                for b in range(B):
                    sp.dma_start(wo[HID * (b % 2):HID * (b % 2) + HID, b // 2, C * b:C * b + C], wout).then_inc(loaded, 16)
                sp.wait_ge(loaded, 160)

            @block.vector
            def _(dve):
                dve.wait_ge(loaded, 160)
                nc.vector.tensor_tensor(wk[:, :, :], wk[:, :, :], wtmp[:, :].unsqueeze(1).broadcast_to([KS, 3, 3 * HID]), ALU.mult).then_inc(stepped, 1)
                dve.wait_ge(stepped, 1)
                nc.vector.tensor_tensor(wk[:, 1, :], wk[:, 1, :], bd[:, :], ALU.add)
                nc.vector.tensor_scalar(x_sb[:, :], x_sb[:, :], bo[:, 0:1], None, ALU.add)

        with ExitStack() as ctx:
            sem = lambda n: ctx.enter_context(nc.semaphore("fc_" + n))
            sbc = lambda n, s, dt=F: ctx.enter_context(nc.sbuf_tensor("fc_" + n, s, dt))
            psum = lambda n, s: ctx.enter_context(nc.psum_tensor("fc_" + n, s, F))
            xs = [sbc(f"xs{i}", [KS, B, TR + 2, W]) for i in range(2)]
            qk = [sbc(f"qk{i}", [P, B, 2 * HID]) for i in range(2)]
            spec = [sbc(f"spec{i}", [P, 2, B, 2 * HID]) for i in range(2)]
            prod = [sbc(f"prod{i}", [P, 2, 2, B, HID]) for i in range(2)]
            spo = [sbc(f"spo{i}", [P, 2, B, HID]) for i in range(2)]
            vsb = sbc("vsb", [P, 2, STRIP])
            vo = sbc("vo", [P, 2, STRIP])
            qps = [psum(f"qps{i}", [P, 512]) for i in range(2)]
            fps = psum("fps", [P, 2, 512])
            ips = [psum(f"ips{i}", [P, 512]) for i in range(2)]
            vps = psum("vps", [P, 512])
            ops = psum("ops", [P, 512])
            strip_in = [sem("strip_in0"), sem("strip_in1")]
            qk_done, qk_sb, spec_done, spec_sb = sem("qk_done"), sem("qk_sb"), sem("spec_done"), sem("spec_sb")
            mul_done, comb_done, back_done, vo_done = sem("mul_done"), sem("comb_done"), sem("back_done"), sem("vo_done")
            v_done, v_sb, out_done, x_done, stored = sem("v_done"), sem("v_sb"), sem("out_done"), sem("x_done"), sem("stored")
            block = ctx.enter_context(nc.Block())

            def strips(eng, body):
                body(0, 0, 0, True, False)
                with eng.Fori(0, NSTRIP // 2 - 1) as h:
                    body(h * 2 + 1, 1, h, False, False)
                    body(h * 2 + 2, 0, h + 1, False, False)
                body(NSTRIP - 1, 1, NSTRIP // 2 - 1, False, True)

            LOADS = 16 * (3 * B + 1)

            @block.sync
            def _(sp):
                def load(s, i, n, first, last):
                    wait(sp, v_done, s, 4, -4)
                    for dx in range(3):
                        for b in range(B):
                            sp.dma_start(xs[i][C * dx:C * dx + C, b, :, :],
                                         xn_d[C * b:C * b + C, ds(s * TR, TR + 2), dx:dx + W]).then_inc(strip_in[i], 16)
                    sp.dma_start(xs[i][3 * C:KS, :, :, :].rearrange("p b r c -> p b (r c)"),
                                 ones_d[:, :, ds(s * STRIP, (TR + 2) * W)]).then_inc(strip_in[i], 16)
                def store(s, i, n, first, last):
                    wait(sp, x_done, s, 2, 2)
                    sp.dma_start(out[:, ds(s * STRIP, STRIP)], x_sb[:, ds(s * STRIP, STRIP)]).then_inc(stored, 16)
                load(0, 0, 0, True, False)
                load(1, 1, 0, False, False)
                with sp.Fori(0, NSTRIP // 2 - 1) as h:
                    load(h * 2 + 2, 0, h + 1, False, False)
                    store(h * 2, 0, h, False, False)
                    load(h * 2 + 3, 1, h + 1, False, False)
                    store(h * 2 + 1, 1, h, False, False)
                store(NSTRIP - 2, 0, 0, False, False)
                store(NSTRIP - 1, 1, 0, False, True)
                sp.wait_ge(stored, 16 * NSTRIP)

            @block.gpsimd
            def _(pool):
                def combine(s, j):
                    m = j % 2
                    wait(pool, mul_done, s, NPP * 2, 2 * j + 2)
                    wait(pool, back_done, s, NPP, j - 1)
                    nc.gpsimd.tensor_tensor(spo[m][:, 0, :, :], prod[m][:, 0, 0, :, :], prod[m][:, 1, 1, :, :], ALU.subtract).then_inc(comb_done, 1)
                    nc.gpsimd.tensor_tensor(spo[m][:, 1, :, :], prod[m][:, 0, 1, :, :], prod[m][:, 1, 0, :, :], ALU.add).then_inc(comb_done, 1)

                def body(s, i, n, first, last):
                    for j in range(NPP):
                        combine(s, j)
                strips(pool, body)

            @block.scalar
            def _(act):
                def spectra(s, j):
                    m = j % 2
                    wait(act, spec_done, s, NPP, j + 1)
                    wait(act, mul_done, s, NPP * 2, 2 * j - 2)
                    nc.scalar.copy(spec[m][:, :, :, :].rearrange("p a b n -> p a (b n)"), fps[:, :, :]).then_inc(spec_sb, 1)

                def values(s, v):
                    wait(act, v_done, s, 4, v + 1)
                    if v == 0:
                        wait(act, out_done, s, 2, 0)
                    nc.scalar.copy(vsb[:, v % 2, HALF * (v // 2):HALF * (v // 2) + HALF], vps[:, 0:HALF]).then_inc(v_sb, 1)

                def body(s, i, n, first, last):
                    values(s, 0)
                    values(s, 1)
                    for j in range(NPP):
                        spectra(s, j)
                        if j == 4:
                            values(s, 2)
                            values(s, 3)
                strips(act, body)

            @block.vector
            def _(dve):
                def take(s, j):
                    m = j % 2
                    wait(dve, qk_done, s, NPP, j + 1)
                    wait(dve, spec_done, s, NPP, j - 1)
                    nc.vector.tensor_copy(qk[m][:, :, :].rearrange("p b n -> p (b n)"), qps[m][:, :]).then_inc(qk_sb, 1)

                def multiply(s, j):
                    m = j % 2
                    wait(dve, spec_sb, s, NPP, j + 1)
                    wait(dve, comb_done, s, 2 * NPP, 2 * j - 2)
                    for part in range(2):
                        nc.vector.tensor_tensor(prod[m][:, part, :, :, :], spec[m][:, :, :, 0:HID],
                                                spec[m][:, part, :, HID:2 * HID].unsqueeze(1).broadcast_to([P, 2, B, HID]), ALU.mult).then_inc(mul_done, 1)

                def weigh(s, j):
                    m = j % 2
                    wait(dve, back_done, s, NPP, j + 1)
                    wait(dve, v_sb, s, 4, 2 if j < 3 else 4)
                    if j == 0:
                        wait(dve, out_done, s, 2, 0)
                    nc.vector.tensor_tensor(vo[:, :, P * j:P * j + P], ips[m][:, 0:2 * P].rearrange("p (a n) -> p a n", a=2),
                                            vsb[:, :, P * j:P * j + P], ALU.mult).then_inc(vo_done, 1)

                def residual(s, h):
                    wait(dve, out_done, s, 2, h + 1)
                    xv = x_sb[:, ds(s * STRIP + HALF * h, HALF)]
                    nc.vector.tensor_tensor(xv, ops[:, 0:HALF], xv, ALU.add).then_inc(x_done, 1)

                def body(s, i, n, first, last):
                    take(s, 0)
                    take(s, 1)
                    for j in range(NPP):
                        multiply(s, j)
                        if j + 2 < NPP:
                            take(s, j + 2)
                        if j >= 1:
                            weigh(s, j - 1)
                    weigh(s, NPP - 1)
                    residual(s, 0)
                    residual(s, 1)
                strips(dve, body)

            @block.tensor
            def _(pe):
                def rows(i, b, at, n):
                    return xs[i][:, b, :, :].rearrange("p r c -> p (r c)")[:, at:at + n]

                def project(s, i, n, j):
                    m = j % 2
                    if j == 0:
                        wait(pe, strip_in[i], n, LOADS, LOADS)
                    wait(pe, qk_sb, s, NPP, j - 1)
                    for b in range(B):
                        for dy in range(3):
                            mm = nc.tensor.matmul(qps[m][:, P * b:P * b + P], rows(i, b, dy * W + P * j, P), wk[:, dy, 0:2 * HID],
                                                  start=(dy == 0), stop=(dy == 2))
                    mm.then_inc(qk_done, 1)

                def values(s, i, v):
                    h, a = v // 2, v % 2
                    wait(pe, v_sb, s, 4, v)
                    for b in range(2):
                        for dy in range(3):
                            mm = nc.tensor.matmul(vps[HID * b:HID * b + HID, 0:HALF], wk[:, dy, 2 * HID:3 * HID],
                                                  rows(i, 2 * a + b, dy * W + HALF * h, HALF),
                                                  start=(dy == 0), stop=(dy == 2))
                    mm.then_inc(v_done, 1)

                def forward(s, j):
                    m = j % 2
                    wait(pe, qk_sb, s, NPP, j + 1)
                    wait(pe, spec_sb, s, NPP, j)
                    for part in range(2):
                        mm = nc.tensor.matmul(fps[:, part, :], dft[:, part, :], qk[m][:, :, :].rearrange("p b n -> p (b n)"), start=True, stop=True)
                    mm.then_inc(spec_done, 1)

                def back(s, j):
                    m = j % 2
                    wait(pe, comb_done, s, 2 * NPP, 2 * j + 2)
                    wait(pe, vo_done, s, NPP, j - 1)
                    for a in range(2):
                        for part in range(2):
                            mm = nc.tensor.matmul(ips[m][:, P * a:P * a + P], spo[m][:, part, 2 * a:2 * a + 2, :].rearrange("p b n -> p (b n)"),
                                                  dft[:, 2 + part, :], start=(part == 0), stop=(part == 1))
                    mm.then_inc(back_done, 1)

                def merge(s, h):
                    wait(pe, vo_done, s, NPP, 3 * h + 3)
                    wait(pe, x_done, s, 2, h)
                    for a in range(2):
                        mm = nc.tensor.matmul(ops[:, 0:HALF], wo[:, a, :], vo[:, a, HALF * h:HALF * h + HALF], start=(a == 0), stop=(a == 1))
                    mm.then_inc(out_done, 1)

                def body(s, i, n, first, last):
                    project(s, i, n, 0)
                    project(s, i, n, 1)
                    values(s, i, 0)
                    forward(s, 0)
                    values(s, i, 1)
                    for j in range(2, NPP):
                        project(s, i, n, j)
                        forward(s, j - 1)
                        back(s, j - 2)
                    values(s, i, 2)
                    forward(s, NPP - 1)
                    values(s, i, 3)
                    back(s, NPP - 2)
                    merge(s, 0)
                    back(s, NPP - 1)
                    merge(s, 1)
                strips(pe, body)


def host_l3(wh, bh, wd, bdw, wo, bo):
    wh, wd = wh.reshape(192, C), wd.reshape(192, 3, 3)
    whid = np.concatenate([np.tile(wh.T, (3, 1)), np.tile(bh, (3, 1))], 0)
    t = wd.transpose(2, 1, 0)
    wdw = np.concatenate([np.repeat(t, C, 0), t], 0)
    bd = np.zeros((KS, 192), np.float32)
    bd[3 * C + 1] = bdw
    wout = wo.reshape(C, HID).T
    ones = np.zeros((3, B, H + 2, W), np.float32)
    ones[:, :, 1:H + 1] = 1
    ones[0, :, :, 0] = 0
    ones[2, :, :, W - 1] = 0
    r, c = np.arange(64) // 8, np.arange(64) % 8
    th = 2 * np.pi * (r[:, None] * r[None] + c[:, None] * c[None]) / 8
    z = np.zeros((4, P, P))
    for q in range(2):
        s = slice(64 * q, 64 * q + 64)
        z[0, s, s] = np.cos(th)
        z[1, s, s] = -np.sin(th)
        z[2, s, s] = np.cos(th) / 64
        z[3, s, s] = -np.sin(th) / 64
    return dict(whid=whid, wdw=wdw, bdw=bd, wout=wout, bout=np.tile(bo, 4)[:, None], ones=ones.reshape(3, B, -1),
                dft=np.ascontiguousarray(z.transpose(1, 0, 2)).astype(np.float32))




def stage_load(nc, x_sb, x):
    with ExitStack() as ctx:
        x_loaded = ctx.enter_context(nc.semaphore("x_loaded"))
        block = ctx.enter_context(nc.Block())

        @block.sync
        def _(sp):
            sp.dma_start(x_sb[:, :], x).then_inc(x_loaded, 16)
            sp.wait_ge(x_loaded, 16)


def program(nc, a, out):
    dram = lambda n, s: nc.dram_tensor(n, s, F, kind="Internal").ap()
    with ExitStack() as ctx:
        x_sb = ctx.enter_context(nc.sbuf_tensor("x_sb", [P, NPIX], F))
        stage_load(nc, x_sb, a["x"])
        stage_attention(nc, x_sb, a["wqkvT"], a["rel"], a["halves"], a["headmask"], a["ident"])
        stage_deform(nc, x_sb, a["convw"], a["bias"], a["coord"], a["ixb"], a["dcn"], a["ident"],
                     dram("deform_image", [P, TY, TY]), dram("deform_table", [1 + B * TROWS * TX, ENTRY]))
        stage_fourier(nc, x_sb, a["fw"], a["fh"], a["ch"], a["ih"], a["iw"], a["w1"], a["w2"],
                      a["lin1"], a["b1"], a["lin2"], a["b2"], a["ident"])
        stage_fftconv(nc, x_sb, a["whid"], a["wdw"], a["bdw"], a["wout"], a["bout"], a["ones"], a["dft"],
                      dram("gate_image", [P, H + 2, W + 2]), out)


def kernel(**inputs):
    import concourse.bacc as bacc
    from concourse.bass_utils import run_bass_kernel_spmd

    i = {k: np.asarray(v) for k, v in inputs.items()}
    qkv = i["L0_conv_w_qkv"].reshape(3, C, C).transpose(2, 0, 1)
    rel = np.concatenate([i["L0_conv_rel_h"].reshape(WIN, D // 2), i["L0_conv_rel_w"].reshape(WIN, D // 2)], 1).T
    arrays = dict(
        x=i["x"].reshape(P, NPIX), wqkvT=qkv, rel=np.tile(rel, (P // D, 1)), **host_consts(),
        **host_l1(*(i["L1_conv_" + n] for n in ("offset_w", "offset_b", "mask_w", "mask_b", "dcn_w"))),
        **host_l2(), w1=i["L2_conv_w1"], w2=i["L2_conv_w2"], lin1=i["L2_conv_lin1_w"], b1=i["L2_conv_lin1_b"][:, None],
        lin2=i["L2_conv_lin2_w"], b2=np.tile(i["L2_conv_lin2_b"], B)[:, None],
        **host_l3(*(i["L3_conv_" + n] for n in ("w_hidden", "b_hidden", "w_dw", "b_dw", "w_out", "b_out"))))
    arrays = {k: np.ascontiguousarray(v) for k, v in arrays.items()}
    nc = bacc.Bacc("TRN2", target_bir_lowering=False, num_devices=1)
    handles = {k: nc.dram_tensor("in_" + k, v.shape, mybir.dt.from_np(v.dtype), kind="ExternalInput").ap()
               for k, v in arrays.items()}
    out = nc.dram_tensor("out", [P, NPIX], F, kind="ExternalOutput").ap()
    program(nc, handles, out)
    r = run_bass_kernel_spmd(nc, [{"in_" + k: v for k, v in arrays.items()}], core_ids=[0])
    return r.results[0]["out"].reshape(B, C, H, W)
```

```python
from contextlib import ExitStack, contextmanager

import numpy as np

import concourse.bass as bass
from concourse import mybir

F=mybir.dt.float32; ALU=mybir.AluOpType; ACT=mybir.ActivationFunctionType; AX=mybir.AxisListType
B, C, H, W = 4, 32, 96, 96
P = B * C
NPIX = H * W
ds = bass.ds


@contextmanager
def when(eng, flag):
    if flag is None:
        yield
    else:
        with eng.If(eng.value_load(flag, min_val=0, max_val=1) > 0):
            yield


def stage_norm(nc, name, x_sb, xpad, pad, far=None):
    wide = xpad.shape[2]
    with ExitStack() as ctx:
        stats = ctx.enter_context(nc.sbuf_tensor(name + "_stats", [P, 18, 6], F))
        agg = ctx.enter_context(nc.sbuf_tensor(name + "_agg", [P, 8], F))
        stats_done = ctx.enter_context(nc.semaphore(name + "_stats_done"))
        var_ready = ctx.enter_context(nc.semaphore(name + "_var_ready"))
        root_ready = ctx.enter_context(nc.semaphore(name + "_root_ready"))
        step_done = ctx.enter_context(nc.semaphore(name + "_step_done"))
        border_done = ctx.enter_context(nc.semaphore(name + "_border_done"))
        block = ctx.enter_context(nc.Block())
        mean, var, std, rstd, t = (agg[:, k:k + 1] for k in range(5))

        @block.gpsimd
        def _(pool):
            with when(pool, far):
                nc.gpsimd.memset(xpad[:, 0:pad, :], 0.0)
                nc.gpsimd.memset(xpad[:, H + pad:H + 2 * pad, :], 0.0)
                nc.gpsimd.memset(xpad[:, pad:H + pad, 0:pad], 0.0)
                nc.gpsimd.memset(xpad[:, pad:H + pad, W + pad:wide], 0.0).then_inc(border_done, 1)

        @block.vector
        def _(dve):
            with when(dve, far):
                for k in range(18):
                    nc.vector.bn_stats(stats[:, k, :], x_sb[:, k * 512:(k + 1) * 512]).then_inc(stats_done, 1)
                dve.wait_ge(stats_done, 18)
                nc.vector.bn_aggr(agg[:, 0:2], stats[:, :, :]).then_inc(step_done, 1)
                dve.wait_ge(step_done, 1)
                nc.vector.tensor_scalar(var, var, 1e-5, None, ALU.add).then_inc(var_ready, 1)
                dve.wait_ge(root_ready, 1)
                nc.vector.reciprocal(rstd, std).then_inc(step_done, 1)
                dve.wait_ge(step_done, 2)
                nc.vector.tensor_tensor(t, rstd, rstd, ALU.mult).then_inc(step_done, 1)
                dve.wait_ge(step_done, 3)
                nc.vector.tensor_tensor(t, t, var, ALU.mult).then_inc(step_done, 1)
                dve.wait_ge(step_done, 4)
                nc.vector.tensor_scalar(t, t, -0.5, 1.5, ALU.mult, ALU.add).then_inc(step_done, 1)
                dve.wait_ge(step_done, 5)
                nc.vector.tensor_tensor(rstd, rstd, t, ALU.mult).then_inc(step_done, 1)
                dve.wait_ge(step_done, 6)
                nc.vector.tensor_scalar(xpad[:, pad:H + pad, pad:W + pad],
                                        x_sb[:, :].rearrange("p (h w) -> p h w", h=H),
                                        mean, rstd, ALU.subtract, ALU.mult)

        @block.scalar
        def _(act):
            with when(act, far):
                act.wait_ge(var_ready, 1)
                nc.scalar.activation(std, var, ACT.Sqrt).then_inc(root_ready, 1)


BLK, HALO, HEADS = 8, 3, 4
D = C // HEADS
WIN = BLK + 2 * HALO
NK = WIN * WIN
HK = NK // 2
NWIN = (H // BLK) * (W // BLK)
Q64 = BLK * BLK


def wait(eng, s, w, k, c):
    if isinstance(w, int):
        if k * w + c > 0:
            eng.wait_ge(s, k * w + c)
    else:
        eng.wait_ge(s, w * k + c)


NROW = W // BLK
HALFROW = NROW // 2


def stage_attention(nc, x_sb, wqkvT, rel, halves, headmask, unitmask, ident_d, q_dram):
    PADDED = H + 2 * HALO
    with ExitStack() as outer:
        sb = lambda n, s, dt=F: outer.enter_context(nc.sbuf_tensor("at_" + n, s, dt))
        xp = sb("xp", [P, PADDED, PADDED])
        stage_norm(nc, "gn0", x_sb, xp, HALO)
        kp = sb("kp", [P, PADDED, PADDED])
        wbd = sb("wbd", [P, 3, P])
        relc = sb("relc", [P, WIN])
        relhw = sb("relhw", [P, WIN, WIN])
        half = sb("half", [P, 2])
        hm = sb("hm", [P, HEADS])
        um = sb("um", [P, B * HEADS])
        ident = sb("ident", [P, P])
        with ExitStack() as ctx:
            sem = lambda n: ctx.enter_context(nc.semaphore("ap_" + n))
            ps = [ctx.enter_context(nc.psum_tensor(f"ap_ps{i}", [P, 512], F)) for i in range(4)]
            qrow = [ctx.enter_context(nc.sbuf_tensor(f"ap_qrow{i}", [P, NROW, Q64], F)) for i in range(2)]
            zeroed, loaded, rel_step = sem("zeroed"), sem("loaded"), sem("rel_step")
            keys_done, keys_out, queries_done, queries_out = sem("keys_done"), sem("keys_out"), sem("queries_done"), sem("queries_out")
            stored = [sem("stored0"), sem("stored1")]
            block = ctx.enter_context(nc.Block())
            KROWS = PADDED // 3

            @block.gpsimd
            def _(pool):
                nc.gpsimd.memset(wbd[:, :, :], 0.0).then_inc(zeroed, 1)

            @block.sync
            def _(sp):
                sp.dma_start(relc[:, :], rel).then_inc(loaded, 16)
                sp.dma_start(half[:, :], halves).then_inc(loaded, 16)
                sp.dma_start(hm[:, :], headmask).then_inc(loaded, 16)
                sp.dma_start(um[:, :], unitmask).then_inc(loaded, 16)
                sp.dma_start(ident[:, :], ident_d).then_inc(loaded, 16)
                sp.wait_ge(zeroed, 1)
                for b in range(B):
                    sp.dma_start(wbd[C * b:C * b + C, :, C * b:C * b + C], wqkvT).then_inc(loaded, 16)
                with sp.Fori(0, NROW // 2) as i:
                    for s in range(2):
                        sp.wait_ge(queries_out, i * 4 + (2 * s + 2))
                        sp.dma_start(q_dram[:, ds(i * 2 + s, 1), :, :].rearrange("p y x q -> p (y x) q"), qrow[s][:, :, :]).then_inc(stored[s], 16)
                for s in range(2):
                    sp.wait_ge(stored[s], 16 * NROW // 2)

            LOADED = 16 * 9

            @block.vector
            def _(dve):
                dve.wait_ge(loaded, LOADED)
                nc.vector.tensor_scalar(relhw[:, :, :], relc[:, :].unsqueeze(2).broadcast_to([P, WIN, WIN]),
                                        half[:, 0:1], None, ALU.mult).then_inc(rel_step, 1)
                dve.wait_ge(rel_step, 1)
                nc.vector.scalar_tensor_tensor(relhw[:, :, :], relc[:, :].unsqueeze(1).broadcast_to([P, WIN, WIN]),
                                               half[:, 1:2], relhw[:, :, :], ALU.mult, ALU.add)
                with dve.Fori(0, KROWS // 2) as i:
                    for s in range(2):
                        dve.wait_ge(keys_done, i * 2 + s + 1)
                        nc.vector.tensor_copy(kp[:, ds(i * 6 + 3 * s, 3), :],
                                              ps[s][:, 0:3 * PADDED].rearrange("p (r c) -> p r c", r=3)).then_inc(keys_out, 1)

            @block.scalar
            def _(act):
                def half_row(i, r, h, j):
                    act.wait_ge(queries_done, i * 4 + (2 * r + h + 1))
                    if h == 0 and j is not None:
                        wait(act, stored[r], j, 16, 0)
                    nc.scalar.activation(qrow[r][:, :, 32 * h:32 * h + 32].rearrange("p x (r c) -> p x r c", r=4),
                                         ps[2 + h][:, 0:4 * W].rearrange("p (r x c) -> p x r c", r=4, x=NROW),
                                         ACT.Copy, scale=D ** -0.5).then_inc(queries_out, 1)
                for r in range(2):
                    for h in range(2):
                        half_row(0, r, h, None)
                with act.Fori(1, NROW // 2) as i:
                    for r in range(2):
                        for h in range(2):
                            half_row(i, r, h, i)

            @block.tensor
            def _(pe):
                pe.wait_ge(loaded, LOADED)

                def key_rows(i, s):
                    wait(pe, keys_out, i, 2, s - 1)
                    nc.tensor.matmul(ps[s][:, 0:3 * PADDED], wbd[:, 1, :], xp[:, ds(i * 6 + 3 * s, 3), :],
                                     start=True, stop=True).then_inc(keys_done, 1)

                def query_rows(i, s):
                    wait(pe, queries_out, i, 2, s - 1)
                    nc.tensor.matmul(ps[2 + s][:, 0:4 * W], wbd[:, 0, :],
                                     xp[:, ds(i * 8 + (HALO + 4 * s), 4), HALO:HALO + W],
                                     start=True, stop=True).then_inc(queries_done, 1)

                def both(i):
                    for s in range(2):
                        key_rows(i, s)
                        query_rows(i, s)
                both(0)
                with pe.Fori(1, NROW) as i:
                    both(i)
                with pe.Fori(NROW, KROWS // 2) as i:
                    for s in range(2):
                        key_rows(i, s)

        with ExitStack() as ctx:
            sem = lambda n: ctx.enter_context(nc.semaphore("at_" + n))
            sbc = lambda n, s, dt=F: ctx.enter_context(nc.sbuf_tensor("at_" + n, s, dt))
            qhalf = [sbc(f"qhalf{i}", [P, HALFROW, Q64]) for i in range(2)]
            kw = [sbc(f"kw{i}", [P, NK]) for i in range(2)]
            qw = [sbc(f"qw{i}", [P, B * HEADS, Q64]) for i in range(2)]
            xw = [sbc(f"xw{i}", [P, NK]) for i in range(2)]
            vs = [sbc(f"vs{i}", [HK, 2, P]) for i in range(2)]
            nmx = sbc("nmx", [P, B, 2])
            sums = sbc("sums", [P, B, 2])
            rs = sbc("rs", [P, B, 2])
            probs = [sbc(f"probs{b}", [P, 2, NK]) for b in range(B)]
            pts = [[sbc(f"pts{i}_{b}", [HK, 2, 2, P]) for b in range(B)] for i in range(2)]
            sc = [ctx.enter_context(nc.psum_tensor(f"at_sc{b}", [P, 512], F)) for b in range(B)]
            pt = [ctx.enter_context(nc.psum_tensor(f"at_pt{i}", [P, 512], F)) for i in range(2)]
            ov = [ctx.enter_context(nc.psum_tensor(f"at_ov{i}", [P, 512], F)) for i in range(2)]
            scores_ready, max_ready, exp_done, inv_ready = sem("scores_ready"), sem("max_ready"), sem("exp_done"), sem("inv_ready")
            normed, pt_ready, pts_ready = sem("normed"), sem("pt_ready"), sem("pts_ready")
            pv_done, v_ready, vs_ready = sem("pv_done"), sem("v_ready"), sem("vs_ready")
            keys_ready, q_ready, xw_ready, res_step = sem("keys_ready"), sem("q_ready"), sem("xw_ready"), sem("res_step")
            q_loaded = [sem("q_loaded0"), sem("q_loaded1")]
            block = ctx.enter_context(nc.Block())

            def there(w):
                return not isinstance(w, int) or 0 <= w < NWIN

            def rows(eng, step):
                for w in (-2, -1):
                    step(w, 0, w)
                for x in range(NROW):
                    step(x, 0, x)
                with eng.Fori(1, NROW - 1) as gy:
                    for x in range(NROW):
                        step(gy * NROW + x, gy, x)
                for x in range(NROW):
                    step((NROW - 1) * NROW + x, NROW - 1, x)
                step(NWIN, NROW - 1, NROW)

            def corner(gy, x):
                over = x // NROW
                return gy * BLK + over * BLK, (x - over * NROW) * BLK

            @block.sync
            def _(sp):
                def load(gy, h):
                    wait(sp, q_ready, gy, NROW, HALFROW * (h + 1) - NROW)
                    sp.dma_start(qhalf[h][:, :, :], q_dram[:, ds(gy, 1), HALFROW * h:HALFROW * h + HALFROW, :].rearrange("p y x q -> p (y x) q")
                                 ).then_inc(q_loaded[h], 16)
                for h in range(2):
                    load(0, h)
                with sp.Fori(1, NROW) as gy:
                    for h in range(2):
                        load(gy, h)

            @block.gpsimd
            def _(pool):
                def spread(w, gy, x):
                    over = x // NROW
                    x -= over * NROW
                    wait(pool, q_loaded[x // HALFROW], gy, 16, 16 + 16 * over)
                    wait(pool, scores_ready, w, B, B * (-1))
                    nc.gpsimd.tensor_tensor(qw[x % 2][:, :, :], qhalf[x // HALFROW][:, x % HALFROW:x % HALFROW + 1, :].broadcast_to([P, B * HEADS, Q64]),
                                            um[:, :].unsqueeze(2).broadcast_to([P, B * HEADS, Q64]), ALU.mult).then_inc(q_ready, 1)

                def norm(w, b):
                    wait(pool, inv_ready, w, B, b + 1)
                    nc.gpsimd.tensor_tensor(probs[b][:, :, :], probs[b][:, :, :],
                                            rs[:, b, :].unsqueeze(2).broadcast_to([P, 2, NK]), ALU.mult).then_inc(normed, 1)

                def step(w, gy, x):
                    if there(w):
                        norm(w, 3)
                    if there(w + 2):
                        spread(w + 2, gy, x + 2)
                    if there(w + 1):
                        for b in range(3):
                            norm(w + 1, b)
                rows(pool, step)

            @block.vector
            def _(dve):
                def keys(w, gy, x):
                    y0, x0 = corner(gy, x)
                    wait(dve, scores_ready, w, B, -B)
                    nc.vector.tensor_tensor(kw[x % 2][:, :].rearrange("p (r c) -> p r c", r=WIN),
                                            kp[:, ds(y0, WIN), ds(x0, WIN)], relhw[:, :, :], ALU.add).then_inc(keys_ready, 1)

                def maxes(w, b):
                    wait(dve, scores_ready, w, B, b + 1)
                    wait(dve, exp_done, w, 2 * B, 2 * b + 2 - 2 * B)
                    nc.vector.tensor_reduce(nmx[:, b, :], sc[b][:, 0:2 * NK].rearrange("p (j k) -> p j k", j=2),
                                            AX.X, ALU.max, negate=True).then_inc(max_ready, 1)

                def inverse(w, b):
                    wait(dve, exp_done, w, 2 * B, 2 * b + 2)
                    wait(dve, normed, w, B, b + 1 - B)
                    nc.vector.reciprocal(rs[:, b, :], sums[:, b, :]).then_inc(inv_ready, 1)

                def evac(w, b, s):
                    wait(dve, pt_ready, w, B, b + 1)
                    wait(dve, pv_done, w, 1, -1)
                    nc.vector.tensor_copy(pts[s][b][:, :, :, :],
                                          pt[b % 2][0:HK, :].rearrange("p (c j q) -> p c j q", c=2, j=2)).then_inc(pts_ready, 1)

                def residual(w, gy, x):
                    y0, x0 = corner(gy, x)
                    wait(dve, pv_done, w, 1, 1)
                    xv = x_sb[:, :].rearrange("p (h w) -> p h w", h=H)[:, ds(y0, BLK), ds(x0, BLK)]
                    for h in range(HEADS):
                        if h:
                            wait(dve, res_step, w, HEADS, h)
                        nc.vector.scalar_tensor_tensor(
                            xv, ov[x % 2][:, Q64 * h:Q64 * h + Q64].rearrange("p (r c) -> p r c", r=BLK),
                            hm[:, h:h + 1], xv, ALU.mult, ALU.add).then_inc(res_step, 1)

                def step(w, gy, x):
                    for b in range(B):
                        if there(w):
                            evac(w, b, x % 2)
                        if there(w + 1):
                            maxes(w + 1, b)
                        if b == 0:
                            if there(w):
                                inverse(w, 3)
                            if there(w + 2):
                                keys(w + 2, gy, x + 2)
                        elif there(w + 1):
                            inverse(w + 1, b - 1)
                        if b == 2 and there(w + (-1)):
                            residual(w + (-1), gy, x - 1)
                rows(dve, step)

            @block.scalar
            def _(act):
                def crop(w, gy, x):
                    y0, x0 = corner(gy, x)
                    wait(act, v_ready, w, 1, -1)
                    nc.scalar.copy(xw[x % 2][:, :].rearrange("p (r c) -> p r c", r=WIN),
                                   xp[:, ds(y0, WIN), ds(x0, WIN)]).then_inc(xw_ready, 1)

                def values(w, s):
                    wait(act, v_ready, w, 1, 1)
                    wait(act, pv_done, w, 1, -1)
                    nc.scalar.copy(vs[s][:, :, :], ov[1 - s][0:HK, 256:512].rearrange("p (c o) -> p c o", c=2)).then_inc(vs_ready, 1)

                def exps(w, b):
                    wait(act, max_ready, w, B, b + 1)
                    wait(act, pt_ready, w, B, b + 1 - B)
                    wait(act, inv_ready, w, B, b + 1 - B)
                    for j in range(2):
                        nc.scalar.activation(probs[b][:, j, :], sc[b][:, NK * j:NK * j + NK], ACT.Exp,
                                             bias=nmx[:, b, j:j + 1], accum_out=sums[:, b, j:j + 1]).then_inc(exp_done, 1)

                def step(w, gy, x):
                    if there(w + 1):
                        exps(w + 1, 0)
                        exps(w + 1, 1)
                    if there(w + 2):
                        crop(w + 2, gy, x + 2)
                    if there(w + 1):
                        exps(w + 1, 2)
                        exps(w + 1, 3)
                        values(w + 1, (x + 1) % 2)
                rows(act, step)

            @block.tensor
            def _(pe):
                def score(w, b, s):
                    if b == 0:
                        wait(pe, keys_ready, w, 1, 1)
                        wait(pe, q_ready, w, 1, 1)
                    wait(pe, exp_done, w, 2 * B, 2 * b + 2 - 2 * B)
                    for j in range(2):
                        mm = nc.tensor.matmul(sc[b][:, NK * j:NK * j + NK], qw[s][:, HEADS * b + 2 * j:HEADS * b + 2 * j + 2, :],
                                              kw[s][:, :], start=True, stop=True)
                    mm.then_inc(scores_ready, 1)

                def value(w, s):
                    wait(pe, xw_ready, w, 1, 1)
                    wait(pe, res_step, w, HEADS, -2 * HEADS)
                    for c in range(2):
                        mm = nc.tensor.matmul(ov[1 - s][0:HK, 256 + P * c:256 + P * c + P], xw[s][:, HK * c:HK * c + HK],
                                              wbd[:, 2, :], start=True, stop=True)
                    mm.then_inc(v_ready, 1)

                def transposed(w, b):
                    wait(pe, normed, w, B, b + 1)
                    wait(pe, pts_ready, w, B, b - 1)
                    for c in range(2):
                        for j in range(2):
                            o = (2 * c + j) * P
                            mm = nc.tensor.transpose(pt[b % 2][0:HK, o:o + P], probs[b][:, j, HK * c:HK * c + HK], ident[:, :])
                    mm.then_inc(pt_ready, 1)

                def weigh(w, s):
                    wait(pe, pts_ready, w, B, B)
                    if not isinstance(w, int) or w < NWIN - 1:
                        wait(pe, vs_ready, w, 1, 2)
                    else:
                        wait(pe, vs_ready, w, 1, 1)
                    for c in range(2):
                        for b in range(B):
                            mm = nc.tensor.matmul(ov[s][C * b:C * b + C, 0:256], vs[s][:, c, C * b:C * b + C],
                                                  pts[s][b][:, c, :, :], start=(c == 0), stop=(c == 1))
                    mm.then_inc(pv_done, 1)

                def step(w, s):
                    for b in range(B):
                        if there(w):
                            transposed(w, b)
                        if there(w + 1):
                            score(w + 1, b, 1 - s)
                        if b == 1 and there(w + (-1)):
                            weigh(w + (-1), 1 - s)
                        if b == 2 and there(w + 1):
                            value(w + 1, 1 - s)
                for w in range(-1, 2):
                    step(w, w % 2)
                with pe.Fori(1, NWIN // 2 - 1) as g:
                    step(g * 2, 0)
                    step(g * 2 + 1, 1)
                for w in range(NWIN - 2, NWIN + 1):
                    step(w, w % 2)


def host_consts():
    p = np.arange(P)
    return dict(
        halves=np.stack([(p % D < D // 2), (p % D >= D // 2)], 1).astype(np.float32),
        headmask=((p % C)[:, None] // D == np.arange(HEADS)[None]).astype(np.float32),
        unitmask=(p[:, None] // D == np.arange(B * HEADS)[None]).astype(np.float32),
        ident=np.eye(P, dtype=np.float32))



I32 = mybir.dt.int32
U32 = mybir.dt.uint32
TAPS = 9
TR = 8
NSTRIP, TPS = H // TR, TR * W // P
UNITS = TPS * B
EDGE = 2
TY, TX = H + 2 * EDGE, 112
TROWS = TY - 1
ENTRY = 4 * C
GROWS = 9
RING = 4


def stage_deform_far(nc, x_sb, convw, biasr, coord, base_ix, dcn, ident_d, xn_d, table, x_save, far):
    with ExitStack() as ctx:
        restored = ctx.enter_context(nc.semaphore("df_restored"))
        block = ctx.enter_context(nc.Block())

        @block.sync
        def _(sp):
            with when(sp, far):
                sp.dma_start(x_sb[:, :], x_save).then_inc(restored, 16)
                sp.wait_ge(restored, 16)

    LOADS = 16 * 3 * B
    with ExitStack() as outer:
        sb = lambda n, s, dt=F: outer.enter_context(nc.sbuf_tensor("df_" + n, s, dt))
        ident = sb("ident", [P, P])
        wc = sb("wc", [3 * C, 3, 27])
        wd = sb("wd", [P, TAPS, C])
        base = sb("base", [P, UNITS, 2, TAPS])
        bias = sb("bias", [P, 27])
        ixb = sb("ixb", [P, UNITS, TAPS])
        with ExitStack() as ctx:
            xp = ctx.enter_context(nc.sbuf_tensor("df_xp", [P, TY, TX], F))
            stage_norm(nc, "gnf", x_sb, xp, EDGE, far)
            sem = lambda n: ctx.enter_context(nc.semaphore("dt_" + n))
            rows = [ctx.enter_context(nc.sbuf_tensor(f"dt_rows{i}", [P, GROWS + 1, TX], F)) for i in range(2)]
            stage = [ctx.enter_context(nc.sbuf_tensor(f"dt_stage{i}", [TX, GROWS, B, 2, C], F)) for i in range(2)]
            zeros = ctx.enter_context(nc.sbuf_tensor("dt_zeros", [1, 64], F))
            ps = [ctx.enter_context(nc.psum_tensor(f"dt_ps{i}", [P, 4, 512], F)) for i in range(2)]
            zeros_ready, lower, filled, loaded, written = sem("zeros_ready"), sem("lower"), sem("filled"), sem("loaded"), sem("written")
            rows_ready, turned, staged, stored = sem("rows_ready"), sem("turned"), sem("staged"), [sem("stored0"), sem("stored1")]
            block = ctx.enter_context(nc.Block())
            NG = (TY - 1) // GROWS
            assert NG * GROWS == TY - 1 and NG % 2 == 1

            @block.sync
            def _(sp):
                with when(sp, far):
                    for dst, src in ((ident[:, :], ident_d), (wc[:, :, :], convw), (wd[:, :, :], dcn),
                                     (base[:, :, :, :], coord), (bias[:, :], biasr), (ixb[:, :, :], base_ix)):
                        sp.dma_start(dst, src).then_inc(loaded, 16)
                    sp.dma_start(xn_d, xp[:, :, 0:TY]).then_inc(written, 16)

                    sp.wait_ge(zeros_ready, 1)
                    sp.dma_start(table[0:1, 0:64], zeros[0:1, :]).then_inc(written, 16)
                    sp.dma_start(table[B * TROWS * TX:B * TROWS * TX + 1, 64:128], zeros[0:1, :]).then_inc(written, 16)

                    def store(g, s, n):
                        wait(sp, lower, g, 1, 1)
                        wait(sp, staged, g, 1, 1)
                        for b in range(B):
                            for half in range(2):
                                dst = table[ds(g * (GROWS * TX) + (1 - half + b * TROWS * TX), GROWS * TX), 64 * half:64 * half + 64]
                                sp.dma_start(dst.rearrange("(y x) c -> x y c", x=TX),
                                             stage[s][:, :, b, :, :].rearrange("x y r c -> x y (r c)")).then_inc(stored[s], 16)
                    store(0, 0, 0)
                    with sp.Fori(0, NG // 2) as h:
                        store(h * 2 + 1, 1, 0)
                        store(h * 2 + 2, 0, 0)
                    sp.wait_ge(written, 48)
                    sp.wait_ge(loaded, 16 * 6)
                    sp.wait_ge(stored[0], 128 * (NG // 2 + 1))
                    sp.wait_ge(stored[1], 128 * (NG // 2))

            @block.gpsimd
            def _(pool):
                with when(pool, far):
                    nc.gpsimd.memset(zeros[:, :], 0.0).then_inc(zeros_ready, 1)
                    pool.wait_ge(loaded, 16 * 6)
                    nc.gpsimd.tensor_tensor(base[:, :, :, :].rearrange("p u a k -> p u (a k)"), base[:, :, :, :].rearrange("p u a k -> p u (a k)"),
                                            bias[:, 0:18].unsqueeze(1).broadcast_to([P, UNITS, 18]), ALU.add).then_inc(filled, 1)

            @block.scalar
            def _(act):
                with when(act, far):
                    def take(g, s, j):
                        wait(act, turned, g, 1, -1)
                        nc.scalar.copy(rows[s][:, :, :], xp[:, ds(g * GROWS, GROWS + 1), :]).then_inc(rows_ready, 1)

                    def put(g, s, j):
                        wait(act, lower, g, 1, 1)
                        if j is not None:
                            wait(act, stored[s], j, 128, 0)
                        nc.scalar.copy(stage[s][:, :, :, 0, :],
                                       ps[s][0:TX, :, :].rearrange("p k n -> p (k n)")[:, 0:GROWS * P].rearrange("p (y b c) -> p y b c", y=GROWS, b=B)).then_inc(staged, 1)
                    take(0, 0, 0)
                    take(1, 1, 0)
                    put(0, 0, None)
                    take(2, 0, 0)
                    put(1, 1, None)
                    with act.Fori(1, NG // 2) as h:
                        take(h * 2 + 1, 1, 0)
                        put(h * 2, 0, h)
                        take(h * 2 + 2, 0, 0)
                        put(h * 2 + 1, 1, h)
                    put(NG - 1, 0, NG // 2)

            @block.vector
            def _(dve):
                with when(dve, far):
                    def put(g, s, j):
                        wait(dve, turned, g, 1, 1)
                        if j is not None:
                            wait(dve, stored[s], j, 128, 0)
                        nc.vector.tensor_copy(stage[s][:, :, :, 1, :],
                                              ps[s][0:TX, :, :].rearrange("p k n -> p (k n)")[:, P:(GROWS + 1) * P].rearrange("p (y b c) -> p y b c", y=GROWS, b=B)).then_inc(lower, 1)
                    put(0, 0, None)
                    put(1, 1, None)
                    with dve.Fori(1, NG // 2) as h:
                        put(h * 2, 0, h)
                        put(h * 2 + 1, 1, h)
                    put(NG - 1, 0, NG // 2)

            @block.tensor
            def _(pe):
                with when(pe, far):
                    pe.wait_ge(loaded, 16 * 6)
                    def turn(g, s):
                        wait(pe, rows_ready, g, 1, 1)
                        wait(pe, staged, g, 1, -1)
                        for y in range(GROWS + 1):
                            o = y * P
                            mm = nc.tensor.transpose(ps[s][0:TX, o // 512, o % 512:o % 512 + P], rows[s][:, y, :], ident[:, :])
                        mm.then_inc(turned, 1)
                    turn(0, 0)
                    turn(1, 1)
                    with pe.Fori(1, NG // 2) as h:
                        turn(h * 2, 0)
                        turn(h * 2 + 1, 1)
                    turn(NG - 1, 0)

        with ExitStack() as ctx:
            sem = lambda n: ctx.enter_context(nc.semaphore("df_" + n))
            sbc = lambda n, s, dt=F: ctx.enter_context(nc.sbuf_tensor("df_" + n, s, dt))
            psum = lambda n, s: ctx.enter_context(nc.psum_tensor("df_" + n, s, F))
            xs = [sbc(f"xs{i}", [3 * C, B, TR + 2, W]) for i in range(2)]
            pos = sbc("pos", [P, UNITS, 2, TAPS])
            logit = sbc("logit", [P, UNITS, TAPS])
            msk = sbc("msk", [P, UNITS, TAPS])
            ii = sbc("ii", [P, UNITS, 2, TAPS], I32)
            fl = sbc("fl", [P, UNITS, 2, TAPS])
            lt = sbc("lt", [P, UNITS, 2, TAPS])
            ixf = sbc("ixf", [P, UNITS, TAPS])
            gy = sbc("gy", [P, 2, UNITS, TAPS])
            ixu = [sbc(f"ixu{i}", [P, UNITS, TAPS], U32) for i in range(2)]
            wt = [sbc(f"wt{i}", [P, UNITS, TAPS, 4]) for i in range(2)]
            gat = [sbc(f"gat{i}", [P, TAPS, 4, C]) for i in range(RING)]
            gts = [sbc(f"gts{i}", [P, TAPS, P]) for i in range(2)]
            cps = [psum(f"cps{i}", [P, 512]) for i in range(2)]
            tps = psum("tps", [P, 3, 512])
            ops = [psum(f"ops{i}", [P, 512]) for i in range(2)]
            strip_in = [sem("strip_in0"), sem("strip_in1")]
            conv_done, conv_read, logit_ready, mask_ready, chain = sem("conv_done"), sem("conv_read"), sem("logit_ready"), sem("mask_ready"), sem("chain")
            coords_ready, slot_free = sem("coords_ready"), sem("slot_free")
            gathered = [sem(f"gathered{i}") for i in range(RING)]
            weighted, turned, turned_sb, mixed, added = sem("weighted"), sem("turned"), sem("turned_sb"), sem("mixed"), sem("added")
            block = ctx.enter_context(nc.Block())

            def strips(eng, body):
                body(0, 0, True, False)
                with eng.Fori(0, NSTRIP // 2 - 1) as h:
                    body(h * 2 + 1, 1, False, False)
                    body(h * 2 + 2, 0, False, False)
                body(NSTRIP - 1, 1, False, True)

            @block.sync
            def _(sp):
                with when(sp, far):
                    def load(s, i, first, last):
                        wait(sp, conv_done, s, 1, -1)
                        for dx in range(3):
                            for b in range(B):
                                sp.dma_start(xs[i][C * dx:C * dx + C, b, :, :],
                                             xn_d[C * b:C * b + C, ds(s * TR + EDGE - 1, TR + 2), EDGE - 1 + dx:EDGE - 1 + dx + W]
                                             ).then_inc(strip_in[i], 16)
                    strips(sp, load)

            @block.tensor
            def _(pe):
                with when(pe, far):
                    def conv_strip(s, i, half):
                        wait(pe, strip_in[i], half, LOADS, LOADS)
                        wait(pe, conv_read, s, 4, 0)
                        for t in range(TPS):
                            for b in range(B):
                                u = t * B + b
                                for dy in range(3):
                                    mm = nc.tensor.matmul(cps[u // 12][:, 27 * (u % 12):27 * (u % 12) + 27],
                                                          xs[i][:, b, :, :].rearrange("p r c -> p (r c)")[:, dy * W + P * t:dy * W + P * t + P], wc[:, dy, :],
                                                          start=(dy == 0), stop=(dy == 2))
                        mm.then_inc(conv_done, 1)

                    def turn(s, u):
                        wait(pe, weighted, s, UNITS, u + 1)
                        wait(pe, turned_sb, s, UNITS, u)
                        for k in range(TAPS):
                            mm = nc.tensor.transpose(tps[:, k // 4, P * (k % 4):P * (k % 4) + P], gat[u % RING][:, k, :, :], ident[:, :])
                        mm.then_inc(turned, 1)

                    def mix(s, u):
                        t, b = u // B, u % B
                        wait(pe, turned_sb, s, UNITS, u + 1)
                        if b == 0:
                            wait(pe, added, s, TPS, t - 1)
                        for k in range(TAPS):
                            mm = nc.tensor.matmul(ops[t % 2][C * b:C * b + C, 0:P], wd[:, k, :], gts[u % 2][:, k, :],
                                                  start=(k == 0), stop=(k == TAPS - 1))
                        mm.then_inc(mixed, 1)

                    def strip(s, i, half, last):
                        if not last:
                            conv_strip(s + 1, 1 - i, half)
                        for u in range(UNITS):
                            turn(s, u)
                            mix(s, u)
                    conv_strip(0, 0, 0)
                    strip(0, 0, 0, False)
                    with pe.Fori(0, NSTRIP // 2 - 1) as h:
                        strip(h * 2 + 1, 1, h + 1, False)
                        strip(h * 2 + 2, 0, h + 1, False)
                    strip(NSTRIP - 1, 1, 0, True)

            @block.scalar
            def _(act):
                with when(act, far):
                    def sigmoid(s):
                        wait(act, logit_ready, s, 1, 1)
                        nc.scalar.activation(msk[:, :, :], logit[:, :, :], ACT.Sigmoid).then_inc(mask_ready, 1)

                    def strip(s, i, first, last):
                        if not last:
                            sigmoid(s + 1)
                        for u in range(UNITS):
                            wait(act, turned, s, UNITS, u + 1)
                            wait(act, mixed, s, UNITS, u - 1)
                            nc.scalar.copy(gts[u % 2][:, :, :].rearrange("p k n -> p (k n)"),
                                           tps[:, :, :].rearrange("p k n -> p (k n)")[:, 0:TAPS * P]).then_inc(turned_sb, 1)
                    sigmoid(0)
                    strips(act, strip)

            @block.gpsimd
            def _(pool):
                with when(pool, far):
                    def strip(s, i, first, last):
                        wait(pool, coords_ready, s, 1, 1)
                        for u in range(UNITS):
                            wait(pool, turned, s, UNITS, u + 1 - RING)
                            pool.sem_inc(slot_free, 1)
                            for k in range(TAPS):
                                pool.indirect_dma_start(gat[u % RING][:, k, :, :].rearrange("p a c -> p (a c)"), None, table,
                                                        bass.IndirectOffsetOnAxis(ap=ixu[i][:, u, k:k + 1], axis=0)
                                                        ).then_inc(gathered[u % RING], 16)
                    strips(pool, strip)

            @block.vector
            def _(dve):
                with when(dve, far):
                    STEPS = 13

                    def coords(s, i):
                        n = [0]

                        def link(ins):
                            n[0] += 1
                            ins.then_inc(chain, 1)
                            wait(dve, chain, s, STEPS, n[0])
                        wait(dve, conv_done, s, 1, 1)
                        wait(dve, mask_ready, s, 1, 0)
                        for h in range(2):
                            u0 = 12 * h
                            conv = cps[h][:, 0:324].rearrange("p (u o) -> p u o", u=12)
                            nc.vector.tensor_tensor(pos[:, u0:u0 + 12, :, :].rearrange("p u a k -> p u (a k)"), conv[:, :, 0:18],
                                                    base[:, u0:u0 + 12, :, :].rearrange("p u a k -> p u (a k)"), ALU.add).then_inc(conv_read, 1)
                            nc.vector.tensor_tensor(logit[:, u0:u0 + 12, :], conv[:, :, 18:27],
                                                    bias[:, 18:27].unsqueeze(1).broadcast_to([P, 12, 9]), ALU.add).then_inc(conv_read, 1)
                        wait(dve, conv_read, s, 4, 4)
                        nc.vector.tensor_scalar(base[:, :, 0, :], base[:, :, 0, :], float(TR), None, ALU.add).then_inc(logit_ready, 1)
                        link(nc.vector.tensor_scalar(pos[:, :, :, :], pos[:, :, :, :], -float(EDGE), float(H), ALU.max, ALU.min))
                        link(nc.vector.tensor_copy(ii[:, :, :, :], pos[:, :, :, :]))
                        link(nc.vector.tensor_copy(fl[:, :, :, :], ii[:, :, :, :]))
                        link(nc.vector.tensor_tensor(lt[:, :, :, :], pos[:, :, :, :], fl[:, :, :, :], ALU.is_lt))
                        link(nc.vector.tensor_tensor(fl[:, :, :, :], fl[:, :, :, :], lt[:, :, :, :], ALU.subtract))
                        link(nc.vector.tensor_tensor(pos[:, :, :, :], pos[:, :, :, :], fl[:, :, :, :], ALU.subtract))
                        link(nc.vector.scalar_tensor_tensor(ixf[:, :, :], fl[:, :, 0, :], float(TX), fl[:, :, 1, :], ALU.mult, ALU.add))
                        wait(dve, mask_ready, s, 1, 1)
                        link(nc.vector.tensor_tensor(ixu[i][:, :, :], ixf[:, :, :], ixb[:, :, :], ALU.add))
                        link(nc.vector.tensor_tensor(gy[:, 1, :, :], pos[:, :, 0, :], msk[:, :, :], ALU.mult))
                        link(nc.vector.tensor_tensor(gy[:, 0, :, :], msk[:, :, :], gy[:, 1, :, :], ALU.subtract))
                        link(nc.vector.tensor_tensor(wt[i][:, :, :, 3], gy[:, 1, :, :], pos[:, :, 1, :], ALU.mult))
                        link(nc.vector.tensor_tensor(wt[i][:, :, :, 2], gy[:, 0, :, :], pos[:, :, 1, :], ALU.mult))
                        link(nc.vector.tensor_tensor(wt[i][:, :, :, 1], gy[:, 1, :, :], wt[i][:, :, :, 3], ALU.subtract))
                        assert n[0] == STEPS
                        nc.vector.tensor_tensor(wt[i][:, :, :, 0], gy[:, 0, :, :], wt[i][:, :, :, 2], ALU.subtract).then_inc(coords_ready, 1)

                    def strip(s, i, first, last):
                        wait(dve, coords_ready, s, 1, 1)
                        if not last:
                            coords(s + 1, 1 - i)
                        for u in range(UNITS):
                            wait(dve, gathered[u % RING], s, 16 * TAPS * (UNITS // RING), 16 * TAPS * (u // RING + 1))
                            nc.vector.tensor_tensor(gat[u % RING][:, :, :, :], gat[u % RING][:, :, :, :],
                                                    wt[i][:, u, :, :].unsqueeze(3).broadcast_to([P, TAPS, 4, C]), ALU.mult).then_inc(weighted, 1)
                            if u % B == 1 and u > B:
                                residual(s, u // B - 1)
                        residual(s, TPS - 1)

                    def residual(s, t):
                        wait(dve, mixed, s, UNITS, B * t + B)
                        xv = x_sb[:, ds(s * (TR * W) + P * t, P)]
                        nc.vector.tensor_tensor(xv, xv, ops[t % 2][:, 0:P], ALU.add).then_inc(added, 1)
                    coords(0, 0)
                    strips(dve, strip)


def host_l1(ow, ob, mw, mb, dw):
    wk = np.concatenate([ow[0::2], ow[1::2], mw], 0)
    convw = np.ascontiguousarray(wk.transpose(3, 1, 2, 0).reshape(3 * C, 3, 27))
    bias = np.tile(np.concatenate([ob[0::2], ob[1::2], mb]), (P, 1))
    dcn = np.tile(dw.reshape(C, C, 9).transpose(1, 2, 0), (4, 1, 1))
    p = np.arange(P)
    k = np.arange(9)
    u = np.arange(UNITS)
    px = P * (u // B)[None, :] + p[:, None]
    r, c = px // W, px % W
    coord = np.zeros((P, UNITS, 2, 9), np.float32)
    coord[:, :, 0, :] = r[:, :, None] - 1 + (k // 3)[None, None]
    coord[:, :, 1, :] = c[:, :, None] - 1 + (k % 3)[None, None]
    ixb = np.zeros((P, UNITS, 9), np.float32)
    ixb[:] = (1 + (u % B) * TROWS * TX + EDGE * TX + EDGE)[None, :, None]
    return dict(convw=convw, bias=np.ascontiguousarray(bias), coord=coord, ixb=ixb, dcn=np.ascontiguousarray(dcn))



F16 = mybir.dt.float16
DR = 4
DPX = DR * W
DTILES = H // DR
BK = B * TAPS
LOW = 64
PROWS = LOW + BK
UNIT = 32.0


def stage_deform_near(nc, x_sb, convw, convb, rep, sel, dcn, shifts, ident_d, x_save, far):
    with ExitStack() as ctx:
        sb = lambda n, s, dt=F: ctx.enter_context(nc.sbuf_tensor("dn_" + n, s, dt))
        sem = lambda n: ctx.enter_context(nc.semaphore("dn_" + n))
        psum = lambda n, s: ctx.enter_context(nc.psum_tensor("dn_" + n, s, F))
        xp = sb("xp", [P, H + 2 * EDGE, W + 2 * EDGE])
        stage_norm(nc, "gn1", x_sb, xp, EDGE)
        wconv = sb("wconv", [P, TAPS, 3 * BK])
        bconv = sb("bconv", [3 * BK, 1])
        repw = sb("repw", [3 * BK, 3, PROWS])
        self32 = sb("self32", [PROWS, TAPS, P])
        selw = sb("selw", [PROWS, TAPS, P], F16)
        wd = sb("wd", [P, TAPS, P])
        shift = sb("shift", [PROWS, 3])
        ident = sb("ident", [P, P])
        maps = sb("maps", [3 * BK, DPX])
        hat_y = sb("hat_y", [PROWS, 3, DPX])
        hat_x = sb("hat_x", [PROWS, 3, DPX])
        mask = sb("mask", [PROWS, DPX])
        corner = sb("corner", [PROWS, 3, 3, DPX])
        parts = [sb(f"parts{i}", [PROWS, 3, 3, DPX], F16) for i in range(2)]
        prod = [sb(f"prod{i}", [P, 9, DPX]) for i in range(2)]
        part_sum = [sb(f"part_sum{i}", [P, 4, DPX]) for i in range(2)]
        most = sb("most", [PROWS, 2 * DTILES])
        top = sb("top", [PROWS, 1])
        peak = sb("peak", [1, 1])
        wps = [psum(f"wps{i}", [P, 3, 512]) for i in range(2)]
        ops = psum("ops", [P, 512])
        aps = psum("aps", [P, 512])
        loaded, saved, wd_zero, sel_ready = sem("loaded"), sem("saved"), sem("wd_zero"), sem("sel_ready")
        conv_done, maps_ready, copied = sem("conv_done"), sem("maps_ready"), sem("copied")
        dist_ready, mask_ready, hats_ready, most_ready = sem("dist_ready"), sem("mask_ready"), sem("hats_ready"), sem("most_ready")
        scaled, corner_ready, high_ready, parts_ready = sem("scaled"), sem("corner_ready"), sem("high_ready"), sem("parts_ready")
        weights_ready, products, pairs_done, last_done = sem("weights_ready"), sem("products"), sem("pairs_done"), sem("last_done")
        contracted, added, top_ready, turned = sem("contracted"), sem("added"), sem("top_ready"), sem("turned")
        block = ctx.enter_context(nc.Block())

        def tiles(eng, body):
            body(0, 0, 0)
            body(1, 1, 0)
            with eng.Fori(1, DTILES // 2 - 1) as h:
                body(h * 2, 0, 0)
                body(h * 2 + 1, 1, 0)
            body(DTILES - 2, 0, 1)
            body(DTILES - 1, 1, 2)

        @block.sync
        def _(sp):
            sp.dma_start(x_save, x_sb[:, :]).then_inc(saved, 16)
            for dst, src in ((wconv[:, :, :], convw), (bconv[:, :], convb), (repw[:, :, :], rep), (self32[:, :, :], sel),
                             (wd[:, :, :], dcn), (shift[:, :], shifts), (ident[:, :], ident_d)):
                sp.dma_start(dst, src).then_inc(loaded, 16)
            sp.wait_ge(saved, 16)

        LOADED = 16 * 7

        @block.tensor
        def _(pe):
            def conv(j, ky):
                if ky == 0:
                    wait(pe, mask_ready, j, 1, 0)
                for kx in range(3):
                    k = 3 * ky + kx
                    mm = nc.tensor.matmul(aps[0:3 * BK, 0:DPX], wconv[:, k, :], xp[:, ds(j * DR + (EDGE - 1 + ky), DR), EDGE - 1 + kx:EDGE - 1 + kx + W],
                                          start=(k == 0), stop=(k == 8))
                if ky == 2:
                    mm.then_inc(conv_done, 1)

            def copy_rows(j, a):
                if a == 0:
                    wait(pe, maps_ready, j, 1, 1)
                else:
                    wait(pe, dist_ready, j, 6, 3 * a)
                nc.tensor.matmul(aps[0:PROWS, 0:DPX], repw[:, a, :], maps[:, :], start=True, stop=True).then_inc(copied, 1)

            def prepare(j, slot):
                if 1 <= slot <= 3:
                    conv(j, slot - 1)
                if slot >= 5 and slot < 8:
                    copy_rows(j, slot - 5)

            def weights(t, i, k, sy):
                n = 3 * k + sy
                if n == 0:
                    wait(pe, parts_ready, t, 3, 3)
                wait(pe, products, t, 27, n - 1)
                for sx in range(3):
                    mm = nc.tensor.matmul(wps[(n + i) % 2][:, sx, 0:DPX], selw[:, k, :], parts[i][:, sy, sx, :], start=True, stop=True)
                mm.then_inc(weights_ready, 1)

            def contract(t, k, i, lo, hi):
                tt, kk = (t, k) if k >= 0 else (t + (-1), k + TAPS)
                if k < 0 and isinstance(t, int) and t == 0:
                    return
                ii = i if k >= 0 else 1 - i
                s = (TAPS * ii + kk) % 2
                if lo == 0:
                    wait(pe, pairs_done, tt, TAPS, kk + 1)
                    if kk == 0:
                        wait(pe, added, tt, 1, 0)
                if hi == 4:
                    wait(pe, last_done, tt, TAPS, kk + 1)
                for q in range(lo, hi):
                    mm = nc.tensor.matmul(ops[:, 0:DPX], wd[:, kk, :], part_sum[s][:, q, :],
                                          start=(kk == 0 and q == 0), stop=(kk == TAPS - 1 and q == 3))
                if hi == 4:
                    mm.then_inc(contracted, 1)

            def tile(t, i, last):
                for k in range(TAPS):
                    weights(t, i, k, 0)
                    contract(t, k - 2, i, 0, 1)
                    weights(t, i, k, 1)
                    contract(t, k - 2, i, 1, 2)
                    weights(t, i, k, 2)
                    contract(t, k - 2, i, 2, 4)
                    if not last:
                        prepare(t + 2, k)
                if last == 2:
                    for k in (7, 8):
                        contract(t, k, i, 0, 4)
            pe.wait_ge(loaded, LOADED)
            pe.wait_ge(sel_ready, 1)
            for j in range(2):
                for slot in range(TAPS):
                    prepare(j, slot)
            tiles(pe, tile)
            pe.wait_ge(top_ready, 1)
            nc.tensor.transpose(aps[0:1, 0:PROWS], top[:, :], ident[0:PROWS, 0:PROWS]).then_inc(turned, 1)

        @block.scalar
        def _(act):
            def high(j, i):
                for sy in range(3):
                    wait(act, corner_ready, j, 3, sy + 1)
                    if sy == 0:
                        wait(act, weights_ready, j, 27, -27)
                    nc.scalar.copy(parts[i][:, sy, :, :], corner[:, sy, :, :]).then_inc(high_ready, 1)

            def distances(j):
                wait(act, conv_done, j, 1, 1)
                nc.scalar.activation(maps[:, :], aps[0:3 * BK, 0:DPX], ACT.Identity, bias=bconv[:, 0:1]).then_inc(maps_ready, 1)
                for a, hat in enumerate((hat_y, hat_x)):
                    wait(act, copied, j, 3, a + 1)
                    if a == 0:
                        wait(act, corner_ready, j, 3, 0)
                    for s in range(3):
                        nc.scalar.activation(hat[:, s, :], aps[0:PROWS, 0:DPX], ACT.Abs, bias=shift[:, s:s + 1], scale=UNIT).then_inc(dist_ready, 1)
                wait(act, copied, j, 3, 3)
                nc.scalar.activation(mask[:, :], aps[0:PROWS, 0:DPX], ACT.Sigmoid).then_inc(mask_ready, 1)

            def tile(t, i, last):
                if last < 2:
                    high(t + 1, 1 - i)
                if not last:
                    distances(t + 2)
            act.wait_ge(loaded, LOADED)
            nc.scalar.copy(selw[:, :, :], self32[:, :, :]).then_inc(sel_ready, 1)
            distances(0)
            high(0, 0)
            distances(1)
            tiles(act, tile)

        @block.gpsimd
        def _(pool):
            def prepare(j, i, slot, paired):
                if slot == 0:
                    wait(pool, hats_ready, j, 2, 1)
                    wait(pool, mask_ready, j, 1, 1)
                    nc.gpsimd.tensor_tensor(hat_y[:, :, :], hat_y[:, :, :], mask[:, :].unsqueeze(1).broadcast_to([PROWS, 3, DPX]),
                                            ALU.mult).then_inc(scaled, 1)
                elif slot <= 3:
                    sy = slot - 1
                    if sy == 0:
                        wait(pool, hats_ready, j, 2, 2)
                        wait(pool, scaled, j, 1, 1)
                    nc.gpsimd.tensor_tensor(corner[:, sy, :, :], hat_x[:, :, :], hat_y[:, sy:sy + 1, :].broadcast_to([PROWS, 3, DPX]),
                                            ALU.mult).then_inc(corner_ready, 1)
                elif slot <= 6:
                    sy = slot - 4
                    wait(pool, high_ready, j, 3, sy + 1)
                    if sy == 0:
                        wait(pool, corner_ready, j, 3, 3)
                    if paired is not None:
                        wait(pool, pairs_done, *paired)
                    nc.gpsimd.tensor_tensor(parts[i][LOW:, sy, :, :], corner[LOW:, sy, :, :], parts[i][LOW:, sy, :, :],
                                            ALU.subtract).then_inc(parts_ready, 1)
                    wait(pool, parts_ready, j, 3, sy + 1)

            def tile(t, i, last):
                for k in range(TAPS):
                    g = (TAPS * i + k) % 2
                    wait(pool, products, t, 27, 3 * k + 3)
                    wait(pool, contracted, t, TAPS, k - 1)
                    nc.gpsimd.tensor_tensor(part_sum[g][:, :, :], prod[g][:, 0:4, :], prod[g][:, 4:8, :], ALU.add).then_inc(pairs_done, 1)
                    if last < 2:
                        prepare(t + 1, 1 - i, k, (t, TAPS, k + 1))
            for slot in range(7):
                prepare(0, 0, slot, None)
            tiles(pool, tile)

        @block.vector
        def _(dve):
            def hats(j, a):
                hat = (hat_y, hat_x)[a]
                wait(dve, dist_ready, j, 6, 3 * a + 3)
                nc.vector.tensor_reduce(most[:, ds(j * 2 + a, 1)], hat[:, 1, :], AX.X, ALU.max).then_inc(most_ready, 1)
                wait(dve, most_ready, j, 2, a + 1)
                nc.vector.tensor_scalar(hat[:, :, :], hat[:, :, :], UNIT, UNIT, ALU.min, ALU.subtract).then_inc(hats_ready, 1)

            def last_sum(t, k, i):
                if k < 0:
                    if isinstance(t, int) and t == 0:
                        return
                    t, k, i = t + (-1), k + TAPS, 1 - i
                g = (TAPS * i + k) % 2
                wait(dve, products, t, 27, 3 * k + 3)
                wait(dve, pairs_done, t, TAPS, k + 1)
                nc.vector.tensor_tensor(part_sum[g][:, 3, :], part_sum[g][:, 3, :], prod[g][:, 8, :], ALU.add).then_inc(last_done, 1)

            def residual(t):
                wait(dve, contracted, t, TAPS, TAPS)
                xv = x_sb[:, ds(t * DPX, DPX)]
                nc.vector.tensor_tensor(xv, xv, ops[:, 0:DPX], ALU.add).then_inc(added, 1)

            def tile(t, i, last):
                for k in range(TAPS):
                    ky, kx = k // 3, k % 3
                    g = (TAPS * i + k) % 2
                    for sy in range(3):
                        n = 3 * k + sy
                        if n == 7 and not (isinstance(t, int) and t == 0):
                            residual(t + (-1))
                        wait(dve, weights_ready, t, 27, n + 1)
                        if sy == 0:
                            wait(dve, pairs_done, t, TAPS, k - 1)
                            wait(dve, last_done, t, TAPS, k - 1)
                        row = xp[:, ds(t * DR + (ky + sy), DR), kx:kx + W]
                        near = bass.AP(row.tensor, row.offset, [row.ap[0], [1, 3], *row.ap[1:]])
                        nc.vector.tensor_tensor(prod[g][:, 3 * sy:3 * sy + 3, :].rearrange("p s (r c) -> p s r c", r=DR),
                                                wps[(n + i) % 2][:, :, 0:DPX].rearrange("p s (r c) -> p s r c", r=DR), near,
                                                ALU.mult).then_inc(products, 1)
                    last_sum(t, k - 1, i)
                    if k >= 7 and not last:
                        hats(t + 2, k - 7)
                if last == 2:
                    last_sum(t, 8, i)
                    residual(t)
            dve.wait_ge(saved, 16)
            for j in range(2):
                if j:
                    dve.wait_ge(corner_ready, 3)
                hats(j, 0)
                hats(j, 1)
            tiles(dve, tile)
            dve.wait_ge(most_ready, 2 * DTILES)
            nc.vector.tensor_reduce(top[:, :], most[:, :], AX.X, ALU.max).then_inc(top_ready, 1)
            dve.wait_ge(turned, 1)
            nc.vector.tensor_reduce(peak[:, :], aps[0:1, 0:PROWS], AX.X, ALU.max).then_inc(top_ready, 1)
            dve.wait_ge(top_ready, 2)
            nc.vector.tensor_scalar(far, peak[:, :], UNIT, None, ALU.is_ge)


def host_l1d(ow, ob, mw, mb, dw):
    w3 = np.stack([ow[0::2], ow[1::2], mw]).reshape(3, TAPS, C, 9)
    convw = np.zeros((B, C, 9, 3, TAPS, B), np.float32)
    wd = np.zeros((B, C, 9, B, C), np.float32)
    sel = np.zeros((PROWS, TAPS, P), np.float32)
    rep = np.zeros((3, TAPS, B, 3, PROWS), np.float32)
    for b in range(B):
        convw[b, :, :, :, :, b] = w3.transpose(2, 3, 0, 1)
        wd[b, :, :, b, :] = dw.reshape(C, C, 9).transpose(1, 2, 0)
        for k in range(TAPS):
            for r in (k * B + b, LOW + k * B + b):
                sel[r, k, C * b:C * b + C] = UNIT ** -2
                for a in range(3):
                    rep[a, k, b, a, r] = 1
    bias = np.repeat(np.stack([ob[0::2], ob[1::2], mb]).reshape(-1), B)[:, None]
    return dict(convw=convw.reshape(P, 9, 3 * BK), convb=np.ascontiguousarray(bias), rep=rep.reshape(3 * BK, 3, PROWS), sel=sel,
                dcnbd=wd.reshape(P, 9, P), shifts=np.tile(-UNIT * np.arange(-1, 2, dtype=np.float32), (PROWS, 1)))



KX, KY = 32, 16
M1 = M2 = 4
L1_IN, HIDN = C * M1 * M2 * 2, 128
FW = 2 * KY + 2 * M2
NG = 4
GX = KX // NG
MODES = GX * KY
ZN = KX * KY * 2
LRows = 8


def stage_fourier(nc, x_sb, fw_d, fh_d, ch_d, ih_d, iw_d, w1, w2, lin1, b1, lin2, b2, ident_d):
    with ExitStack() as outer:
        sb = lambda n, s, dt=F: outer.enter_context(nc.sbuf_tensor("fo_" + n, s, dt))
        ident = sb("ident", [P, P])
        fw = sb("fw", [W, FW])
        fh = sb("fh", [H, 2, 2 * KX])
        ch = sb("ch", [H, 2, 2 * M1])
        ih = sb("ih", [2 * KX, 2 * H])
        iw = sb("iw", [P, 4, W])
        wts = sb("wts", [P, C, GX, KY * 2])
        l1w = sb("l1w", [C, 2 * M1 * M2, HIDN])
        b1s = sb("b1s", [HIDN, 1])
        l2w = sb("l2w", [HIDN, C])
        b2s = sb("b2s", [P, 1])
        y = sb("y", [P, FW, H])
        yt = sb("yt", [H, FW, P])
        z = sb("z", [P, KX, KY, 2])
        zi = sb("zi", [P, B, GX, KY * 2])
        flat = sb("flat", [P, M1, M2, 2])
        fl = sb("fl", [C, B, 2 * M1 * M2])
        corr = sb("corr", [P, 1])
        with ExitStack() as ctx:
            sem = lambda n: ctx.enter_context(nc.semaphore("ff_" + n))
            sbc = lambda n, s, dt=F: ctx.enter_context(nc.sbuf_tensor("ff_" + n, s, dt))
            psum = lambda n, s: ctx.enter_context(nc.psum_tensor("ff_" + n, s, F))
            stats = sbc("stats", [P, 18, 6])
            agg = sbc("agg", [P, 8])
            rows = [sbc(f"rows{i}", [P, LRows, W]) for i in range(2)]
            xt = [sbc(f"xt{i}", [W, LRows, P]) for i in range(2)]
            tps = [psum(f"tps{i}", [P, 2, 512]) for i in range(2)]
            yps = [psum(f"yps{i}", [P, 512]) for i in range(2)]
            zps = [psum(f"zps{i}", [P, 512]) for i in range(2)]
            loaded, moved, root_ready, var_ready, step = sem("loaded"), sem("moved"), sem("root_ready"), sem("var_ready"), sem("step")
            stats_done = sem("stats_done")
            rows_ready, turned, xt_ready, y_done, y_sb = sem("rows_ready"), sem("turned"), sem("xt_ready"), sem("y_done"), sem("y_sb")
            yturned, yt_sb, z_done, z_sb = sem("yturned"), sem("yt_sb"), sem("z_done"), sem("z_sb")
            block = ctx.enter_context(nc.Block())
            mean, var, std, rstd, t = (agg[:, k:k + 1] for k in range(5))
            G8 = H // LRows

            @block.sync
            def _(sp):
                loads = [(ident[:, :], ident_d), (fw[:, :], fw_d), (fh[:, :, :], fh_d), (ch[:, :, :], ch_d), (ih[:, :], ih_d),
                         (iw[:, :, :], iw_d), (l1w[:, :, :], lin1.rearrange("(c j) n -> c j n", c=C)), (b1s[:, :], b1), (l2w[:, :], lin2), (b2s[:, :], b2)]
                for dst, src in loads:
                    sp.dma_start(dst, src).then_inc(loaded, 16)
                for g in range(NG):
                    w = (w1, w2)[g // 2]
                    k0 = GX * (g % 2)
                    sp.dma_start(wts[C * g:C * g + C, :, :, :].rearrange("i o k y -> i o (k y)"),
                                 w[:, :, k0:k0 + GX, :, :].rearrange("i o k y r -> i o (k y r)")).then_inc(loaded, 16)
                sp.wait_ge(loaded, 224)
                sp.wait_ge(z_sb, 3)
                for b in range(B):
                    for g in range(NG):
                        sp.dma_start(zi[C * g:C * g + C, b, :, :].rearrange("i k y -> i (k y)"),
                                     z[C * b:C * b + C, GX * g:GX * g + GX, :, :].rearrange("i k y r -> i (k y r)")).then_inc(moved, 16)
                    sp.dma_start(fl[:, b, :], flat[C * b:C * b + C, :, :, :].rearrange("c a b r -> c (a b r)")).then_inc(moved, 16)
                sp.wait_ge(moved, 16 * B * (NG + 1))

            @block.vector
            def _(dve):
                for k in range(18):
                    nc.vector.bn_stats(stats[:, k, :], x_sb[:, k * 512:(k + 1) * 512]).then_inc(stats_done, 1)
                dve.wait_ge(stats_done, 18)
                nc.vector.bn_aggr(agg[:, 0:2], stats[:, :, :]).then_inc(step, 1)
                dve.wait_ge(step, 1)
                nc.vector.tensor_scalar(var, var, 1e-5, None, ALU.add).then_inc(var_ready, 1)
                dve.wait_ge(root_ready, 1)
                nc.vector.reciprocal(rstd, std).then_inc(step, 1)
                dve.wait_ge(step, 2)
                nc.vector.tensor_tensor(t, rstd, rstd, ALU.mult).then_inc(step, 1)
                dve.wait_ge(step, 3)
                nc.vector.tensor_tensor(t, t, var, ALU.mult).then_inc(step, 1)
                dve.wait_ge(step, 4)
                nc.vector.tensor_scalar(t, t, -0.5, 1.5, ALU.mult, ALU.add).then_inc(step, 1)
                dve.wait_ge(step, 5)
                nc.vector.tensor_tensor(rstd, rstd, t, ALU.mult).then_inc(step, 1)
                dve.wait_ge(step, 6)

                def normalise(g, s):
                    wait(dve, turned, g, 1, -1)
                    nc.vector.tensor_scalar(rows[s][:, :, :].rearrange("p r c -> p (r c)"), x_sb[:, ds(g * (LRows * W), LRows * W)],
                                            mean, rstd, ALU.subtract, ALU.mult).then_inc(rows_ready, 1)

                def keep(g, s):
                    wait(dve, turned, g, 1, 1)
                    wait(dve, y_done, g, 1, -1)
                    nc.vector.tensor_copy(xt[s][:, :, :].rearrange("p r n -> p (r n)"), tps[s][0:W, :, :].rearrange("p k n -> p (k n)")).then_inc(xt_ready, 1)
                normalise(0, 0)
                normalise(1, 1)
                keep(0, 0)
                with dve.Fori(0, G8 // 2 - 1) as h:
                    normalise(h * 2 + 2, 0)
                    keep(h * 2 + 1, 1)
                    normalise(h * 2 + 3, 1)
                    keep(h * 2 + 2, 0)
                keep(G8 - 1, 1)
                for q in range(FW // 4):
                    dve.wait_ge(yturned, q + 1)
                    nc.vector.tensor_copy(yt[:, 4 * q:4 * q + 4, :].rearrange("p f n -> p (f n)"), tps[q % 2][0:H, 0, :]).then_inc(yt_sb, 1)

            @block.scalar
            def _(act):
                act.wait_ge(var_ready, 1)
                nc.scalar.activation(std, var, ACT.Sqrt).then_inc(root_ready, 1)

                def keep(g, s):
                    wait(act, y_done, g, 1, 1)
                    nc.scalar.copy(y[:, :, ds(g * LRows, LRows)], yps[s][:, 0:LRows * FW].rearrange("p (r f) -> p f r", r=LRows)).then_inc(y_sb, 1)
                with act.Fori(0, G8 // 2) as h:
                    keep(h * 2, 0)
                    keep(h * 2 + 1, 1)
                for k in range(2):
                    act.wait_ge(z_done, k + 1)
                    nc.scalar.copy(z[:, :, 8 * k:8 * k + 8, :], zps[k][:, :].rearrange("p (y k r) -> p k y r", y=8, r=2)).then_inc(z_sb, 1)
                act.wait_ge(z_done, 3)
                nc.scalar.copy(flat[:, :, :, :], yps[0][:, 0:2 * M1 * M2].rearrange("p (b a r) -> p a b r", b=M2, r=2)).then_inc(z_sb, 1)

            @block.tensor
            def _(pe):
                pe.wait_ge(loaded, 224)

                def turn(g, s):
                    wait(pe, rows_ready, g, 1, 1)
                    wait(pe, xt_ready, g, 1, -1)
                    for r in range(LRows):
                        mm = nc.tensor.transpose(tps[s][0:W, r // 4, P * (r % 4):P * (r % 4) + P], rows[s][:, r, :], ident[:, :])
                    mm.then_inc(turned, 1)

                def along_width(g, s):
                    wait(pe, xt_ready, g, 1, 1)
                    wait(pe, y_sb, g, 1, -1)
                    for r in range(LRows):
                        mm = nc.tensor.matmul(yps[s][:, FW * r:FW * r + FW], xt[s][:, r, :], fw[:, :], start=True, stop=True)
                    mm.then_inc(y_done, 1)
                turn(0, 0)
                turn(1, 1)
                along_width(0, 0)
                with pe.Fori(0, G8 // 2 - 1) as h:
                    turn(h * 2 + 2, 0)
                    along_width(h * 2 + 1, 1)
                    turn(h * 2 + 3, 1)
                    along_width(h * 2 + 2, 0)
                along_width(G8 - 1, 1)
                pe.wait_ge(y_sb, G8)
                for q in range(FW // 4):
                    if q == 0:
                        pe.wait_ge(xt_ready, G8)
                    if q >= 2:
                        pe.wait_ge(yt_sb, q - 1)
                    for f in range(4):
                        mm = nc.tensor.transpose(tps[q % 2][0:H, 0, P * f:P * f + P], y[:, 4 * q + f, :], ident[:, :])
                    mm.then_inc(yturned, 1)
                for k in range(KY):
                    pe.wait_ge(yt_sb, (2 * k + 1) // 4 + 1)
                    for part in range(2):
                        mm = nc.tensor.matmul(zps[k // 8][:, 64 * (k % 8):64 * (k % 8) + 64], yt[:, 2 * k + part, :], fh[:, part, :],
                                              start=(part == 0), stop=(part == 1))
                    if k % 8 == 7:
                        mm.then_inc(z_done, 1)
                pe.wait_ge(yt_sb, FW // 4)
                for k in range(M2):
                    for part in range(2):
                        mm = nc.tensor.matmul(yps[0][:, 8 * k:8 * k + 8], yt[:, 2 * KY + M2 * part + k, :], ch[:, part, :],
                                              start=(part == 0), stop=(part == 1))
                mm.then_inc(z_done, 1)

        with ExitStack() as ctx:
            sem = lambda n: ctx.enter_context(nc.semaphore("fb_" + n))
            sbc = lambda n, s, dt=F: ctx.enter_context(nc.sbuf_tensor("fb_" + n, s, dt))
            psum = lambda n, s: ctx.enter_context(nc.psum_tensor("fb_" + n, s, F))
            wst = [sbc(f"wst{i}", [P, C, KY, 2]) for i in range(2)]
            zst = [sbc(f"zst{i}", [P, 2, B, KY, 2]) for i in range(2)]
            o = sbc("o", [P, B, GX, KY * 2])
            hb = sbc("hb", [HIDN, B])
            g = sbc("g", [P, H, KY, 2])
            z2 = sbc("z2", [P, KY, 2, KX])
            ot = sbc("ot", [2 * KX, KY, P])
            gt = [sbc(f"gt{i}", [P, 4, P]) for i in range(2)]
            mps = [psum(f"mps{i}", [P, 512]) for i in range(2)]
            hps = psum("hps", [P, 512])
            cps = psum("cps", [P, 512])
            tps = [psum(f"tps{i}", [P, 512]) for i in range(2)]
            ops = [psum(f"ops{i}", [P, 512]) for i in range(2)]
            staged, mixed, o_sb, moved = sem("staged"), sem("mixed"), sem("o_sb"), sem("moved")
            h_done, h_ready, c_done, c_ready = (sem(n) for n in ("h_done", "h_ready", "c_done", "c_ready"))
            sorted_, oturned, ot_sb, g_done, g_sb = sem("sorted"), sem("oturned"), sem("ot_sb"), sem("g_done"), sem("g_sb")
            gturned, gt_sb, back, added = sem("gturned"), sem("gt_sb"), sem("back"), sem("added")
            zstaged, mix_begun = sem("zstaged"), sem("mix_begun")
            block = ctx.enter_context(nc.Block())

            @block.sync
            def _(sp):
                sp.wait_ge(o_sb, GX)
                for b in range(B):
                    for q in range(NG):
                        sp.dma_start(z[C * b:C * b + C, GX * q:GX * q + GX, :, :].rearrange("i k y r -> i (k y r)"),
                                     o[C * q:C * q + C, b, :, :].rearrange("i k y -> i (k y)")).then_inc(moved, 16)
                sp.wait_ge(moved, 256)

            @block.gpsimd
            def _(pool):
                pass

            @block.scalar
            def _(act):
                def stage(k, s):
                    wait(act, mixed, k, 1, -1)
                    nc.scalar.copy(wst[s][:, :, :, :].rearrange("p o y r -> p o (y r)"), wts[:, :, ds(k, 1), :].rearrange("p o k y -> p o (k y)")).then_inc(staged, 1)
                stage(0, 0)
                stage(1, 1)
                with act.Fori(1, GX // 2) as h:
                    stage(h * 2, 0)
                    stage(h * 2 + 1, 1)
                act.wait_ge(h_done, 1)
                nc.scalar.activation(hb[:, :], hps[:, 0:B], ACT.Gelu, bias=b1s[:, 0:1]).then_inc(h_ready, 1)
                act.wait_ge(moved, 256)
                nc.scalar.copy(z2[:, :, :, :], z[:, :, :, :].rearrange("p k y r -> p y r k")).then_inc(sorted_, 1)
                for q in range(KY // 2):
                    act.wait_ge(g_done, q + 1)
                    nc.scalar.copy(g[:, :, 2 * q:2 * q + 2, :],
                                   ops[q % 2][:, 0:4 * H].rearrange("p (y r h) -> p h y r", y=2, r=2)).then_inc(g_sb, 1)
                for q in range(H // 4):
                    act.wait_ge(gturned, q + 1)
                    if q >= 2:
                        act.wait_ge(back, q - 1)
                    nc.scalar.copy(gt[q % 2][:, 0, :], tps[q % 2][:, 0:P]).then_inc(gt_sb, 1)

            @block.vector
            def _(dve):
                def stage(k, s):
                    wait(dve, mixed, k, 1, -1)
                    v = zi[:, :, ds(k, 1), :].rearrange("p b k (y r) -> p (b k) y r", r=2)
                    nc.vector.tensor_copy(zst[s][:, 0, :, :, :], v).then_inc(zstaged, 1)
                    nc.vector.tensor_scalar(zst[s][:, 1, :, :, 0], v[:, :, :, 1], -1.0, None, ALU.mult).then_inc(zstaged, 1)
                    nc.vector.tensor_copy(zst[s][:, 1, :, :, 1], v[:, :, :, 0]).then_inc(zstaged, 1)

                def keep(k, s):
                    wait(dve, mixed, k, 1, 1)
                    nc.vector.tensor_copy(o[:, :, ds(k, 1), :].rearrange("p b k (y r) -> p (b k) y r", r=2),
                                          mps[s][:, 0:KY * 2 * B].rearrange("p (y b r) -> p b y r", y=KY, r=2)).then_inc(o_sb, 1)
                stage(0, 0)
                stage(1, 1)
                keep(0, 0)
                with dve.Fori(0, GX // 2 - 1) as h:
                    stage(h * 2 + 2, 0)
                    keep(h * 2 + 1, 1)
                    stage(h * 2 + 3, 1)
                    keep(h * 2 + 2, 0)
                keep(GX - 1, 1)
                dve.wait_ge(c_done, 1)
                nc.vector.tensor_tensor(corr[:, :], cps[:, 0:1], b2s[:, :], ALU.add).then_inc(c_ready, 1)
                for q in range(KY // 4):
                    dve.wait_ge(oturned, q + 1)
                    nc.vector.tensor_copy(ot[:, 4 * q:4 * q + 4, :].rearrange("p y n -> p (y n)"), tps[q % 2][0:2 * KX, :]).then_inc(ot_sb, 1)
                dve.wait_ge(c_ready, 1)
                for q in range(H // 4):
                    dve.wait_ge(back, q + 1)
                    xv = x_sb[:, 4 * W * q:4 * W * q + 4 * W]
                    nc.vector.scalar_tensor_tensor(xv, ops[q % 2][:, 0:4 * W], corr[:, 0:1], xv, ALU.add, ALU.add).then_inc(added, 1)

            @block.tensor
            def _(pe):
                def mix(k, s):
                    wait(pe, staged, k, 1, 1)
                    wait(pe, zstaged, k, 3, 3)
                    wait(pe, o_sb, k, 1, -1)
                    pe.sem_inc(mix_begun, 1)
                    for m in range(KY):
                        for part in range(2):
                            for q in range(NG):
                                r = slice(C * q, C * q + C)
                                mm = nc.tensor.matmul(mps[s][r, 2 * B * m:2 * B * m + 2 * B], wst[s][r, :, m, part],
                                                      zst[s][r, part, :, m, :], start=(part == 0), stop=(part == 1))
                    mm.then_inc(mixed, 1)
                mix(0, 0)
                mix(1, 1)
                with pe.Fori(1, GX // 2) as h:
                    mix(h * 2, 0)
                    mix(h * 2 + 1, 1)
                for j in range(2 * M1 * M2):
                    mm = nc.tensor.matmul(hps[:, 0:B], l1w[:, j, :], fl[:, :, j], start=(j == 0), stop=(j == 2 * M1 * M2 - 1))
                mm.then_inc(h_done, 1)
                pe.wait_ge(h_ready, 1)
                for b in range(B):
                    mm = nc.tensor.matmul(cps[C * b:C * b + C, 0:1], l2w[:, :], hb[:, b:b + 1], start=True, stop=True)
                mm.then_inc(c_done, 1)
                pe.wait_ge(sorted_, 1)
                for q in range(KY // 4):
                    if q >= 2:
                        pe.wait_ge(ot_sb, q - 1)
                    for j in range(4):
                        mm = nc.tensor.transpose(tps[q % 2][0:2 * KX, P * j:P * j + P], z2[:, 4 * q + j, :, :].rearrange("p r k -> p (r k)"), ident[:, :])
                    mm.then_inc(oturned, 1)
                for q in range(KY // 2):
                    pe.wait_ge(ot_sb, q // 2 + 1)
                    if q >= 2:
                        pe.wait_ge(g_sb, q - 1)
                    for j in range(2):
                        mm = nc.tensor.matmul(ops[q % 2][:, 2 * H * j:2 * H * j + 2 * H], ot[:, 2 * q + j, :], ih[:, :], start=True, stop=True)
                    mm.then_inc(g_done, 1)
                pe.wait_ge(g_sb, KY // 2)
                pe.wait_ge(ot_sb, KY // 4)

                def turn(q):
                    if q >= 2:
                        pe.wait_ge(gt_sb, q - 1)
                    nc.tensor.transpose(tps[q % 2][:, 0:P], g[:, 4 * q:4 * q + 4, :, :].rearrange("p h y r -> p (h y r)"), ident[:, :]).then_inc(gturned, 1)

                def along_width(q):
                    pe.wait_ge(gt_sb, q + 1)
                    if q >= 2:
                        pe.wait_ge(added, q - 1)
                    nc.tensor.matmul(ops[q % 2][:, 0:4 * W], gt[q % 2][:, 0, :], iw[:, :, :].rearrange("p a w -> p (a w)"), start=True, stop=True).then_inc(back, 1)
                turn(0)
                for q in range(H // 4):
                    if q + 1 < H // 4:
                        turn(q + 1)
                    along_width(q)


def host_l2():
    f8 = np.float64
    def cft(n, f):
        L, M = 4, 8
        seg = 1.0 / L
        starts = np.arange(L) / L
        k = np.arange(M)
        nodes = -np.cos((2 * k + 1) * np.pi / (2 * M))
        T = np.cos(k[:, None] * np.arccos(nodes)[None])
        ang = nodes[:, None] * (f * 2 * np.pi * seg / 2)[None]
        Wc = (T @ np.cos(ang) - 1j * (T @ np.sin(ang))) * (seg / 2)
        tc = np.linspace(0, 1, n)
        ts = starts[:, None] + seg / 2 * (nodes[None] + 1)
        right = np.clip(np.searchsorted(tc, ts), 0, n - 1)
        left = np.clip(right - 1, 0, n - 1)
        wr = (ts - tc[left]) / (tc[right] - tc[left])
        ph = np.exp(-2j * np.pi * starts[:, None] * f[None])
        out = np.zeros((n, len(f)), complex)
        for l in range(L):
            for m in range(M):
                v = Wc[m] * ph[l]
                out[left[l, m]] += (1 - wr[l, m]) * v
                out[right[l, m]] += wr[l, m] * v
        return out
    w = np.arange(W)
    ky = np.arange(KY)
    th = 2 * np.pi * w[:, None] * ky[None] / W
    fw = np.zeros((W, FW))
    fw[:, 0:2 * KY:2], fw[:, 1:2 * KY:2] = np.cos(th), -np.sin(th)
    cw = cft(W, np.arange(M2).astype(f8))
    fw[:, 2 * KY:2 * KY + M2], fw[:, 2 * KY + M2:] = cw.real, cw.imag
    kx = np.concatenate([np.arange(16), np.arange(H - 16, H)])
    h = np.arange(H)
    t = 2 * np.pi * ((h[:, None] * kx[None]) % H) / H
    fh = np.zeros((H, 2, KX, 2))
    fh[:, 0, :, 0], fh[:, 0, :, 1] = np.cos(t), -np.sin(t)
    fh[:, 1, :, 0], fh[:, 1, :, 1] = np.sin(t), np.cos(t)
    cc = cft(H, np.array([0., 1., -2., -1.]))
    ch = np.zeros((H, 2, M1, 2))
    ch[:, 0, :, 0], ch[:, 0, :, 1] = cc.real, cc.imag
    ch[:, 1, :, 0], ch[:, 1, :, 1] = -cc.imag, cc.real
    ih = np.zeros((2, KX, 2, H))
    ih[0, :, 0], ih[0, :, 1] = np.cos(t).T, np.sin(t).T
    ih[1, :, 0], ih[1, :, 1] = -np.sin(t).T, np.cos(t).T
    ih /= H
    c = np.where(ky == 0, 1.0, 2.0) / W
    i1 = np.zeros((KY, 2, W))
    i1[:, 0], i1[:, 1] = c[:, None] * np.cos(th).T, -c[:, None] * np.sin(th).T
    iw = np.zeros((4, KY * 2, 4, W))
    for a in range(4):
        iw[a, :, a] = i1.reshape(KY * 2, W)
    r = dict(fw=fw, fh=fh.reshape(H, 2, 2 * KX), ch=ch.reshape(H, 2, 2 * M1), ih=ih.reshape(2 * KX, 2 * H), iw=iw.reshape(P, 4, W))
    return {k: np.ascontiguousarray(v).astype(np.float32) for k, v in r.items()}


EDGE1 = 1
HID = 2 * C
KS = 3 * C + 3
STRIP = TR * W
NPP = STRIP // P
HALF = STRIP // 2


def stage_fftconv(nc, x_sb, whid, wdw, bdw, wout, bout, ones_d, dft_d, xn_d, out):
    with ExitStack() as outer:
        sb = lambda n, s, dt=F: outer.enter_context(nc.sbuf_tensor("fc_" + n, s, dt))
        wk = sb("wk", [KS, 3, 3 * HID])
        wtmp = sb("wtmp", [KS, 3 * HID])
        bd = sb("bd", [KS, 3 * HID])
        wo = sb("wo", [P, 2, P])
        bo = sb("bo", [P, 1])
        dft = sb("dft", [P, 4, P])
        with ExitStack() as ctx:
            xp = ctx.enter_context(nc.sbuf_tensor("fc_xp", [P, H + 2, W + 2], F))
            stage_norm(nc, "gn3", x_sb, xp, 1)
            sem = lambda n: ctx.enter_context(nc.semaphore("fl_" + n))
            loaded, zeroed, stepped = sem("loaded"), sem("zeroed"), sem("stepped")
            block = ctx.enter_context(nc.Block())

            @block.gpsimd
            def _(pool):
                nc.gpsimd.memset(wo[:, :, :], 0.0).then_inc(zeroed, 1)

            @block.sync
            def _(sp):
                sp.dma_start(xn_d, xp[:, :, :]).then_inc(loaded, 16)
                for dst, src in ((wk[:, :, :], wdw), (wtmp[:, :], whid), (bd[:, :], bdw), (bo[:, :], bout), (dft[:, :, :], dft_d)):
                    sp.dma_start(dst, src).then_inc(loaded, 16)
                sp.wait_ge(zeroed, 1)
                for b in range(B):
                    sp.dma_start(wo[HID * (b % 2):HID * (b % 2) + HID, b // 2, C * b:C * b + C], wout).then_inc(loaded, 16)
                sp.wait_ge(loaded, 160)

            @block.vector
            def _(dve):
                dve.wait_ge(loaded, 160)
                nc.vector.tensor_tensor(wk[:, :, :], wk[:, :, :], wtmp[:, :].unsqueeze(1).broadcast_to([KS, 3, 3 * HID]), ALU.mult).then_inc(stepped, 1)
                dve.wait_ge(stepped, 1)
                nc.vector.tensor_tensor(wk[:, 1, :], wk[:, 1, :], bd[:, :], ALU.add)
                nc.vector.tensor_scalar(x_sb[:, :], x_sb[:, :], bo[:, 0:1], None, ALU.add)

        with ExitStack() as ctx:
            sem = lambda n: ctx.enter_context(nc.semaphore("fc_" + n))
            sbc = lambda n, s, dt=F: ctx.enter_context(nc.sbuf_tensor("fc_" + n, s, dt))
            psum = lambda n, s: ctx.enter_context(nc.psum_tensor("fc_" + n, s, F))
            xs = [sbc(f"xs{i}", [KS, B, TR + 2, W]) for i in range(2)]
            qk = [sbc(f"qk{i}", [P, B, 2 * HID]) for i in range(2)]
            spec = [sbc(f"spec{i}", [P, 2, B, 2 * HID]) for i in range(2)]
            prod = [sbc(f"prod{i}", [P, 2, 2, B, HID]) for i in range(2)]
            spo = [sbc(f"spo{i}", [P, 2, B, HID]) for i in range(2)]
            vsb = sbc("vsb", [P, 2, STRIP])
            vo = sbc("vo", [P, 2, STRIP])
            qps = [psum(f"qps{i}", [P, 512]) for i in range(2)]
            fps = psum("fps", [P, 2, 512])
            ips = [psum(f"ips{i}", [P, 512]) for i in range(2)]
            vps = psum("vps", [P, 512])
            ops = psum("ops", [P, 512])
            strip_in = [sem("strip_in0"), sem("strip_in1")]
            qk_done, qk_sb, spec_done, spec_sb = sem("qk_done"), sem("qk_sb"), sem("spec_done"), sem("spec_sb")
            mul_done, comb_done, back_done, vo_done = sem("mul_done"), sem("comb_done"), sem("back_done"), sem("vo_done")
            v_done, v_sb, out_done, x_done, stored = sem("v_done"), sem("v_sb"), sem("out_done"), sem("x_done"), sem("stored")
            block = ctx.enter_context(nc.Block())

            def strips(eng, body):
                body(0, 0, 0, True, False)
                with eng.Fori(0, NSTRIP // 2 - 1) as h:
                    body(h * 2 + 1, 1, h, False, False)
                    body(h * 2 + 2, 0, h + 1, False, False)
                body(NSTRIP - 1, 1, NSTRIP // 2 - 1, False, True)

            LOADS = 16 * (3 * B + 1)

            @block.sync
            def _(sp):
                def load(s, i, n, first, last):
                    wait(sp, v_done, s, 4, -4)
                    for dx in range(3):
                        for b in range(B):
                            sp.dma_start(xs[i][C * dx:C * dx + C, b, :, :],
                                         xn_d[C * b:C * b + C, ds(s * TR, TR + 2), dx:dx + W]).then_inc(strip_in[i], 16)
                    sp.dma_start(xs[i][3 * C:KS, :, :, :].rearrange("p b r c -> p b (r c)"),
                                 ones_d[:, :, ds(s * STRIP, (TR + 2) * W)]).then_inc(strip_in[i], 16)
                def store(s, i, n, first, last):
                    wait(sp, x_done, s, 2, 2)
                    sp.dma_start(out[:, ds(s * STRIP, STRIP)], x_sb[:, ds(s * STRIP, STRIP)]).then_inc(stored, 16)
                load(0, 0, 0, True, False)
                load(1, 1, 0, False, False)
                with sp.Fori(0, NSTRIP // 2 - 1) as h:
                    load(h * 2 + 2, 0, h + 1, False, False)
                    store(h * 2, 0, h, False, False)
                    load(h * 2 + 3, 1, h + 1, False, False)
                    store(h * 2 + 1, 1, h, False, False)
                store(NSTRIP - 2, 0, 0, False, False)
                store(NSTRIP - 1, 1, 0, False, True)
                sp.wait_ge(stored, 16 * NSTRIP)

            @block.gpsimd
            def _(pool):
                def combine(s, j):
                    m = j % 2
                    wait(pool, mul_done, s, NPP * 2, 2 * j + 2)
                    wait(pool, back_done, s, NPP, j - 1)
                    nc.gpsimd.tensor_tensor(spo[m][:, 0, :, :], prod[m][:, 0, 0, :, :], prod[m][:, 1, 1, :, :], ALU.subtract).then_inc(comb_done, 1)
                    nc.gpsimd.tensor_tensor(spo[m][:, 1, :, :], prod[m][:, 0, 1, :, :], prod[m][:, 1, 0, :, :], ALU.add).then_inc(comb_done, 1)

                def body(s, i, n, first, last):
                    for j in range(NPP):
                        combine(s, j)
                strips(pool, body)

            @block.scalar
            def _(act):
                def spectra(s, j):
                    m = j % 2
                    wait(act, spec_done, s, NPP, j + 1)
                    wait(act, mul_done, s, NPP * 2, 2 * j - 2)
                    nc.scalar.copy(spec[m][:, :, :, :].rearrange("p a b n -> p a (b n)"), fps[:, :, :]).then_inc(spec_sb, 1)

                def values(s, v):
                    wait(act, v_done, s, 4, v + 1)
                    if v == 0:
                        wait(act, out_done, s, 2, 0)
                    nc.scalar.copy(vsb[:, v % 2, HALF * (v // 2):HALF * (v // 2) + HALF], vps[:, 0:HALF]).then_inc(v_sb, 1)

                def body(s, i, n, first, last):
                    values(s, 0)
                    values(s, 1)
                    for j in range(NPP):
                        spectra(s, j)
                        if j == 4:
                            values(s, 2)
                            values(s, 3)
                strips(act, body)

            @block.vector
            def _(dve):
                def take(s, j):
                    m = j % 2
                    wait(dve, qk_done, s, NPP, j + 1)
                    wait(dve, spec_done, s, NPP, j - 1)
                    nc.vector.tensor_copy(qk[m][:, :, :].rearrange("p b n -> p (b n)"), qps[m][:, :]).then_inc(qk_sb, 1)

                def multiply(s, j):
                    m = j % 2
                    wait(dve, spec_sb, s, NPP, j + 1)
                    wait(dve, comb_done, s, 2 * NPP, 2 * j - 2)
                    for part in range(2):
                        nc.vector.tensor_tensor(prod[m][:, part, :, :, :], spec[m][:, :, :, 0:HID],
                                                spec[m][:, part, :, HID:2 * HID].unsqueeze(1).broadcast_to([P, 2, B, HID]), ALU.mult).then_inc(mul_done, 1)

                def weigh(s, j):
                    m = j % 2
                    wait(dve, back_done, s, NPP, j + 1)
                    wait(dve, v_sb, s, 4, 2 if j < 3 else 4)
                    if j == 0:
                        wait(dve, out_done, s, 2, 0)
                    nc.vector.tensor_tensor(vo[:, :, P * j:P * j + P], ips[m][:, 0:2 * P].rearrange("p (a n) -> p a n", a=2),
                                            vsb[:, :, P * j:P * j + P], ALU.mult).then_inc(vo_done, 1)

                def residual(s, h):
                    wait(dve, out_done, s, 2, h + 1)
                    xv = x_sb[:, ds(s * STRIP + HALF * h, HALF)]
                    nc.vector.tensor_tensor(xv, ops[:, 0:HALF], xv, ALU.add).then_inc(x_done, 1)

                def body(s, i, n, first, last):
                    take(s, 0)
                    take(s, 1)
                    for j in range(NPP):
                        multiply(s, j)
                        if j + 2 < NPP:
                            take(s, j + 2)
                        if j >= 1:
                            weigh(s, j - 1)
                    weigh(s, NPP - 1)
                    residual(s, 0)
                    residual(s, 1)
                strips(dve, body)

            @block.tensor
            def _(pe):
                def rows(i, b, at, n):
                    return xs[i][:, b, :, :].rearrange("p r c -> p (r c)")[:, at:at + n]

                def project(s, i, n, j):
                    m = j % 2
                    if j == 0:
                        wait(pe, strip_in[i], n, LOADS, LOADS)
                    wait(pe, qk_sb, s, NPP, j - 1)
                    for b in range(B):
                        for dy in range(3):
                            mm = nc.tensor.matmul(qps[m][:, P * b:P * b + P], rows(i, b, dy * W + P * j, P), wk[:, dy, 0:2 * HID],
                                                  start=(dy == 0), stop=(dy == 2))
                    mm.then_inc(qk_done, 1)

                def values(s, i, v):
                    h, a = v // 2, v % 2
                    wait(pe, v_sb, s, 4, v)
                    for b in range(2):
                        for dy in range(3):
                            mm = nc.tensor.matmul(vps[HID * b:HID * b + HID, 0:HALF], wk[:, dy, 2 * HID:3 * HID],
                                                  rows(i, 2 * a + b, dy * W + HALF * h, HALF),
                                                  start=(dy == 0), stop=(dy == 2))
                    mm.then_inc(v_done, 1)

                def forward(s, j):
                    m = j % 2
                    wait(pe, qk_sb, s, NPP, j + 1)
                    wait(pe, spec_sb, s, NPP, j)
                    for part in range(2):
                        mm = nc.tensor.matmul(fps[:, part, :], dft[:, part, :], qk[m][:, :, :].rearrange("p b n -> p (b n)"), start=True, stop=True)
                    mm.then_inc(spec_done, 1)

                def back(s, j):
                    m = j % 2
                    wait(pe, comb_done, s, 2 * NPP, 2 * j + 2)
                    wait(pe, vo_done, s, NPP, j - 1)
                    for a in range(2):
                        for part in range(2):
                            mm = nc.tensor.matmul(ips[m][:, P * a:P * a + P], spo[m][:, part, 2 * a:2 * a + 2, :].rearrange("p b n -> p (b n)"),
                                                  dft[:, 2 + part, :], start=(part == 0), stop=(part == 1))
                    mm.then_inc(back_done, 1)

                def merge(s, h):
                    wait(pe, vo_done, s, NPP, 3 * h + 3)
                    wait(pe, x_done, s, 2, h)
                    for a in range(2):
                        mm = nc.tensor.matmul(ops[:, 0:HALF], wo[:, a, :], vo[:, a, HALF * h:HALF * h + HALF], start=(a == 0), stop=(a == 1))
                    mm.then_inc(out_done, 1)

                def body(s, i, n, first, last):
                    project(s, i, n, 0)
                    project(s, i, n, 1)
                    values(s, i, 0)
                    forward(s, 0)
                    values(s, i, 1)
                    for j in range(2, NPP):
                        project(s, i, n, j)
                        forward(s, j - 1)
                        back(s, j - 2)
                    values(s, i, 2)
                    forward(s, NPP - 1)
                    values(s, i, 3)
                    back(s, NPP - 2)
                    merge(s, 0)
                    back(s, NPP - 1)
                    merge(s, 1)
                strips(pe, body)


def host_l3(wh, bh, wd, bdw, wo, bo):
    wh, wd = wh.reshape(192, C), wd.reshape(192, 3, 3)
    whid = np.concatenate([np.tile(wh.T, (3, 1)), np.tile(bh, (3, 1))], 0)
    t = wd.transpose(2, 1, 0)
    wdw = np.concatenate([np.repeat(t, C, 0), t], 0)
    bd = np.zeros((KS, 192), np.float32)
    bd[3 * C + 1] = bdw
    wout = wo.reshape(C, HID).T
    ones = np.zeros((3, B, H + 2, W), np.float32)
    ones[:, :, 1:H + 1] = 1
    ones[0, :, :, 0] = 0
    ones[2, :, :, W - 1] = 0
    r, c = np.arange(64) // 8, np.arange(64) % 8
    th = 2 * np.pi * (r[:, None] * r[None] + c[:, None] * c[None]) / 8
    z = np.zeros((4, P, P))
    for q in range(2):
        s = slice(64 * q, 64 * q + 64)
        z[0, s, s] = np.cos(th)
        z[1, s, s] = -np.sin(th)
        z[2, s, s] = np.cos(th) / 64
        z[3, s, s] = -np.sin(th) / 64
    return dict(whid=whid, wdw=wdw, bdw=bd, wout=wout, bout=np.tile(bo, 4)[:, None], ones=ones.reshape(3, B, -1),
                dft=np.ascontiguousarray(z.transpose(1, 0, 2)).astype(np.float32))




def stage_load(nc, x_sb, x):
    with ExitStack() as ctx:
        x_loaded = ctx.enter_context(nc.semaphore("x_loaded"))
        block = ctx.enter_context(nc.Block())

        @block.sync
        def _(sp):
            sp.dma_start(x_sb[:, :], x).then_inc(x_loaded, 16)
            sp.wait_ge(x_loaded, 16)


def program(nc, a, out):
    dram = lambda n, s: nc.dram_tensor(n, s, F, kind="Internal").ap()
    with ExitStack() as ctx:
        x_sb = ctx.enter_context(nc.sbuf_tensor("x_sb", [P, NPIX], F))
        stage_load(nc, x_sb, a["x"])
        stage_attention(nc, x_sb, a["wqkvT"], a["rel"], a["halves"], a["headmask"], a["unitmask"], a["ident"],
                        dram("attention_queries", [P, NROW, NROW, Q64]))
        with ExitStack() as deform:
            x_save = dram("deform_save", [P, NPIX])
            far = deform.enter_context(nc.sbuf_tensor("far", [1, 1], I32))[:, :]
            stage_deform_near(nc, x_sb, a["near_convw"], a["near_convb"], a["near_rep"], a["near_sel"], a["near_dcnbd"],
                              a["near_shifts"], a["ident"], x_save, far)
            stage_deform_far(nc, x_sb, a["convw"], a["bias"], a["coord"], a["ixb"], a["dcn"], a["ident"],
                             dram("deform_image", [P, TY, TY]), dram("deform_table", [1 + B * TROWS * TX, ENTRY]), x_save, far)
        stage_fourier(nc, x_sb, a["fw"], a["fh"], a["ch"], a["ih"], a["iw"], a["w1"], a["w2"],
                      a["lin1"], a["b1"], a["lin2"], a["b2"], a["ident"])
        stage_fftconv(nc, x_sb, a["whid"], a["wdw"], a["bdw"], a["wout"], a["bout"], a["ones"], a["dft"],
                      dram("gate_image", [P, H + 2, W + 2]), out)


def kernel(**inputs):
    import concourse.bacc as bacc
    from concourse.bass_utils import run_bass_kernel_spmd

    i = {k: np.asarray(v) for k, v in inputs.items()}
    qkv = i["L0_conv_w_qkv"].reshape(3, C, C).transpose(2, 0, 1)
    rel = np.concatenate([i["L0_conv_rel_h"].reshape(WIN, D // 2), i["L0_conv_rel_w"].reshape(WIN, D // 2)], 1).T
    deform = [i["L1_conv_" + n] for n in ("offset_w", "offset_b", "mask_w", "mask_b", "dcn_w")]
    arrays = dict(
        x=i["x"].reshape(P, NPIX), wqkvT=qkv, rel=np.tile(rel, (P // D, 1)), **host_consts(),
        **host_l1(*deform), **{"near_" + k: v for k, v in host_l1d(*deform).items()},
        **host_l2(), w1=i["L2_conv_w1"], w2=i["L2_conv_w2"], lin1=i["L2_conv_lin1_w"], b1=i["L2_conv_lin1_b"][:, None],
        lin2=i["L2_conv_lin2_w"], b2=np.tile(i["L2_conv_lin2_b"], B)[:, None],
        **host_l3(*(i["L3_conv_" + n] for n in ("w_hidden", "b_hidden", "w_dw", "b_dw", "w_out", "b_out"))))
    arrays = {k: np.ascontiguousarray(v) for k, v in arrays.items()}
    nc = bacc.Bacc("TRN2", target_bir_lowering=False, num_devices=1)
    handles = {k: nc.dram_tensor("in_" + k, v.shape, mybir.dt.from_np(v.dtype), kind="ExternalInput").ap()
               for k, v in arrays.items()}
    out = nc.dram_tensor("out", [P, NPIX], F, kind="ExternalOutput").ap()
    program(nc, handles, out)
    r = run_bass_kernel_spmd(nc, [{"in_" + k: v for k, v in arrays.items()}], core_ids=[0])
    return r.results[0]["out"].reshape(B, C, H, W)
```

```python
from contextlib import ExitStack, contextmanager

import numpy as np

import concourse.bass as bass
from concourse import mybir

F=mybir.dt.float32; ALU=mybir.AluOpType; ACT=mybir.ActivationFunctionType; AX=mybir.AxisListType
B, C, H, W = 4, 32, 96, 96
P = B * C
NPIX = H * W
ds = bass.ds
XPARTS = 6


@contextmanager
def when(eng, flag):
    if flag is None:
        yield
    else:
        with eng.If(eng.value_load(flag, min_val=0, max_val=1) > 0):
            yield


def stage_norm(nc, name, x_sb, xpad, pad, far=None, x_dram=None, loads=(), zeroed=None, blocks=()):
    wide = xpad.shape[2]
    with ExitStack() as ctx:
        stats = ctx.enter_context(nc.sbuf_tensor(name + "_stats", [P, 18, 6], F))
        agg = ctx.enter_context(nc.sbuf_tensor(name + "_agg", [P, 8], F))
        stats_done = ctx.enter_context(nc.semaphore(name + "_stats_done"))
        var_ready = ctx.enter_context(nc.semaphore(name + "_var_ready"))
        root_ready = ctx.enter_context(nc.semaphore(name + "_root_ready"))
        step_done = ctx.enter_context(nc.semaphore(name + "_step_done"))
        x_in = [ctx.enter_context(nc.semaphore(name + f"_x_in{k}")) for k in range(XPARTS if x_dram is not None else 0)]
        if loads:
            const_in = ctx.enter_context(nc.semaphore(name + "_const_in"))
        if blocks:
            zeros_done = ctx.enter_context(nc.semaphore(name + "_zeros_done"))
        block = ctx.enter_context(nc.Block())
        mean, var, std, rstd, t = (agg[:, k:k + 1] for k in range(5))

        @block.gpsimd
        def _(pool):
            with when(pool, far):
                if zeroed is not None:
                    nc.gpsimd.memset(zeroed, 0.0).then_inc(zeros_done, 1)
                nc.gpsimd.memset(xpad[:, 0:pad, :], 0.0)
                nc.gpsimd.memset(xpad[:, H + pad:H + 2 * pad, :], 0.0)
                nc.gpsimd.memset(xpad[:, pad:H + pad, 0:pad], 0.0)
                nc.gpsimd.memset(xpad[:, pad:H + pad, W + pad:wide], 0.0)

        @block.sync
        def _(sp):
            with when(sp, far):
                if x_dram is not None:
                    for k in range(XPARTS):
                        part = slice(k * NPIX // XPARTS, (k + 1) * NPIX // XPARTS)
                        sp.dma_start(x_sb[:, part], x_dram[:, part]).then_inc(x_in[k], 16)
                for to, source in loads:
                    sp.dma_start(to, source).then_inc(const_in, 16)
                if blocks:
                    sp.wait_ge(zeros_done, 1)
                for to, source in blocks:
                    sp.dma_start(to, source).then_inc(const_in, 16)
                if len(loads) + len(blocks) > 0:
                    sp.wait_ge(const_in, 16 * (len(loads) + len(blocks)))

        @block.vector
        def _(dve):
            with when(dve, far):
                for k in range(18):
                    if x_dram is not None and k % (18 // XPARTS) == 0:
                        dve.wait_ge(x_in[k // (18 // XPARTS)], 16)
                    nc.vector.bn_stats(stats[:, k, :], x_sb[:, k * 512:(k + 1) * 512]).then_inc(stats_done, 1)
                dve.wait_ge(stats_done, 18)
                nc.vector.bn_aggr(agg[:, 0:2], stats[:, :, :]).then_inc(step_done, 1)
                dve.wait_ge(step_done, 1)
                nc.vector.tensor_scalar(var, var, 1e-5, None, ALU.add).then_inc(var_ready, 1)
                dve.wait_ge(root_ready, 1)
                nc.vector.reciprocal(rstd, std).then_inc(step_done, 1)
                dve.wait_ge(step_done, 2)
                nc.vector.tensor_tensor(t, rstd, rstd, ALU.mult).then_inc(step_done, 1)
                dve.wait_ge(step_done, 3)
                nc.vector.tensor_tensor(t, t, var, ALU.mult).then_inc(step_done, 1)
                dve.wait_ge(step_done, 4)
                nc.vector.tensor_scalar(t, t, -0.5, 1.5, ALU.mult, ALU.add).then_inc(step_done, 1)
                dve.wait_ge(step_done, 5)
                nc.vector.tensor_tensor(rstd, rstd, t, ALU.mult).then_inc(step_done, 1)
                dve.wait_ge(step_done, 6)
                nc.vector.tensor_scalar(xpad[:, pad:H + pad, pad:W + pad],
                                        x_sb[:, :].rearrange("p (h w) -> p h w", h=H),
                                        mean, rstd, ALU.subtract, ALU.mult)

        @block.scalar
        def _(act):
            with when(act, far):
                act.wait_ge(var_ready, 1)
                nc.scalar.activation(std, var, ACT.Sqrt).then_inc(root_ready, 1)


BLK, HALO, HEADS = 8, 3, 4
D = C // HEADS
WIN = BLK + 2 * HALO
NK = WIN * WIN
HK = NK // 2
NWIN = (H // BLK) * (W // BLK)
Q64 = BLK * BLK


def wait(eng, s, w, k, c):
    if isinstance(w, int):
        if k * w + c > 0:
            eng.wait_ge(s, k * w + c)
    else:
        eng.wait_ge(s, w * k + c)


NROW = W // BLK
HALFROW = NROW // 2


def stage_attention(nc, x_dram, x_sb, wqkvT, rel, halves, headmask, unitmask, ident_d, q_dram):
    PADDED = H + 2 * HALO
    with ExitStack() as outer:
        sb = lambda n, s, dt=F: outer.enter_context(nc.sbuf_tensor("at_" + n, s, dt))
        xp = sb("xp", [P, PADDED, PADDED])
        kp = sb("kp", [P, PADDED, PADDED])
        wbd = sb("wbd", [P, 3, P])
        relc = sb("relc", [P, WIN])
        relhw = sb("relhw", [P, WIN, WIN])
        half = sb("half", [P, 2])
        hm = sb("hm", [P, HEADS])
        um = sb("um", [P, B * HEADS])
        ident = sb("ident", [P, P])
        stage_norm(nc, "gn0", x_sb, xp, HALO, x_dram=x_dram,
                   loads=((relc[:, :], rel), (half[:, :], halves), (hm[:, :], headmask), (um[:, :], unitmask), (ident[:, :], ident_d)),
                   zeroed=wbd[:, :, :], blocks=[(wbd[C * b:C * b + C, :, C * b:C * b + C], wqkvT) for b in range(B)])
        with ExitStack() as ctx:
            sem = lambda n: ctx.enter_context(nc.semaphore("ap_" + n))
            ps = [ctx.enter_context(nc.psum_tensor(f"ap_ps{i}", [P, 512], F)) for i in range(4)]
            qrow = [ctx.enter_context(nc.sbuf_tensor(f"ap_qrow{i}", [P, NROW, Q64], F)) for i in range(2)]
            rel_step = sem("rel_step")
            keys_done, keys_out, queries_done, queries_out = sem("keys_done"), sem("keys_out"), sem("queries_done"), sem("queries_out")
            stored = [sem("stored0"), sem("stored1")]
            block = ctx.enter_context(nc.Block())
            KROWS = PADDED // 3

            @block.sync
            def _(sp):
                with sp.Fori(0, NROW // 2) as i:
                    for s in range(2):
                        sp.wait_ge(queries_out, i * 4 + (2 * s + 2))
                        sp.dma_start(q_dram[:, ds(i * 2 + s, 1), :, :].rearrange("p y x q -> p (y x) q"), qrow[s][:, :, :]).then_inc(stored[s], 16)
                for s in range(2):
                    sp.wait_ge(stored[s], 16 * NROW // 2)

            @block.vector
            def _(dve):
                nc.vector.tensor_scalar(relhw[:, :, :], relc[:, :].unsqueeze(2).broadcast_to([P, WIN, WIN]),
                                        half[:, 0:1], None, ALU.mult).then_inc(rel_step, 1)
                dve.wait_ge(rel_step, 1)
                nc.vector.scalar_tensor_tensor(relhw[:, :, :], relc[:, :].unsqueeze(1).broadcast_to([P, WIN, WIN]),
                                               half[:, 1:2], relhw[:, :, :], ALU.mult, ALU.add)
                with dve.Fori(0, KROWS // 2) as i:
                    for s in range(2):
                        dve.wait_ge(keys_done, i * 2 + s + 1)
                        nc.vector.tensor_copy(kp[:, ds(i * 6 + 3 * s, 3), :],
                                              ps[s][:, 0:3 * PADDED].rearrange("p (r c) -> p r c", r=3)).then_inc(keys_out, 1)

            @block.scalar
            def _(act):
                def half_row(i, r, h, j):
                    act.wait_ge(queries_done, i * 4 + (2 * r + h + 1))
                    if h == 0 and j is not None:
                        wait(act, stored[r], j, 16, 0)
                    nc.scalar.activation(qrow[r][:, :, 32 * h:32 * h + 32].rearrange("p x (r c) -> p x r c", r=4),
                                         ps[2 + h][:, 0:4 * W].rearrange("p (r x c) -> p x r c", r=4, x=NROW),
                                         ACT.Copy, scale=D ** -0.5).then_inc(queries_out, 1)
                for r in range(2):
                    for h in range(2):
                        half_row(0, r, h, None)
                with act.Fori(1, NROW // 2) as i:
                    for r in range(2):
                        for h in range(2):
                            half_row(i, r, h, i)

            @block.tensor
            def _(pe):
                def key_rows(i, s):
                    wait(pe, keys_out, i, 2, s - 1)
                    nc.tensor.matmul(ps[s][:, 0:3 * PADDED], wbd[:, 1, :], xp[:, ds(i * 6 + 3 * s, 3), :],
                                     start=True, stop=True).then_inc(keys_done, 1)

                def query_rows(i, s):
                    wait(pe, queries_out, i, 2, s - 1)
                    nc.tensor.matmul(ps[2 + s][:, 0:4 * W], wbd[:, 0, :],
                                     xp[:, ds(i * 8 + (HALO + 4 * s), 4), HALO:HALO + W],
                                     start=True, stop=True).then_inc(queries_done, 1)

                def both(i):
                    for s in range(2):
                        key_rows(i, s)
                        query_rows(i, s)
                both(0)
                with pe.Fori(1, NROW) as i:
                    both(i)
                with pe.Fori(NROW, KROWS // 2) as i:
                    for s in range(2):
                        key_rows(i, s)

        with ExitStack() as ctx:
            sem = lambda n: ctx.enter_context(nc.semaphore("at_" + n))
            sbc = lambda n, s, dt=F: ctx.enter_context(nc.sbuf_tensor("at_" + n, s, dt))
            qhalf = [sbc(f"qhalf{i}", [P, HALFROW, Q64]) for i in range(2)]
            kw = [sbc(f"kw{i}", [P, NK]) for i in range(2)]
            qw = [sbc(f"qw{i}", [P, B * HEADS, Q64]) for i in range(2)]
            xw = [sbc(f"xw{i}", [P, NK]) for i in range(2)]
            vs = [sbc(f"vs{i}", [HK, 2, P]) for i in range(2)]
            nmx = sbc("nmx", [P, B, 2])
            sums = sbc("sums", [P, B, 2])
            rs = sbc("rs", [P, B, 2])
            probs = [sbc(f"probs{b}", [P, 2, NK]) for b in range(B)]
            pts = [[sbc(f"pts{i}_{b}", [HK, 2, 2, P]) for b in range(B)] for i in range(2)]
            sc = [ctx.enter_context(nc.psum_tensor(f"at_sc{b}", [P, 512], F)) for b in range(B)]
            pt = [ctx.enter_context(nc.psum_tensor(f"at_pt{i}", [P, 512], F)) for i in range(2)]
            ov = [ctx.enter_context(nc.psum_tensor(f"at_ov{i}", [P, 512], F)) for i in range(2)]
            scores_ready, max_ready, exp_done, inv_ready = sem("scores_ready"), sem("max_ready"), sem("exp_done"), sem("inv_ready")
            normed, pt_ready, pts_ready, last_pts_ready = sem("normed"), sem("pt_ready"), sem("pts_ready"), sem("last_pts_ready")
            pv_done, v_ready, vs_ready = sem("pv_done"), sem("v_ready"), sem("vs_ready")
            keys_ready, q_ready, xw_ready, res_step = sem("keys_ready"), sem("q_ready"), sem("xw_ready"), sem("res_step")
            q_loaded = [sem("q_loaded0"), sem("q_loaded1")]
            block = ctx.enter_context(nc.Block())

            def there(w):
                return not isinstance(w, int) or 0 <= w < NWIN

            def rows(eng, step):
                for w in (-2, -1):
                    step(w, 0, w)
                for x in range(NROW):
                    step(x, 0, x)
                with eng.Fori(1, NROW - 1) as gy:
                    for x in range(NROW):
                        step(gy * NROW + x, gy, x)
                for x in range(NROW):
                    step((NROW - 1) * NROW + x, NROW - 1, x)
                step(NWIN, NROW - 1, NROW)

            def corner(gy, x):
                over = x // NROW
                return gy * BLK + over * BLK, (x - over * NROW) * BLK

            @block.sync
            def _(sp):
                def load(gy, h):
                    wait(sp, q_ready, gy, NROW, HALFROW * (h + 1) - NROW)
                    sp.dma_start(qhalf[h][:, :, :], q_dram[:, ds(gy, 1), HALFROW * h:HALFROW * h + HALFROW, :].rearrange("p y x q -> p (y x) q")
                                 ).then_inc(q_loaded[h], 16)
                for h in range(2):
                    load(0, h)
                with sp.Fori(1, NROW) as gy:
                    for h in range(2):
                        load(gy, h)

            @block.gpsimd
            def _(pool):
                def spread(w, gy, x):
                    over = x // NROW
                    x -= over * NROW
                    wait(pool, q_loaded[x // HALFROW], gy, 16, 16 + 16 * over)
                    wait(pool, scores_ready, w, B, -B)
                    nc.gpsimd.tensor_tensor(qw[x % 2][:, :, :], qhalf[x // HALFROW][:, x % HALFROW:x % HALFROW + 1, :].broadcast_to([P, B * HEADS, Q64]),
                                            um[:, :].unsqueeze(2).broadcast_to([P, B * HEADS, Q64]), ALU.mult).then_inc(q_ready, 1)

                def norm(w, b):
                    wait(pool, inv_ready, w, B, b + 1)
                    nc.gpsimd.tensor_tensor(probs[b][:, :, :], probs[b][:, :, :],
                                            rs[:, b, :].unsqueeze(2).broadcast_to([P, 2, NK]), ALU.mult).then_inc(normed, 1)

                def step(w, gy, x):
                    if there(w):
                        norm(w, 3)
                    if there(w + 2):
                        spread(w + 2, gy, x + 2)
                    if there(w + 1):
                        for b in range(3):
                            norm(w + 1, b)
                rows(pool, step)

            @block.vector
            def _(dve):
                def keys(w, gy, x):
                    y0, x0 = corner(gy, x)
                    wait(dve, scores_ready, w, B, -B)
                    nc.vector.tensor_tensor(kw[x % 2][:, :].rearrange("p (r c) -> p r c", r=WIN),
                                            kp[:, ds(y0, WIN), ds(x0, WIN)], relhw[:, :, :], ALU.add).then_inc(keys_ready, 1)

                def maxes(w, b):
                    wait(dve, scores_ready, w, B, b + 1)
                    wait(dve, exp_done, w, 2 * B, 2 * b + 2 - 2 * B)
                    nc.vector.tensor_reduce(nmx[:, b, :], sc[b][:, 0:2 * NK].rearrange("p (j k) -> p j k", j=2),
                                            AX.X, ALU.max, negate=True).then_inc(max_ready, 1)

                def inverse(w, b):
                    wait(dve, exp_done, w, 2 * B, 2 * b + 2)
                    wait(dve, normed, w, B, b + 1 - B)
                    nc.vector.reciprocal(rs[:, b, :], sums[:, b, :]).then_inc(inv_ready, 1)

                def evac(w, b, s):
                    wait(dve, pt_ready, w, B, b + 1)
                    wait(dve, pv_done, w, 1, -1)
                    nc.vector.tensor_copy(pts[s][b][:, :, :, :],
                                          pt[b % 2][0:HK, :].rearrange("p (c j q) -> p c j q", c=2, j=2)).then_inc(pts_ready, 1)

                def residual(w, gy, x, heads):
                    if not there(w):
                        return
                    y0, x0 = corner(gy, x)
                    xv = x_sb[:, :].rearrange("p (h w) -> p h w", h=H)[:, ds(y0, BLK), ds(x0, BLK)]
                    for h in heads:
                        if h:
                            wait(dve, res_step, w, HEADS, h)
                        else:
                            wait(dve, pv_done, w, 1, 1)
                        nc.vector.scalar_tensor_tensor(
                            xv, ov[x % 2][:, Q64 * h:Q64 * h + Q64].rearrange("p (r c) -> p r c", r=BLK),
                            hm[:, h:h + 1], xv, ALU.mult, ALU.add).then_inc(res_step, 1)

                def step(w, gy, x):
                    for b in range(B):
                        if there(w) and b < B - 1:
                            evac(w, b, x % 2)
                        if b == 3:
                            residual(w + (-1), gy, x - 1, [2])
                        if there(w + 1):
                            maxes(w + 1, b)
                        if b == 2:
                            residual(w + (-1), gy, x - 1, [0])
                        if b == 0:
                            if there(w):
                                inverse(w, 3)
                            if there(w + 2):
                                keys(w + 2, gy, x + 2)
                        elif there(w + 1):
                            inverse(w + 1, b - 1)
                        if b == 2:
                            residual(w + (-1), gy, x - 1, [1])
                        if b == 3:
                            residual(w + (-1), gy, x - 1, [3])
                rows(dve, step)

            @block.scalar
            def _(act):
                def crop(w, gy, x):
                    y0, x0 = corner(gy, x)
                    wait(act, v_ready, w, 1, -1)
                    nc.scalar.copy(xw[x % 2][:, :].rearrange("p (r c) -> p r c", r=WIN),
                                   xp[:, ds(y0, WIN), ds(x0, WIN)]).then_inc(xw_ready, 1)

                def values(w, s):
                    wait(act, v_ready, w, 1, 1)
                    wait(act, pv_done, w, 1, -1)
                    nc.scalar.copy(vs[s][:, :, :], ov[1 - s][0:HK, 256:512].rearrange("p (c o) -> p c o", c=2)).then_inc(vs_ready, 1)

                def evac(w, s):
                    wait(act, pt_ready, w, B, B)
                    wait(act, pv_done, w, 1, -1)
                    nc.scalar.copy(pts[s][B - 1][:, :, :, :],
                                   pt[(B - 1) % 2][0:HK, :].rearrange("p (c j q) -> p c j q", c=2, j=2)).then_inc(last_pts_ready, 1)

                def exps(w, b):
                    wait(act, max_ready, w, B, b + 1)
                    wait(act, pt_ready, w, B, b + 1 - B)
                    wait(act, inv_ready, w, B, b + 1 - B)
                    for j in range(2):
                        nc.scalar.activation(probs[b][:, j, :], sc[b][:, NK * j:NK * j + NK], ACT.Exp,
                                             bias=nmx[:, b, j:j + 1], accum_out=sums[:, b, j:j + 1]).then_inc(exp_done, 1)

                def step(w, gy, x):
                    if there(w + 1):
                        exps(w + 1, 0)
                        exps(w + 1, 1)
                    if there(w + 2):
                        crop(w + 2, gy, x + 2)
                    if there(w + 1):
                        exps(w + 1, 2)
                        values(w + 1, (x + 1) % 2)
                    if there(w):
                        evac(w, x % 2)
                    if there(w + 1):
                        exps(w + 1, 3)
                rows(act, step)

            @block.tensor
            def _(pe):
                def score(w, b, s):
                    if b == 0:
                        wait(pe, keys_ready, w, 1, 1)
                        wait(pe, q_ready, w, 1, 1)
                    wait(pe, exp_done, w, 2 * B, 2 * b + 2 - 2 * B)
                    for j in range(2):
                        mm = nc.tensor.matmul(sc[b][:, NK * j:NK * j + NK], qw[s][:, HEADS * b + 2 * j:HEADS * b + 2 * j + 2, :],
                                              kw[s][:, :], start=True, stop=True)
                    mm.then_inc(scores_ready, 1)

                def value(w, s):
                    wait(pe, xw_ready, w, 1, 1)
                    wait(pe, res_step, w, HEADS, -2 * HEADS)
                    for c in range(2):
                        mm = nc.tensor.matmul(ov[1 - s][0:HK, 256 + P * c:256 + P * c + P], xw[s][:, HK * c:HK * c + HK],
                                              wbd[:, 2, :], start=True, stop=True)
                    mm.then_inc(v_ready, 1)

                def transposed(w, b):
                    wait(pe, normed, w, B, b + 1)
                    if b == 1:
                        wait(pe, last_pts_ready, w, 1, 0)
                    else:
                        wait(pe, pts_ready, w, B - 1, max(b - 1, 0))
                    for c in range(2):
                        for j in range(2):
                            o = (2 * c + j) * P
                            mm = nc.tensor.transpose(pt[b % 2][0:HK, o:o + P], probs[b][:, j, HK * c:HK * c + HK], ident[:, :])
                    mm.then_inc(pt_ready, 1)

                def weigh(w, s):
                    wait(pe, pts_ready, w, B - 1, B - 1)
                    wait(pe, last_pts_ready, w, 1, 1)
                    if not isinstance(w, int) or w < NWIN - 1:
                        wait(pe, vs_ready, w, 1, 2)
                    else:
                        wait(pe, vs_ready, w, 1, 1)
                    for c in range(2):
                        for b in range(B):
                            mm = nc.tensor.matmul(ov[s][C * b:C * b + C, 0:256], vs[s][:, c, C * b:C * b + C],
                                                  pts[s][b][:, c, :, :], start=(c == 0), stop=(c == 1))
                    mm.then_inc(pv_done, 1)

                def step(w, s):
                    for b in range(B):
                        if there(w):
                            transposed(w, b)
                        if there(w + 1):
                            score(w + 1, b, 1 - s)
                        if b == 1 and there(w + (-1)):
                            weigh(w + (-1), 1 - s)
                        if b == 2 and there(w + 1):
                            value(w + 1, 1 - s)
                for w in range(-1, 2):
                    step(w, w % 2)
                with pe.Fori(1, NWIN // 2 - 1) as g:
                    step(g * 2, 0)
                    step(g * 2 + 1, 1)
                for w in range(NWIN - 2, NWIN + 1):
                    step(w, w % 2)


def host_consts():
    p = np.arange(P)
    return dict(
        halves=np.stack([(p % D < D // 2), (p % D >= D // 2)], 1).astype(np.float32),
        headmask=((p % C)[:, None] // D == np.arange(HEADS)[None]).astype(np.float32),
        unitmask=(p[:, None] // D == np.arange(B * HEADS)[None]).astype(np.float32),
        ident=np.eye(P, dtype=np.float32))



I32 = mybir.dt.int32
U32 = mybir.dt.uint32
TAPS = 9
TR = 8
NSTRIP, TPS = H // TR, TR * W // P
UNITS = TPS * B
EDGE = 2
TY, TX = H + 2 * EDGE, 112
TROWS = TY - 1
ENTRY = 4 * C
GROWS = 9
RING = 4


def stage_deform_far(nc, x_sb, convw, biasr, coord, base_ix, dcn, ident_d, xn_d, table, x_save, far):
    with ExitStack() as ctx:
        restored = ctx.enter_context(nc.semaphore("df_restored"))
        block = ctx.enter_context(nc.Block())

        @block.sync
        def _(sp):
            with when(sp, far):
                sp.dma_start(x_sb[:, :], x_save).then_inc(restored, 16)
                sp.wait_ge(restored, 16)

    LOADS = 16 * 3 * B
    with ExitStack() as outer:
        sb = lambda n, s, dt=F: outer.enter_context(nc.sbuf_tensor("df_" + n, s, dt))
        ident = sb("ident", [P, P])
        wc = sb("wc", [3 * C, 3, 27])
        wd = sb("wd", [P, TAPS, C])
        base = sb("base", [P, UNITS, 2, TAPS])
        bias = sb("bias", [P, 27])
        ixb = sb("ixb", [P, UNITS, TAPS])
        with ExitStack() as ctx:
            xp = ctx.enter_context(nc.sbuf_tensor("df_xp", [P, TY, TX], F))
            stage_norm(nc, "gnf", x_sb, xp, EDGE, far)
            sem = lambda n: ctx.enter_context(nc.semaphore("dt_" + n))
            rows = [ctx.enter_context(nc.sbuf_tensor(f"dt_rows{i}", [P, GROWS + 1, TX], F)) for i in range(2)]
            stage = [ctx.enter_context(nc.sbuf_tensor(f"dt_stage{i}", [TX, GROWS, B, 2, C], F)) for i in range(2)]
            zeros = ctx.enter_context(nc.sbuf_tensor("dt_zeros", [1, 64], F))
            ps = [ctx.enter_context(nc.psum_tensor(f"dt_ps{i}", [P, 4, 512], F)) for i in range(2)]
            zeros_ready, lower, loaded, written = sem("zeros_ready"), sem("lower"), sem("loaded"), sem("written")
            rows_ready, turned, staged, stored = sem("rows_ready"), sem("turned"), sem("staged"), [sem("stored0"), sem("stored1")]
            block = ctx.enter_context(nc.Block())
            NG = (TY - 1) // GROWS
            assert NG * GROWS == TY - 1 and NG % 2 == 1

            @block.sync
            def _(sp):
                with when(sp, far):
                    for dst, src in ((ident[:, :], ident_d), (wc[:, :, :], convw), (wd[:, :, :], dcn),
                                     (base[:, :, :, :], coord), (bias[:, :], biasr), (ixb[:, :, :], base_ix)):
                        sp.dma_start(dst, src).then_inc(loaded, 16)
                    sp.dma_start(xn_d, xp[:, :, 0:TY]).then_inc(written, 16)

                    sp.wait_ge(zeros_ready, 1)
                    sp.dma_start(table[0:1, 0:64], zeros[0:1, :]).then_inc(written, 16)
                    sp.dma_start(table[B * TROWS * TX:B * TROWS * TX + 1, 64:128], zeros[0:1, :]).then_inc(written, 16)

                    def store(g, s):
                        wait(sp, lower, g, 1, 1)
                        wait(sp, staged, g, 1, 1)
                        for b in range(B):
                            for half in range(2):
                                dst = table[ds(g * (GROWS * TX) + (1 - half + b * TROWS * TX), GROWS * TX), 64 * half:64 * half + 64]
                                sp.dma_start(dst.rearrange("(y x) c -> x y c", x=TX),
                                             stage[s][:, :, b, :, :].rearrange("x y r c -> x y (r c)")).then_inc(stored[s], 16)
                    store(0, 0)
                    with sp.Fori(0, NG // 2) as h:
                        store(h * 2 + 1, 1)
                        store(h * 2 + 2, 0)
                    sp.wait_ge(written, 48)
                    sp.wait_ge(loaded, 16 * 6)
                    sp.wait_ge(stored[0], 128 * (NG // 2 + 1))
                    sp.wait_ge(stored[1], 128 * (NG // 2))

            @block.gpsimd
            def _(pool):
                with when(pool, far):
                    nc.gpsimd.memset(zeros[:, :], 0.0).then_inc(zeros_ready, 1)
                    pool.wait_ge(loaded, 16 * 6)
                    nc.gpsimd.tensor_tensor(base[:, :, :, :].rearrange("p u a k -> p u (a k)"), base[:, :, :, :].rearrange("p u a k -> p u (a k)"),
                                            bias[:, 0:18].unsqueeze(1).broadcast_to([P, UNITS, 18]), ALU.add)

            @block.scalar
            def _(act):
                with when(act, far):
                    def take(g, s):
                        wait(act, turned, g, 1, -1)
                        nc.scalar.copy(rows[s][:, :, :], xp[:, ds(g * GROWS, GROWS + 1), :]).then_inc(rows_ready, 1)

                    def put(g, s, j):
                        wait(act, lower, g, 1, 1)
                        if j is not None:
                            wait(act, stored[s], j, 128, 0)
                        nc.scalar.copy(stage[s][:, :, :, 0, :],
                                       ps[s][0:TX, :, :].rearrange("p k n -> p (k n)")[:, 0:GROWS * P].rearrange("p (y b c) -> p y b c", y=GROWS, b=B)).then_inc(staged, 1)
                    take(0, 0)
                    take(1, 1)
                    put(0, 0, None)
                    take(2, 0)
                    put(1, 1, None)
                    with act.Fori(1, NG // 2) as h:
                        take(h * 2 + 1, 1)
                        put(h * 2, 0, h)
                        take(h * 2 + 2, 0)
                        put(h * 2 + 1, 1, h)
                    put(NG - 1, 0, NG // 2)

            @block.vector
            def _(dve):
                with when(dve, far):
                    def put(g, s, j):
                        wait(dve, turned, g, 1, 1)
                        if j is not None:
                            wait(dve, stored[s], j, 128, 0)
                        nc.vector.tensor_copy(stage[s][:, :, :, 1, :],
                                              ps[s][0:TX, :, :].rearrange("p k n -> p (k n)")[:, P:(GROWS + 1) * P].rearrange("p (y b c) -> p y b c", y=GROWS, b=B)).then_inc(lower, 1)
                    put(0, 0, None)
                    put(1, 1, None)
                    with dve.Fori(1, NG // 2) as h:
                        put(h * 2, 0, h)
                        put(h * 2 + 1, 1, h)
                    put(NG - 1, 0, NG // 2)

            @block.tensor
            def _(pe):
                with when(pe, far):
                    pe.wait_ge(loaded, 16 * 6)
                    def turn(g, s):
                        wait(pe, rows_ready, g, 1, 1)
                        wait(pe, staged, g, 1, -1)
                        for y in range(GROWS + 1):
                            o = y * P
                            mm = nc.tensor.transpose(ps[s][0:TX, o // 512, o % 512:o % 512 + P], rows[s][:, y, :], ident[:, :])
                        mm.then_inc(turned, 1)
                    turn(0, 0)
                    turn(1, 1)
                    with pe.Fori(1, NG // 2) as h:
                        turn(h * 2, 0)
                        turn(h * 2 + 1, 1)
                    turn(NG - 1, 0)

        with ExitStack() as ctx:
            sem = lambda n: ctx.enter_context(nc.semaphore("df_" + n))
            sbc = lambda n, s, dt=F: ctx.enter_context(nc.sbuf_tensor("df_" + n, s, dt))
            psum = lambda n, s: ctx.enter_context(nc.psum_tensor("df_" + n, s, F))
            xs = [sbc(f"xs{i}", [3 * C, B, TR + 2, W]) for i in range(2)]
            pos = sbc("pos", [P, UNITS, 2, TAPS])
            logit = sbc("logit", [P, UNITS, TAPS])
            msk = sbc("msk", [P, UNITS, TAPS])
            ii = sbc("ii", [P, UNITS, 2, TAPS], I32)
            fl = sbc("fl", [P, UNITS, 2, TAPS])
            lt = sbc("lt", [P, UNITS, 2, TAPS])
            ixf = sbc("ixf", [P, UNITS, TAPS])
            gy = sbc("gy", [P, 2, UNITS, TAPS])
            ixu = [sbc(f"ixu{i}", [P, UNITS, TAPS], U32) for i in range(2)]
            wt = [sbc(f"wt{i}", [P, UNITS, TAPS, 4]) for i in range(2)]
            gat = [sbc(f"gat{i}", [P, TAPS, 4, C]) for i in range(RING)]
            gts = [sbc(f"gts{i}", [P, TAPS, P]) for i in range(2)]
            cps = [psum(f"cps{i}", [P, 512]) for i in range(2)]
            tps = psum("tps", [P, 3, 512])
            ops = [psum(f"ops{i}", [P, 512]) for i in range(2)]
            strip_in = [sem("strip_in0"), sem("strip_in1")]
            conv_done, conv_read, logit_ready, mask_ready, chain = sem("conv_done"), sem("conv_read"), sem("logit_ready"), sem("mask_ready"), sem("chain")
            coords_ready, slot_free = sem("coords_ready"), sem("slot_free")
            gathered = [sem(f"gathered{i}") for i in range(RING)]
            weighted, turned, turned_sb, mixed, added = sem("weighted"), sem("turned"), sem("turned_sb"), sem("mixed"), sem("added")
            block = ctx.enter_context(nc.Block())

            def strips(eng, body):
                body(0, 0, True, False)
                with eng.Fori(0, NSTRIP // 2 - 1) as h:
                    body(h * 2 + 1, 1, False, False)
                    body(h * 2 + 2, 0, False, False)
                body(NSTRIP - 1, 1, False, True)

            @block.sync
            def _(sp):
                with when(sp, far):
                    def load(s, i, first, last):
                        wait(sp, conv_done, s, 1, -1)
                        for dx in range(3):
                            for b in range(B):
                                sp.dma_start(xs[i][C * dx:C * dx + C, b, :, :],
                                             xn_d[C * b:C * b + C, ds(s * TR + EDGE - 1, TR + 2), EDGE - 1 + dx:EDGE - 1 + dx + W]
                                             ).then_inc(strip_in[i], 16)
                    load(0, 0, True, False)
                    load(1, 1, False, False)
                    load(2, 0, False, False)
                    with sp.Fori(1, NSTRIP // 2 - 1) as h:
                        load(h * 2 + 1, 1, False, False)
                        load(h * 2 + 2, 0, False, False)
                    load(NSTRIP - 1, 1, False, True)

            @block.tensor
            def _(pe):
                with when(pe, far):
                    def conv_strip(s, i, half):
                        wait(pe, strip_in[i], half, LOADS, LOADS)
                        wait(pe, conv_read, s, 4, 0)
                        for t in range(TPS):
                            for b in range(B):
                                u = t * B + b
                                for dy in range(3):
                                    mm = nc.tensor.matmul(cps[u // 12][:, 27 * (u % 12):27 * (u % 12) + 27],
                                                          xs[i][:, b, :, :].rearrange("p r c -> p (r c)")[:, dy * W + P * t:dy * W + P * t + P], wc[:, dy, :],
                                                          start=(dy == 0), stop=(dy == 2))
                        mm.then_inc(conv_done, 1)

                    def turn(s, u):
                        wait(pe, weighted, s, UNITS, u + 1)
                        wait(pe, turned_sb, s, UNITS, u)
                        for k in range(TAPS):
                            mm = nc.tensor.transpose(tps[:, k // 4, P * (k % 4):P * (k % 4) + P], gat[u % RING][:, k, :, :], ident[:, :])
                        mm.then_inc(turned, 1)

                    def mix(s, u):
                        t, b = u // B, u % B
                        wait(pe, turned_sb, s, UNITS, u + 1)
                        if b == 0:
                            wait(pe, added, s, TPS, t - 1)
                        for k in range(TAPS):
                            mm = nc.tensor.matmul(ops[t % 2][C * b:C * b + C, 0:P], wd[:, k, :], gts[u % 2][:, k, :],
                                                  start=(k == 0), stop=(k == TAPS - 1))
                        mm.then_inc(mixed, 1)

                    def strip(s, i, half, last):
                        if not last:
                            conv_strip(s + 1, 1 - i, half)
                        for u in range(UNITS):
                            turn(s, u)
                            mix(s, u)
                    conv_strip(0, 0, 0)
                    strip(0, 0, 0, False)
                    with pe.Fori(0, NSTRIP // 2 - 1) as h:
                        strip(h * 2 + 1, 1, h + 1, False)
                        strip(h * 2 + 2, 0, h + 1, False)
                    strip(NSTRIP - 1, 1, 0, True)

            @block.scalar
            def _(act):
                with when(act, far):
                    def sigmoid(s):
                        wait(act, logit_ready, s, 1, 1)
                        nc.scalar.activation(msk[:, :, :], logit[:, :, :], ACT.Sigmoid).then_inc(mask_ready, 1)

                    def strip(s, i, first, last):
                        if not last:
                            sigmoid(s + 1)
                        for u in range(UNITS):
                            wait(act, turned, s, UNITS, u + 1)
                            wait(act, mixed, s, UNITS, u - 1)
                            nc.scalar.copy(gts[u % 2][:, :, :].rearrange("p k n -> p (k n)"),
                                           tps[:, :, :].rearrange("p k n -> p (k n)")[:, 0:TAPS * P]).then_inc(turned_sb, 1)
                    sigmoid(0)
                    strips(act, strip)

            @block.gpsimd
            def _(pool):
                with when(pool, far):
                    def strip(s, i, first, last):
                        wait(pool, coords_ready, s, 1, 1)
                        for u in range(UNITS):
                            wait(pool, turned, s, UNITS, u + 1 - RING)
                            pool.sem_inc(slot_free, 1)
                            for k in range(TAPS):
                                pool.indirect_dma_start(gat[u % RING][:, k, :, :].rearrange("p a c -> p (a c)"), None, table,
                                                        bass.IndirectOffsetOnAxis(ap=ixu[i][:, u, k:k + 1], axis=0)
                                                        ).then_inc(gathered[u % RING], 16)
                    strips(pool, strip)

            @block.vector
            def _(dve):
                with when(dve, far):
                    STEPS = 13

                    def coords(s, i):
                        n = [0]

                        def link(ins):
                            n[0] += 1
                            ins.then_inc(chain, 1)
                            wait(dve, chain, s, STEPS, n[0])
                        wait(dve, conv_done, s, 1, 1)
                        wait(dve, mask_ready, s, 1, 0)
                        for h in range(2):
                            u0 = 12 * h
                            conv = cps[h][:, 0:324].rearrange("p (u o) -> p u o", u=12)
                            nc.vector.tensor_tensor(pos[:, u0:u0 + 12, :, :].rearrange("p u a k -> p u (a k)"), conv[:, :, 0:18],
                                                    base[:, u0:u0 + 12, :, :].rearrange("p u a k -> p u (a k)"), ALU.add).then_inc(conv_read, 1)
                            nc.vector.tensor_tensor(logit[:, u0:u0 + 12, :], conv[:, :, 18:27],
                                                    bias[:, 18:27].unsqueeze(1).broadcast_to([P, 12, 9]), ALU.add).then_inc(conv_read, 1)
                        wait(dve, conv_read, s, 4, 4)
                        nc.vector.tensor_scalar(base[:, :, 0, :], base[:, :, 0, :], float(TR), None, ALU.add).then_inc(logit_ready, 1)
                        link(nc.vector.tensor_scalar(pos[:, :, :, :], pos[:, :, :, :], -float(EDGE), float(H), ALU.max, ALU.min))
                        link(nc.vector.tensor_copy(ii[:, :, :, :], pos[:, :, :, :]))
                        link(nc.vector.tensor_copy(fl[:, :, :, :], ii[:, :, :, :]))
                        link(nc.vector.tensor_tensor(lt[:, :, :, :], pos[:, :, :, :], fl[:, :, :, :], ALU.is_lt))
                        link(nc.vector.tensor_tensor(fl[:, :, :, :], fl[:, :, :, :], lt[:, :, :, :], ALU.subtract))
                        link(nc.vector.tensor_tensor(pos[:, :, :, :], pos[:, :, :, :], fl[:, :, :, :], ALU.subtract))
                        link(nc.vector.scalar_tensor_tensor(ixf[:, :, :], fl[:, :, 0, :], float(TX), fl[:, :, 1, :], ALU.mult, ALU.add))
                        wait(dve, mask_ready, s, 1, 1)
                        link(nc.vector.tensor_tensor(ixu[i][:, :, :], ixf[:, :, :], ixb[:, :, :], ALU.add))
                        link(nc.vector.tensor_tensor(gy[:, 1, :, :], pos[:, :, 0, :], msk[:, :, :], ALU.mult))
                        link(nc.vector.tensor_tensor(gy[:, 0, :, :], msk[:, :, :], gy[:, 1, :, :], ALU.subtract))
                        link(nc.vector.tensor_tensor(wt[i][:, :, :, 3], gy[:, 1, :, :], pos[:, :, 1, :], ALU.mult))
                        link(nc.vector.tensor_tensor(wt[i][:, :, :, 2], gy[:, 0, :, :], pos[:, :, 1, :], ALU.mult))
                        link(nc.vector.tensor_tensor(wt[i][:, :, :, 1], gy[:, 1, :, :], wt[i][:, :, :, 3], ALU.subtract))
                        assert n[0] == STEPS
                        nc.vector.tensor_tensor(wt[i][:, :, :, 0], gy[:, 0, :, :], wt[i][:, :, :, 2], ALU.subtract).then_inc(coords_ready, 1)

                    def strip(s, i, first, last):
                        wait(dve, coords_ready, s, 1, 1)
                        if not last:
                            coords(s + 1, 1 - i)
                        for u in range(UNITS):
                            wait(dve, gathered[u % RING], s, 16 * TAPS * (UNITS // RING), 16 * TAPS * (u // RING + 1))
                            nc.vector.tensor_tensor(gat[u % RING][:, :, :, :], gat[u % RING][:, :, :, :],
                                                    wt[i][:, u, :, :].unsqueeze(3).broadcast_to([P, TAPS, 4, C]), ALU.mult).then_inc(weighted, 1)
                            if u % B == 1 and u > B:
                                residual(s, u // B - 1)
                        residual(s, TPS - 1)

                    def residual(s, t):
                        wait(dve, mixed, s, UNITS, B * t + B)
                        xv = x_sb[:, ds(s * (TR * W) + P * t, P)]
                        nc.vector.tensor_tensor(xv, xv, ops[t % 2][:, 0:P], ALU.add).then_inc(added, 1)
                    coords(0, 0)
                    strips(dve, strip)


def host_l1(ow, ob, mw, mb, dw):
    wk = np.concatenate([ow[0::2], ow[1::2], mw], 0)
    convw = np.ascontiguousarray(wk.transpose(3, 1, 2, 0).reshape(3 * C, 3, 27))
    bias = np.tile(np.concatenate([ob[0::2], ob[1::2], mb]), (P, 1))
    dcn = np.tile(dw.reshape(C, C, 9).transpose(1, 2, 0), (4, 1, 1))
    p = np.arange(P)
    k = np.arange(9)
    u = np.arange(UNITS)
    px = P * (u // B)[None, :] + p[:, None]
    r, c = px // W, px % W
    coord = np.zeros((P, UNITS, 2, 9), np.float32)
    coord[:, :, 0, :] = r[:, :, None] - 1 + (k // 3)[None, None]
    coord[:, :, 1, :] = c[:, :, None] - 1 + (k % 3)[None, None]
    ixb = np.zeros((P, UNITS, 9), np.float32)
    ixb[:] = (1 + (u % B) * TROWS * TX + EDGE * TX + EDGE)[None, :, None]
    return dict(convw=convw, bias=np.ascontiguousarray(bias), coord=coord, ixb=ixb, dcn=np.ascontiguousarray(dcn))



F16 = mybir.dt.float16
DR = 4
DPX = DR * W
DTILES = H // DR
BK = B * TAPS
LAG = 3
LOW = 64
PROWS = LOW + BK
UNIT = 32.0


def stage_deform_near(nc, x_sb, convw, convb, rep, sel, dcn, shifts, ident_d, x_save, far):
    with ExitStack() as ctx:
        sb = lambda n, s, dt=F: ctx.enter_context(nc.sbuf_tensor("dn_" + n, s, dt))
        sem = lambda n: ctx.enter_context(nc.semaphore("dn_" + n))
        psum = lambda n, s: ctx.enter_context(nc.psum_tensor("dn_" + n, s, F))
        xp = sb("xp", [P, H + 2 * EDGE, W + 2 * EDGE])
        wconv = sb("wconv", [P, TAPS, 3 * BK])
        bconv = sb("bconv", [3 * BK, 1])
        repw = sb("repw", [3 * BK, 3, PROWS])
        self32 = sb("self32", [PROWS, TAPS, P])
        selw = sb("selw", [PROWS, TAPS, P], F16)
        wd = sb("wd", [P, TAPS, P])
        shift = sb("shift", [PROWS, 4])
        ident = sb("ident", [P, P])
        stage_norm(nc, "gn1", x_sb, xp, EDGE,
                   loads=((wconv[:, :, :], convw), (bconv[:, :], convb), (repw[:, :, :], rep), (self32[:, :, :], sel),
                          (shift[:, :], shifts), (wd[:, :, :], dcn), (ident[:, :], ident_d)))
        maps = sb("maps", [3 * BK, DPX])
        hat_y = sb("hat_y", [PROWS, 3, DPX])
        hat_x = sb("hat_x", [PROWS, 3, DPX])
        mask = sb("mask", [PROWS, DPX])
        corner = sb("corner", [PROWS, 3, 3, DPX])
        parts = [sb(f"parts{i}", [PROWS, 3, 3, DPX], F16) for i in range(2)]
        prod = [sb(f"prod{i}", [P, 9, DPX]) for i in range(2)]
        part_sum = [sb(f"part_sum{i}", [P, 4, DPX]) for i in range(LAG)]
        least = sb("least", [PROWS, 2 * DTILES])
        lowest = sb("lowest", [PROWS, 1])
        bottom = sb("bottom", [1, 1])
        wps = [psum(f"wps{i}", [P, 3, 512]) for i in range(2)]
        ops = psum("ops", [P, 512])
        aps = psum("aps", [P, 512])
        saved, sel_ready = sem("saved"), sem("sel_ready")
        conv_done, maps_ready, copied = sem("conv_done"), sem("maps_ready"), sem("copied")
        dist_ready, mask_ready, hats_ready, least_ready = sem("dist_ready"), sem("mask_ready"), sem("hats_ready"), sem("least_ready")
        scaled, corner_ready, high_ready, parts_ready = sem("scaled"), sem("corner_ready"), sem("high_ready"), sem("parts_ready")
        weights_ready, products, pairs_done, last_done = sem("weights_ready"), sem("products"), sem("pairs_done"), sem("last_done")
        contracted, added, lowest_ready, turned = sem("contracted"), sem("added"), sem("lowest_ready"), sem("turned")
        block = ctx.enter_context(nc.Block())

        def tiles(eng, body):
            body(0, 0, 0)
            body(1, 1, 0)
            with eng.Fori(1, DTILES // 2 - 1) as h:
                body(h * 2, 0, 0)
                body(h * 2 + 1, 1, 0)
            body(DTILES - 2, 0, 1)
            body(DTILES - 1, 1, 2)

        @block.sync
        def _(sp):
            sp.dma_start(x_save, x_sb[:, :]).then_inc(saved, 16)
            sp.wait_ge(saved, 16)

        @block.tensor
        def _(pe):
            def conv(j, k):
                if k == 0:
                    wait(pe, mask_ready, j, 1, 0)
                mm = nc.tensor.matmul(aps[0:3 * BK, 0:DPX], wconv[:, k, :], xp[:, ds(j * DR + (EDGE - 1 + k // 3), DR), EDGE - 1 + k % 3:EDGE - 1 + k % 3 + W],
                                      start=(k == 0), stop=(k == TAPS - 1))
                if k == TAPS - 1:
                    mm.then_inc(conv_done, 1)

            def copy_rows(j, a):
                if a == 0:
                    wait(pe, maps_ready, j, 1, 1)
                else:
                    wait(pe, dist_ready, j, 6, 3 * a)
                nc.tensor.matmul(aps[0:PROWS, 0:DPX], repw[:, a, :], maps[:, :], start=True, stop=True).then_inc(copied, 1)

            CONV_AT = {2: (0,), 3: (1,), 4: (2,), 5: (3, 4), 6: (5, 6), 7: (7, 8)}

            def weights(t, i, k, sy):
                n = 3 * k + sy
                if n == 0:
                    wait(pe, parts_ready, t, 3, 3)
                wait(pe, products, t, 27, n - 1)
                for sx in range(3):
                    mm = nc.tensor.matmul(wps[(n + i) % 2][:, sx, 0:DPX], selw[:, k, :], parts[i][:, sy, sx, :], start=True, stop=True)
                mm.then_inc(weights_ready, 1)

            def contract(t, k, lo, hi):
                if lo == hi:
                    return
                tt, kk = (t, k) if k >= 0 else (t + (-1), k + TAPS)
                if k < 0 and isinstance(t, int) and t == 0:
                    return
                s = kk % LAG
                if lo == 0:
                    wait(pe, pairs_done, tt, TAPS, kk + 1)
                    if kk == 0:
                        wait(pe, added, tt, 1, 0)
                if hi == 4:
                    wait(pe, last_done, tt, TAPS, kk + 1)
                for q in range(lo, hi):
                    mm = nc.tensor.matmul(ops[:, 0:DPX], wd[:, kk, :], part_sum[s][:, q, :],
                                          start=(kk == 0 and q == 0), stop=(kk == TAPS - 1 and q == 3))
                if hi == 4:
                    mm.then_inc(contracted, 1)

            def tile(t, i, last):
                for k in range(TAPS):
                    for sy in range(3):
                        weights(t, i, k, sy)
                        first, end = ((0, 0), (0, 2), (2, 4))[sy] if k == LAG else ((0, 1), (1, 2), (2, 4))[sy]
                        contract(t, k - LAG, first, end)
                        if k < 2 and sy == 0 and last < 2:
                            copy_rows(t + 1, k + 1)
                        if not last:
                            if sy < len(CONV_AT.get(k, ())):
                                conv(t + 2, CONV_AT[k][sy])
                            if k == TAPS - 1 and sy == 1:
                                copy_rows(t + 2, 0)
                if last == 2:
                    for k in range(TAPS - LAG, TAPS):
                        contract(t, k, 0, 4)
            pe.wait_ge(sel_ready, 1)
            for j in range(2):
                for k in range(TAPS):
                    conv(j, k)
                copy_rows(j, 0)
                if j == 0:
                    copy_rows(j, 1)
                    copy_rows(j, 2)
            tiles(pe, tile)
            pe.wait_ge(lowest_ready, 1)
            nc.tensor.transpose(aps[0:1, 0:PROWS], lowest[:, :], ident[0:PROWS, 0:PROWS]).then_inc(turned, 1)

        @block.scalar
        def _(act):
            def high(j, i, sy):
                wait(act, corner_ready, j, 3, sy + 1)
                if sy == 0:
                    wait(act, weights_ready, j, 27, -27)
                nc.scalar.copy(parts[i][:, sy, :, :], corner[:, sy, :, :]).then_inc(high_ready, 1)

            def bias_maps(j):
                wait(act, conv_done, j, 1, 1)
                nc.scalar.activation(maps[:, :], aps[0:3 * BK, 0:DPX], ACT.Identity, bias=bconv[:, 0:1]).then_inc(maps_ready, 1)

            def distances(j, a):
                wait(act, copied, j, 3, a + 1)
                if a == 0:
                    wait(act, corner_ready, j, 3, 0)
                wait(act, least_ready, j, 2, a - 1)
                hat = (hat_y, hat_x)[a]
                for s in range(3):
                    nc.scalar.activation(hat[:, s, :], aps[0:PROWS, 0:DPX], ACT.Abs, bias=shift[:, s:s + 1], scale=UNIT).then_inc(dist_ready, 1)
                wait(act, dist_ready, j, 6, 3 * a + 3)
                nc.scalar.activation(hat[:, :, :], hat[:, :, :], ACT.Relu, bias=shift[:, 3:4], scale=-1.0).then_inc(hats_ready, 1)

            def masks(j):
                wait(act, copied, j, 3, 3)
                nc.scalar.activation(mask[:, :], aps[0:PROWS, 0:DPX], ACT.Sigmoid).then_inc(mask_ready, 1)

            def tile(t, i, last):
                if last < 2:
                    distances(t + 1, 1)
                    masks(t + 1)
                    for sy in range(3):
                        high(t + 1, 1 - i, sy)
                if not last:
                    bias_maps(t + 2)
                    distances(t + 2, 0)
            nc.scalar.copy(selw[:, :, :], self32[:, :, :]).then_inc(sel_ready, 1)
            bias_maps(0)
            distances(0, 0)
            distances(0, 1)
            masks(0)
            bias_maps(1)
            for sy in range(3):
                high(0, 0, sy)
            distances(1, 0)
            tiles(act, tile)

        @block.gpsimd
        def _(pool):
            def prepare(j, slot):
                if slot == 2:
                    wait(pool, hats_ready, j, 2, 1)
                    wait(pool, least_ready, j, 2, 1)
                    wait(pool, mask_ready, j, 1, 1)
                    nc.gpsimd.tensor_tensor(hat_y[:, :, :], hat_y[:, :, :], mask[:, :].unsqueeze(1).broadcast_to([PROWS, 3, DPX]),
                                            ALU.mult).then_inc(scaled, 1)
                elif 3 <= slot <= 5:
                    sy = slot - 3
                    if sy == 0:
                        wait(pool, parts_ready, j, 3, 0)
                    if sy == 0:
                        wait(pool, hats_ready, j, 2, 2)
                        wait(pool, scaled, j, 1, 1)
                    nc.gpsimd.tensor_tensor(corner[:, sy, :, :], hat_x[:, :, :], hat_y[:, sy:sy + 1, :].broadcast_to([PROWS, 3, DPX]),
                                            ALU.mult).then_inc(corner_ready, 1)

            def tile(t, i, last):
                for k in range(TAPS):
                    g = (TAPS * i + k) % 2
                    wait(pool, products, t, 27, 3 * k + 3)
                    wait(pool, contracted, t, TAPS, k - LAG + 1)
                    nc.gpsimd.tensor_tensor(part_sum[k % LAG][:, :, :], prod[g][:, 0:4, :], prod[g][:, 4:8, :], ALU.add).then_inc(pairs_done, 1)
                    if last < 2:
                        prepare(t + 1, k)
            for slot in range(TAPS):
                prepare(0, slot)
            tiles(pool, tile)

        @block.vector
        def _(dve):
            def smallest(j, a):
                hat = (hat_y, hat_x)[a]
                wait(dve, hats_ready, j, 2, a + 1)
                nc.vector.tensor_reduce(least[:, ds(j * 2 + a, 1)], hat[:, 1, :], AX.X, ALU.min).then_inc(least_ready, 1)

            def low(j, i, sy):
                wait(dve, high_ready, j, 3, sy + 1)
                nc.vector.tensor_tensor(parts[i][LOW:, sy, :, :], corner[LOW:, sy, :, :], parts[i][LOW:, sy, :, :],
                                        ALU.subtract).then_inc(parts_ready, 1)

            def last_sum(t, k, i):
                if k < 0:
                    if isinstance(t, int) and t == 0:
                        return
                    t, k, i = t + (-1), k + TAPS, 1 - i
                g = (TAPS * i + k) % 2
                wait(dve, products, t, 27, 3 * k + 3)
                wait(dve, pairs_done, t, TAPS, k + 1)
                nc.vector.tensor_tensor(part_sum[k % LAG][:, 3, :], part_sum[k % LAG][:, 3, :], prod[g][:, 8, :], ALU.add).then_inc(last_done, 1)

            def residual(t):
                wait(dve, contracted, t, TAPS, TAPS)
                if isinstance(t, int) and t == 0:
                    dve.wait_ge(saved, 16)
                xv = x_sb[:, ds(t * DPX, DPX)]
                nc.vector.tensor_tensor(xv, xv, ops[:, 0:DPX], ALU.add).then_inc(added, 1)

            def tile(t, i, last):
                for k in range(TAPS):
                    ky, kx = k // 3, k % 3
                    g = (TAPS * i + k) % 2
                    for sy in range(3):
                        n = 3 * k + sy
                        if n == 3 * LAG and not (isinstance(t, int) and t == 0):
                            residual(t + (-1))
                        wait(dve, weights_ready, t, 27, n + 1)
                        if sy == 0:
                            wait(dve, pairs_done, t, TAPS, k - 1)
                        if sy == 1:
                            last_sum(t, k - 2, i)
                        if sy == 2:
                            wait(dve, last_done, t, TAPS, k - 1)
                        row = xp[:, ds(t * DR + (ky + sy), DR), kx:kx + W]
                        near = bass.AP(row.tensor, row.offset, [row.ap[0], [1, 3], *row.ap[1:]])
                        nc.vector.tensor_tensor(prod[g][:, 3 * sy:3 * sy + 3, :].rearrange("p s (r c) -> p s r c", r=DR),
                                                wps[(n + i) % 2][:, :, 0:DPX].rearrange("p s (r c) -> p s r c", r=DR), near,
                                                ALU.mult).then_inc(products, 1)
                    if k < 2 and last < 2:
                        smallest(t + 1, k)
                    if 5 <= k <= 7 and last < 2:
                        low(t + 1, 1 - i, k - 5)
                if last == 2:
                    last_sum(t, 7, i)
                    last_sum(t, 8, i)
                    residual(t)
            smallest(0, 0)
            smallest(0, 1)
            for sy in range(3):
                low(0, 0, sy)
            tiles(dve, tile)
            dve.wait_ge(least_ready, 2 * DTILES)
            nc.vector.tensor_reduce(lowest[:, :], least[:, :], AX.X, ALU.min).then_inc(lowest_ready, 1)
            dve.wait_ge(turned, 1)
            nc.vector.tensor_reduce(bottom[:, :], aps[0:1, 0:PROWS], AX.X, ALU.min).then_inc(lowest_ready, 1)
            dve.wait_ge(lowest_ready, 2)
            nc.vector.tensor_scalar(far, bottom[:, :], 0.0, None, ALU.is_le)


def host_l1d(ow, ob, mw, mb, dw):
    w3 = np.stack([ow[0::2], ow[1::2], mw]).reshape(3, TAPS, C, 9)
    convw = np.zeros((B, C, 9, 3, TAPS, B), np.float32)
    wd = np.zeros((B, C, 9, B, C), np.float32)
    sel = np.zeros((PROWS, TAPS, P), np.float32)
    rep = np.zeros((3, TAPS, B, 3, PROWS), np.float32)
    for b in range(B):
        convw[b, :, :, :, :, b] = w3.transpose(2, 3, 0, 1)
        wd[b, :, :, b, :] = dw.reshape(C, C, 9).transpose(1, 2, 0)
        for k in range(TAPS):
            for r in (k * B + b, LOW + k * B + b):
                sel[r, k, C * b:C * b + C] = UNIT ** -2
                for a in range(3):
                    rep[a, k, b, a, r] = 1
    bias = np.repeat(np.stack([ob[0::2], ob[1::2], mb]).reshape(-1), B)[:, None]
    return dict(convw=convw.reshape(P, 9, 3 * BK), convb=np.ascontiguousarray(bias), rep=rep.reshape(3 * BK, 3, PROWS), sel=sel,
                dcnbd=wd.reshape(P, 9, P), shifts=np.tile(UNIT * np.array([1, 0, -1, 1], np.float32), (PROWS, 1)))



KX, KY = 32, 16
M1 = M2 = 4
L1_IN, HIDN = C * M1 * M2 * 2, 128
FW = 2 * KY + 2 * M2
NG = 4
GX = KX // NG
MODES = GX * KY
ZM = NG * B * 2
LRows = 8


def stage_fourier(nc, x_sb, fw_d, fh_d, ch_d, ih_d, iw_d, w1, w2, lin1, b1, lin2, b2, ident_d):
    with ExitStack() as outer:
        sb = lambda n, s, dt=F: outer.enter_context(nc.sbuf_tensor("fo_" + n, s, dt))
        ident = sb("ident", [P, P])
        fw = sb("fw", [W, FW])
        fh = sb("fh", [H, 2, 2 * KX])
        ch = sb("ch", [H, 2, 2 * M1])
        ih = sb("ih", [2 * KX, 2 * H])
        iw = sb("iw", [P, 4, W])
        wts = sb("wts", [P, C, GX, KY * 2])
        l1w = sb("l1w", [C, 2 * M1 * M2, HIDN])
        b1s = sb("b1s", [HIDN, 1])
        l2w = sb("l2w", [HIDN, C])
        b2s = sb("b2s", [P, 1])
        y = sb("y", [P, FW, H])
        yt = sb("yt", [H, FW, P])
        z = sb("z", [P, KX, KY, 2])
        zi = sb("zi", [P, B, GX, KY * 2])
        flat = sb("flat", [P, M1, M2, 2])
        fl = sb("fl", [C, B, 2 * M1 * M2])
        corr = sb("corr", [P, 1])
        with ExitStack() as ctx:
            sem = lambda n: ctx.enter_context(nc.semaphore("ff_" + n))
            sbc = lambda n, s, dt=F: ctx.enter_context(nc.sbuf_tensor("ff_" + n, s, dt))
            psum = lambda n, s: ctx.enter_context(nc.psum_tensor("ff_" + n, s, F))
            stats = sbc("stats", [P, 18, 6])
            agg = sbc("agg", [P, 8])
            rows = [sbc(f"rows{i}", [P, LRows, W]) for i in range(2)]
            xt = [sbc(f"xt{i}", [W, LRows, P]) for i in range(2)]
            tps = [psum(f"tps{i}", [P, 2, 512]) for i in range(2)]
            yps = [psum(f"yps{i}", [P, 512]) for i in range(2)]
            zps = [psum(f"zps{i}", [P, 512]) for i in range(2)]
            loaded_first, loaded, moved, root_ready, var_ready, step = sem("loaded_first"), sem("loaded"), sem("moved"), sem("root_ready"), sem("var_ready"), sem("step")
            stats_done = sem("stats_done")
            rows_ready, turned, xt_ready, y_done, y_sb = sem("rows_ready"), sem("turned"), sem("xt_ready"), sem("y_done"), sem("y_sb")
            yturned, yt_sb, z_done, z_sb = sem("yturned"), sem("yt_sb"), sem("z_done"), sem("z_sb")
            block = ctx.enter_context(nc.Block())
            mean, var, std, rstd, t = (agg[:, k:k + 1] for k in range(5))
            G8 = H // LRows

            @block.sync
            def _(sp):
                loads = [(ident[:, :], ident_d), (fw[:, :], fw_d), (fh[:, :, :], fh_d), (ch[:, :, :], ch_d), (ih[:, :], ih_d),
                         (iw[:, :, :], iw_d), (l1w[:, :, :], lin1.rearrange("(c j) n -> c j n", c=C)), (b1s[:, :], b1), (l2w[:, :], lin2), (b2s[:, :], b2)]
                for k, (dst, src) in enumerate(loads):
                    sp.dma_start(dst, src).then_inc(loaded_first if k < 4 else loaded, 16)
                for g in range(NG):
                    w = (w1, w2)[g // 2]
                    k0 = GX * (g % 2)
                    sp.dma_start(wts[C * g:C * g + C, :, :, :].rearrange("i o k y -> i o (k y)"),
                                 w[:, :, k0:k0 + GX, :, :].rearrange("i o k y r -> i o (k y r)")).then_inc(loaded, 16)
                sp.wait_ge(loaded, 160)
                sp.wait_ge(z_sb, 3)
                for b in range(B):
                    for g in range(NG):
                        sp.dma_start(zi[C * g:C * g + C, b, :, :].rearrange("i k y -> i (k y)"),
                                     z[C * b:C * b + C, GX * g:GX * g + GX, :, :].rearrange("i k y r -> i (k y r)")).then_inc(moved, 16)
                    sp.dma_start(fl[:, b, :], flat[C * b:C * b + C, :, :, :].rearrange("c a b r -> c (a b r)")).then_inc(moved, 16)
                sp.wait_ge(moved, 16 * B * (NG + 1))

            @block.vector
            def _(dve):
                for k in range(18):
                    nc.vector.bn_stats(stats[:, k, :], x_sb[:, k * 512:(k + 1) * 512]).then_inc(stats_done, 1)
                dve.wait_ge(stats_done, 18)
                nc.vector.bn_aggr(agg[:, 0:2], stats[:, :, :]).then_inc(step, 1)
                dve.wait_ge(step, 1)
                nc.vector.tensor_scalar(var, var, 1e-5, None, ALU.add).then_inc(var_ready, 1)
                dve.wait_ge(root_ready, 1)
                nc.vector.reciprocal(rstd, std).then_inc(step, 1)
                dve.wait_ge(step, 2)
                nc.vector.tensor_tensor(t, rstd, rstd, ALU.mult).then_inc(step, 1)
                dve.wait_ge(step, 3)
                nc.vector.tensor_tensor(t, t, var, ALU.mult).then_inc(step, 1)
                dve.wait_ge(step, 4)
                nc.vector.tensor_scalar(t, t, -0.5, 1.5, ALU.mult, ALU.add).then_inc(step, 1)
                dve.wait_ge(step, 5)
                nc.vector.tensor_tensor(rstd, rstd, t, ALU.mult).then_inc(step, 1)
                dve.wait_ge(step, 6)

                def normalise(g, s):
                    wait(dve, turned, g, 1, -1)
                    nc.vector.tensor_scalar(rows[s][:, :, :].rearrange("p r c -> p (r c)"), x_sb[:, ds(g * (LRows * W), LRows * W)],
                                            mean, rstd, ALU.subtract, ALU.mult).then_inc(rows_ready, 1)

                def keep(g, s):
                    wait(dve, turned, g, 1, 1)
                    wait(dve, y_done, g, 1, -1)
                    nc.vector.tensor_copy(xt[s][:, :, :].rearrange("p r n -> p (r n)"), tps[s][0:W, :, :].rearrange("p k n -> p (k n)")).then_inc(xt_ready, 1)
                normalise(0, 0)
                normalise(1, 1)
                keep(0, 0)
                normalise(2, 0)
                keep(1, 1)
                with dve.Fori(1, G8 // 2 - 1) as h:
                    normalise(h * 2 + 1, 1)
                    keep(h * 2, 0)
                    normalise(h * 2 + 2, 0)
                    keep(h * 2 + 1, 1)
                normalise(G8 - 1, 1)
                keep(G8 - 2, 0)
                keep(G8 - 1, 1)
                for q in range(FW // 4):
                    dve.wait_ge(yturned, q + 1)
                    nc.vector.tensor_copy(yt[:, 4 * q:4 * q + 4, :].rearrange("p f n -> p (f n)"), tps[q % 2][0:H, 0, :]).then_inc(yt_sb, 1)

            @block.scalar
            def _(act):
                act.wait_ge(var_ready, 1)
                nc.scalar.activation(std, var, ACT.Sqrt).then_inc(root_ready, 1)

                def keep(g, s):
                    wait(act, y_done, g, 1, 1)
                    nc.scalar.copy(y[:, :, ds(g * LRows, LRows)], yps[s][:, 0:LRows * FW].rearrange("p (r f) -> p f r", r=LRows)).then_inc(y_sb, 1)
                with act.Fori(0, G8 // 2) as h:
                    keep(h * 2, 0)
                    keep(h * 2 + 1, 1)
                for k in range(2):
                    act.wait_ge(z_done, k + 1)
                    nc.scalar.copy(z[:, :, 8 * k:8 * k + 8, :], zps[k][:, :].rearrange("p (y k r) -> p k y r", y=8, r=2)).then_inc(z_sb, 1)
                act.wait_ge(z_done, 3)
                nc.scalar.copy(flat[:, :, :, :], yps[0][:, 0:2 * M1 * M2].rearrange("p (b a r) -> p a b r", b=M2, r=2)).then_inc(z_sb, 1)

            @block.tensor
            def _(pe):
                pe.wait_ge(loaded_first, 16 * 4)

                def turn(g, s):
                    wait(pe, rows_ready, g, 1, 1)
                    wait(pe, xt_ready, g, 1, -1)
                    for r in range(LRows):
                        mm = nc.tensor.transpose(tps[s][0:W, r // 4, P * (r % 4):P * (r % 4) + P], rows[s][:, r, :], ident[:, :])
                    mm.then_inc(turned, 1)

                def along_width(g, s):
                    wait(pe, xt_ready, g, 1, 1)
                    wait(pe, y_sb, g, 1, -1)
                    for r in range(LRows):
                        mm = nc.tensor.matmul(yps[s][:, FW * r:FW * r + FW], xt[s][:, r, :], fw[:, :], start=True, stop=True)
                    mm.then_inc(y_done, 1)
                turn(0, 0)
                turn(1, 1)
                along_width(0, 0)
                turn(2, 0)
                along_width(1, 1)
                with pe.Fori(1, G8 // 2 - 1) as h:
                    turn(h * 2 + 1, 1)
                    along_width(h * 2, 0)
                    turn(h * 2 + 2, 0)
                    along_width(h * 2 + 1, 1)
                turn(G8 - 1, 1)
                along_width(G8 - 2, 0)
                along_width(G8 - 1, 1)
                pe.wait_ge(y_sb, G8)
                for q in range(FW // 4):
                    if q == 0:
                        pe.wait_ge(xt_ready, G8)
                    if q >= 2:
                        pe.wait_ge(yt_sb, q - 1)
                    for f in range(4):
                        mm = nc.tensor.transpose(tps[q % 2][0:H, 0, P * f:P * f + P], y[:, 4 * q + f, :], ident[:, :])
                    mm.then_inc(yturned, 1)
                for k in range(KY):
                    pe.wait_ge(yt_sb, (2 * k + 1) // 4 + 1)
                    for part in range(2):
                        mm = nc.tensor.matmul(zps[k // 8][:, 64 * (k % 8):64 * (k % 8) + 64], yt[:, 2 * k + part, :], fh[:, part, :],
                                              start=(part == 0), stop=(part == 1))
                    if k % 8 == 7:
                        mm.then_inc(z_done, 1)
                pe.wait_ge(yt_sb, FW // 4)
                for k in range(M2):
                    for part in range(2):
                        mm = nc.tensor.matmul(yps[0][:, 8 * k:8 * k + 8], yt[:, 2 * KY + M2 * part + k, :], ch[:, part, :],
                                              start=(part == 0), stop=(part == 1))
                mm.then_inc(z_done, 1)

        with ExitStack() as ctx:
            sem = lambda n: ctx.enter_context(nc.semaphore("fb_" + n))
            sbc = lambda n, s, dt=F: ctx.enter_context(nc.sbuf_tensor("fb_" + n, s, dt))
            psum = lambda n, s: ctx.enter_context(nc.psum_tensor("fb_" + n, s, F))
            wst = [sbc(f"wst{i}", [P, C, KY, 2]) for i in range(2)]
            zst = [sbc(f"zst{i}", [P, 2, KY, NG, B, 2]) for i in range(2)]
            o = sbc("o", [C, B, NG, GX, KY * 2])
            hb = sbc("hb", [HIDN, B])
            g = sbc("g", [P, H, KY, 2])
            z2 = sbc("z2", [P, KY, 2, KX])
            ot = sbc("ot", [2 * KX, KY, P])
            gt = [sbc(f"gt{i}", [P, 4, P]) for i in range(2)]
            mps = [psum(f"mps{i}", [P, 512]) for i in range(2)]
            hps = psum("hps", [P, 512])
            cps = psum("cps", [P, 512])
            tps = [psum(f"tps{i}", [P, 512]) for i in range(2)]
            ops = [psum(f"ops{i}", [P, 512]) for i in range(2)]
            staged, mixed, o_sb, moved = sem("staged"), sem("mixed"), sem("o_sb"), sem("moved")
            h_done, h_ready, c_done, c_ready = (sem(n) for n in ("h_done", "h_ready", "c_done", "c_ready"))
            sorted_, oturned, ot_sb, g_done, g_sb = sem("sorted"), sem("oturned"), sem("ot_sb"), sem("g_done"), sem("g_sb")
            gturned, gt_sb, back, added = sem("gturned"), sem("gt_sb"), sem("back"), sem("added")
            zeroed, zstaged, mix_begun = sem("zeroed"), sem("zstaged"), sem("mix_begun")
            block = ctx.enter_context(nc.Block())

            @block.sync
            def _(sp):
                sp.wait_ge(o_sb, NG * GX)
                for b in range(B):
                    sp.dma_start(z[C * b:C * b + C, :, :, :].rearrange("i k y r -> i (k y r)"),
                                 o[:, b, :, :, :].rearrange("i q k y -> i (q k y)")).then_inc(moved, 16)
                sp.wait_ge(moved, 16 * B)

            @block.gpsimd
            def _(pool):
                for i in range(2):
                    nc.gpsimd.memset(zst[i][:, :, :, :, :, :], 0.0).then_inc(zeroed, 1)

            @block.scalar
            def _(act):
                def stage(k, s):
                    wait(act, mixed, k, 1, -1)
                    nc.scalar.copy(wst[s][:, :, :, :].rearrange("p o y r -> p o (y r)"), wts[:, :, ds(k, 1), :].rearrange("p o k y -> p o (k y)")).then_inc(staged, 1)
                stage(0, 0)
                stage(1, 1)
                with act.Fori(1, GX // 2) as h:
                    stage(h * 2, 0)
                    stage(h * 2 + 1, 1)
                act.wait_ge(h_done, 1)
                nc.scalar.activation(hb[:, :], hps[:, 0:B], ACT.Gelu, bias=b1s[:, 0:1]).then_inc(h_ready, 1)
                act.wait_ge(moved, 16 * B)
                nc.scalar.copy(z2[:, :, :, :], z[:, :, :, :].rearrange("p k y r -> p y r k")).then_inc(sorted_, 1)
                for q in range(KY // 2):
                    act.wait_ge(g_done, q + 1)
                    nc.scalar.copy(g[:, :, 2 * q:2 * q + 2, :],
                                   ops[q % 2][:, 0:4 * H].rearrange("p (y r h) -> p h y r", y=2, r=2)).then_inc(g_sb, 1)
                for q in range(H // 4):
                    act.wait_ge(gturned, q + 1)
                    if q >= 2:
                        act.wait_ge(back, q - 1)
                    nc.scalar.copy(gt[q % 2][:, 0, :], tps[q % 2][:, 0:P]).then_inc(gt_sb, 1)

            @block.vector
            def _(dve):
                def stage(k, s):
                    wait(dve, mixed, k, 1, -1)
                    for q in range(NG):
                        r = slice(C * q, C * q + C)
                        v = zi[r, :, ds(k, 1), :].rearrange("p b k (y r) -> p (b k) y r", r=2)
                        to = zst[s][r, :, :, q, :, :].rearrange("p a y b r -> p a b y r")
                        nc.vector.tensor_copy(to[:, 0], v).then_inc(zstaged, 1)
                        nc.vector.tensor_scalar(to[:, 1, :, :, 0], v[:, :, :, 1], -1.0, None, ALU.mult).then_inc(zstaged, 1)
                        nc.vector.tensor_copy(to[:, 1, :, :, 1], v[:, :, :, 0]).then_inc(zstaged, 1)

                def keep(k, s):
                    wait(dve, mixed, k, 1, 1)
                    for q in range(NG):
                        nc.vector.tensor_copy(o[:, :, q, ds(k, 1), :].rearrange("p b k (y r) -> p (b k) y r", r=2),
                                              mps[s][0:C, :].rearrange("p (y q b r) -> p q b y r", y=KY, q=NG, r=2)[:, q]).then_inc(o_sb, 1)
                dve.wait_ge(zeroed, 2)
                stage(0, 0)
                stage(1, 1)
                keep(0, 0)
                with dve.Fori(0, GX // 2 - 1) as h:
                    stage(h * 2 + 2, 0)
                    keep(h * 2 + 1, 1)
                    stage(h * 2 + 3, 1)
                    keep(h * 2 + 2, 0)
                keep(GX - 1, 1)
                dve.wait_ge(c_done, 1)
                nc.vector.tensor_tensor(corr[:, :], cps[:, 0:1], b2s[:, :], ALU.add).then_inc(c_ready, 1)
                for q in range(KY // 4):
                    dve.wait_ge(oturned, q + 1)
                    nc.vector.tensor_copy(ot[:, 4 * q:4 * q + 4, :].rearrange("p y n -> p (y n)"), tps[q % 2][0:2 * KX, :]).then_inc(ot_sb, 1)
                dve.wait_ge(c_ready, 1)
                for q in range(H // 4):
                    dve.wait_ge(back, q + 1)
                    xv = x_sb[:, 4 * W * q:4 * W * q + 4 * W]
                    nc.vector.scalar_tensor_tensor(xv, ops[q % 2][:, 0:4 * W], corr[:, 0:1], xv, ALU.add, ALU.add).then_inc(added, 1)

            @block.tensor
            def _(pe):
                def mix(k, s):
                    wait(pe, staged, k, 1, 1)
                    wait(pe, zstaged, k, 3 * NG, 3 * NG)
                    wait(pe, o_sb, k, NG, -NG)
                    pe.sem_inc(mix_begun, 1)
                    for m in range(KY):
                        for part in range(2):
                            mm = nc.tensor.matmul(mps[s][0:C, ZM * m:ZM * m + ZM], wst[s][:, :, m, part],
                                                  zst[s][:, part, m, :, :, :], start=(part == 0), stop=(part == 1))
                    mm.then_inc(mixed, 1)
                mix(0, 0)
                mix(1, 1)
                with pe.Fori(1, GX // 2) as h:
                    mix(h * 2, 0)
                    mix(h * 2 + 1, 1)
                for j in range(2 * M1 * M2):
                    mm = nc.tensor.matmul(hps[:, 0:B], l1w[:, j, :], fl[:, :, j], start=(j == 0), stop=(j == 2 * M1 * M2 - 1))
                mm.then_inc(h_done, 1)
                pe.wait_ge(h_ready, 1)
                for b in range(B):
                    mm = nc.tensor.matmul(cps[C * b:C * b + C, 0:1], l2w[:, :], hb[:, b:b + 1], start=True, stop=True)
                mm.then_inc(c_done, 1)
                pe.wait_ge(sorted_, 1)
                for q in range(KY // 4):
                    if q >= 2:
                        pe.wait_ge(ot_sb, q - 1)
                    for j in range(4):
                        mm = nc.tensor.transpose(tps[q % 2][0:2 * KX, P * j:P * j + P], z2[:, 4 * q + j, :, :].rearrange("p r k -> p (r k)"), ident[:, :])
                    mm.then_inc(oturned, 1)
                for q in range(KY // 2):
                    pe.wait_ge(ot_sb, q // 2 + 1)
                    if q >= 2:
                        pe.wait_ge(g_sb, q - 1)
                    for j in range(2):
                        mm = nc.tensor.matmul(ops[q % 2][:, 2 * H * j:2 * H * j + 2 * H], ot[:, 2 * q + j, :], ih[:, :], start=True, stop=True)
                    mm.then_inc(g_done, 1)
                pe.wait_ge(g_sb, KY // 2)
                pe.wait_ge(ot_sb, KY // 4)

                def turn(q):
                    if q >= 2:
                        pe.wait_ge(gt_sb, q - 1)
                    nc.tensor.transpose(tps[q % 2][:, 0:P], g[:, 4 * q:4 * q + 4, :, :].rearrange("p h y r -> p (h y r)"), ident[:, :]).then_inc(gturned, 1)

                def along_width(q):
                    pe.wait_ge(gt_sb, q + 1)
                    if q >= 2:
                        pe.wait_ge(added, q - 1)
                    nc.tensor.matmul(ops[q % 2][:, 0:4 * W], gt[q % 2][:, 0, :], iw[:, :, :].rearrange("p a w -> p (a w)"), start=True, stop=True).then_inc(back, 1)
                turn(0)
                for q in range(H // 4):
                    if q + 1 < H // 4:
                        turn(q + 1)
                    along_width(q)


def host_l2():
    f8 = np.float64
    def cft(n, f):
        L, M = 4, 8
        seg = 1.0 / L
        starts = np.arange(L) / L
        k = np.arange(M)
        nodes = -np.cos((2 * k + 1) * np.pi / (2 * M))
        T = np.cos(k[:, None] * np.arccos(nodes)[None])
        ang = nodes[:, None] * (f * 2 * np.pi * seg / 2)[None]
        Wc = (T @ np.cos(ang) - 1j * (T @ np.sin(ang))) * (seg / 2)
        tc = np.linspace(0, 1, n)
        ts = starts[:, None] + seg / 2 * (nodes[None] + 1)
        right = np.clip(np.searchsorted(tc, ts), 0, n - 1)
        left = np.clip(right - 1, 0, n - 1)
        wr = (ts - tc[left]) / (tc[right] - tc[left])
        ph = np.exp(-2j * np.pi * starts[:, None] * f[None])
        out = np.zeros((n, len(f)), complex)
        for l in range(L):
            for m in range(M):
                v = Wc[m] * ph[l]
                out[left[l, m]] += (1 - wr[l, m]) * v
                out[right[l, m]] += wr[l, m] * v
        return out
    w = np.arange(W)
    ky = np.arange(KY)
    th = 2 * np.pi * w[:, None] * ky[None] / W
    fw = np.zeros((W, FW))
    fw[:, 0:2 * KY:2], fw[:, 1:2 * KY:2] = np.cos(th), -np.sin(th)
    cw = cft(W, np.arange(M2).astype(f8))
    fw[:, 2 * KY:2 * KY + M2], fw[:, 2 * KY + M2:] = cw.real, cw.imag
    kx = np.concatenate([np.arange(16), np.arange(H - 16, H)])
    h = np.arange(H)
    t = 2 * np.pi * ((h[:, None] * kx[None]) % H) / H
    fh = np.zeros((H, 2, KX, 2))
    fh[:, 0, :, 0], fh[:, 0, :, 1] = np.cos(t), -np.sin(t)
    fh[:, 1, :, 0], fh[:, 1, :, 1] = np.sin(t), np.cos(t)
    cc = cft(H, np.array([0., 1., -2., -1.]))
    ch = np.zeros((H, 2, M1, 2))
    ch[:, 0, :, 0], ch[:, 0, :, 1] = cc.real, cc.imag
    ch[:, 1, :, 0], ch[:, 1, :, 1] = -cc.imag, cc.real
    ih = np.zeros((2, KX, 2, H))
    ih[0, :, 0], ih[0, :, 1] = np.cos(t).T, np.sin(t).T
    ih[1, :, 0], ih[1, :, 1] = -np.sin(t).T, np.cos(t).T
    ih /= H
    c = np.where(ky == 0, 1.0, 2.0) / W
    i1 = np.zeros((KY, 2, W))
    i1[:, 0], i1[:, 1] = c[:, None] * np.cos(th).T, -c[:, None] * np.sin(th).T
    iw = np.zeros((4, KY * 2, 4, W))
    for a in range(4):
        iw[a, :, a] = i1.reshape(KY * 2, W)
    r = dict(fw=fw, fh=fh.reshape(H, 2, 2 * KX), ch=ch.reshape(H, 2, 2 * M1), ih=ih.reshape(2 * KX, 2 * H), iw=iw.reshape(P, 4, W))
    return {k: np.ascontiguousarray(v).astype(np.float32) for k, v in r.items()}


EDGE1 = 1
HID = 2 * C
KS = 3 * C + 3
STRIP = TR * W
NPP = STRIP // P
HALF = STRIP // 2


def stage_fftconv(nc, x_sb, whid, wdw, bdw, wout, bout, ones_d, dft_d, out):
    with ExitStack() as outer:
        sb = lambda n, s, dt=F: outer.enter_context(nc.sbuf_tensor("fc_" + n, s, dt))
        wk = sb("wk", [KS, 3, 3 * HID])
        wtmp = sb("wtmp", [KS, 3 * HID])
        bd = sb("bd", [KS, 3 * HID])
        wo = sb("wo", [P, 2, P])
        bo = sb("bo", [P, 1])
        dft = sb("dft", [P, 5, P])
        xp = sb("xp", [P, H + 2, W + 2])
        stage_norm(nc, "gn3", x_sb, xp, 1,
                   loads=((wk[:, :, :], wdw), (wtmp[:, :], whid), (bd[:, :], bdw), (bo[:, :], bout), (dft[:, :, :], dft_d)),
                   zeroed=wo[:, :, :], blocks=[(wo[HID * (b % 2):HID * (b % 2) + HID, b // 2, C * b:C * b + C], wout) for b in range(B)])
        with ExitStack() as ctx:
            sem = lambda n: ctx.enter_context(nc.semaphore("fc_" + n))
            sbc = lambda n, s, dt=F: ctx.enter_context(nc.sbuf_tensor("fc_" + n, s, dt))
            psum = lambda n, s: ctx.enter_context(nc.psum_tensor("fc_" + n, s, F))
            xs = [sbc(f"xs{i}", [KS, B, TR + 2, W]) for i in range(2)]
            qk = [sbc(f"qk{i}", [P, B, 2 * HID]) for i in range(2)]
            spec = [sbc(f"spec{i}", [P, 2, B, 2 * HID]) for i in range(2)]
            prod = [sbc(f"prod{i}", [P, 2, B, HID]) for i in range(2)]
            spo = [sbc(f"spo{i}", [P, B, HID]) for i in range(2)]
            vsb = sbc("vsb", [P, 2, STRIP])
            vo = sbc("vo", [P, 2, STRIP])
            qps = [psum(f"qps{i}", [P, 512]) for i in range(2)]
            fps = psum("fps", [P, 2, 512])
            ips = [psum(f"ips{i}", [P, 512]) for i in range(2)]
            vps = psum("vps", [P, 512])
            ops = psum("ops", [P, 512])
            strip_in = [sem("strip_in0"), sem("strip_in1")]
            qk_done, qk_sb, spec_done, spec_sb = sem("qk_done"), sem("qk_sb"), sem("spec_done"), sem("spec_sb")
            mul_done, comb_done, back_done, vo_done = sem("mul_done"), sem("comb_done"), sem("back_done"), sem("vo_done")
            wk_ready, biased = sem("wk_ready"), sem("biased")
            v_done, v_sb, out_done, x_done, stored = sem("v_done"), sem("v_sb"), sem("out_done"), sem("x_done"), sem("stored")
            block = ctx.enter_context(nc.Block())

            def strips(eng, body):
                body(0, 0, 0, True, False)
                with eng.Fori(0, NSTRIP // 2 - 1) as h:
                    body(h * 2 + 1, 1, h, False, False)
                    body(h * 2 + 2, 0, h + 1, False, False)
                body(NSTRIP - 1, 1, NSTRIP // 2 - 1, False, True)

            LOADS = 16 * (3 * B + 1)

            @block.sync
            def _(sp):
                def load(s, i, n, first, last):
                    wait(sp, v_done, s, 4, -4)
                    for dx in range(3):
                        for b in range(B):
                            sp.dma_start(xs[i][C * dx:C * dx + C, b, :, :],
                                         xp[C * b:C * b + C, ds(s * TR, TR + 2), dx:dx + W]).then_inc(strip_in[i], 16)
                    sp.dma_start(xs[i][3 * C:KS, :, :, :].rearrange("p b r c -> p b (r c)"),
                                 ones_d[:, :, ds(s * STRIP, (TR + 2) * W)]).then_inc(strip_in[i], 16)
                def store(s, i, n, first, last):
                    wait(sp, x_done, s, 2, 2)
                    sp.dma_start(out[:, ds(s * STRIP, STRIP)], x_sb[:, ds(s * STRIP, STRIP)]).then_inc(stored, 16)
                load(0, 0, 0, True, False)
                load(1, 1, 0, False, False)
                with sp.Fori(0, NSTRIP // 2 - 1) as h:
                    load(h * 2 + 2, 0, h + 1, False, False)
                    store(h * 2, 0, h, False, False)
                    load(h * 2 + 3, 1, h + 1, False, False)
                    store(h * 2 + 1, 1, h, False, False)
                store(NSTRIP - 2, 0, 0, False, False)
                store(NSTRIP - 1, 1, 0, False, True)
                sp.wait_ge(stored, 16 * NSTRIP)

            @block.gpsimd
            def _(pool):
                def combine(s, j):
                    m = j % 2
                    wait(pool, mul_done, s, NPP, j + 1)
                    wait(pool, back_done, s, NPP, j - 1)
                    nc.gpsimd.tensor_tensor(spo[m][:, :, :], prod[m][:, 0, :, :], prod[m][:, 1, :, :], ALU.add).then_inc(comb_done, 1)

                def body(s, i, n, first, last):
                    for j in range(NPP):
                        combine(s, j)
                strips(pool, body)

            @block.scalar
            def _(act):
                def spectra(s, j):
                    m = j % 2
                    wait(act, spec_done, s, NPP, j + 1)
                    wait(act, mul_done, s, NPP, j - 1)
                    nc.scalar.copy(spec[m][:, :, :, :].rearrange("p a b n -> p a (b n)"), fps[:, :, :]).then_inc(spec_sb, 1)

                def values(s, v):
                    wait(act, v_done, s, 4, v + 1)
                    if v == 0:
                        wait(act, out_done, s, 2, 0)
                    nc.scalar.copy(vsb[:, v % 2, HALF * (v // 2):HALF * (v // 2) + HALF], vps[:, 0:HALF]).then_inc(v_sb, 1)

                def body(s, i, n, first, last):
                    values(s, 0)
                    values(s, 1)
                    for j in range(NPP):
                        spectra(s, j)
                        if j == 4:
                            values(s, 2)
                            values(s, 3)
                strips(act, body)

            @block.vector
            def _(dve):
                def take(s, j):
                    m = j % 2
                    wait(dve, qk_done, s, NPP, j + 1)
                    wait(dve, spec_done, s, NPP, j - 1)
                    nc.vector.tensor_copy(qk[m][:, :, :].rearrange("p b n -> p (b n)"), qps[m][:, :]).then_inc(qk_sb, 1)

                def multiply(s, j):
                    m = j % 2
                    wait(dve, spec_sb, s, NPP, j + 1)
                    wait(dve, comb_done, s, NPP, j - 1)
                    nc.vector.tensor_tensor(prod[m][:, :, :, :], spec[m][:, :, :, 0:HID], spec[m][:, :, :, HID:2 * HID], ALU.mult).then_inc(mul_done, 1)

                def weigh(s, j):
                    m = j % 2
                    wait(dve, back_done, s, NPP, j + 1)
                    wait(dve, v_sb, s, 4, 2 if j < 3 else 4)
                    if j == 0:
                        wait(dve, out_done, s, 2, 0)
                    nc.vector.tensor_tensor(vo[:, :, P * j:P * j + P], ips[m][:, 0:2 * P].rearrange("p (a n) -> p a n", a=2),
                                            vsb[:, :, P * j:P * j + P], ALU.mult).then_inc(vo_done, 1)

                def residual(s, h):
                    wait(dve, out_done, s, 2, h + 1)
                    xv = x_sb[:, ds(s * STRIP + HALF * h, HALF)]
                    if h == 0 and isinstance(s, int) and s == 0:
                        dve.wait_ge(biased, 1)
                    nc.vector.tensor_tensor(xv, ops[:, 0:HALF], xv, ALU.add).then_inc(x_done, 1)

                def body(s, i, n, first, last):
                    take(s, 0)
                    if not first:
                        weigh(s + (-1), NPP - 1)
                        residual(s + (-1), 0)
                    take(s, 1)
                    if not first:
                        residual(s + (-1), 1)
                    for j in range(NPP):
                        multiply(s, j)
                        if j + 2 < NPP:
                            take(s, j + 2)
                        if j >= 1:
                            weigh(s, j - 1)
                    if last:
                        weigh(s, NPP - 1)
                        residual(s, 0)
                        residual(s, 1)
                nc.vector.tensor_tensor(wk[:, :, :], wk[:, :, :], wtmp[:, :].unsqueeze(1).broadcast_to([KS, 3, 3 * HID]), ALU.mult).then_inc(wk_ready, 1)
                dve.wait_ge(wk_ready, 1)
                nc.vector.tensor_tensor(wk[:, 1, :], wk[:, 1, :], bd[:, :], ALU.add).then_inc(wk_ready, 1)
                nc.vector.tensor_scalar(x_sb[:, :], x_sb[:, :], bo[:, 0:1], None, ALU.add).then_inc(biased, 1)
                strips(dve, body)

            @block.tensor
            def _(pe):
                def rows(i, b, at, n):
                    return xs[i][:, b, :, :].rearrange("p r c -> p (r c)")[:, at:at + n]

                def project(s, i, n, j):
                    m = j % 2
                    if j == 0:
                        wait(pe, strip_in[i], n, LOADS, LOADS)
                    wait(pe, qk_sb, s, NPP, j - 1)
                    for b in range(B):
                        for dy in range(3):
                            mm = nc.tensor.matmul(qps[m][:, P * b:P * b + P], rows(i, b, dy * W + P * j, P), wk[:, dy, 0:2 * HID],
                                                  start=(dy == 0), stop=(dy == 2))
                    mm.then_inc(qk_done, 1)

                def values(s, i, v):
                    h, a = v // 2, v % 2
                    wait(pe, v_sb, s, 4, v)
                    for b in range(2):
                        for dy in range(3):
                            mm = nc.tensor.matmul(vps[HID * b:HID * b + HID, 0:HALF], wk[:, dy, 2 * HID:3 * HID],
                                                  rows(i, 2 * a + b, dy * W + HALF * h, HALF),
                                                  start=(dy == 0), stop=(dy == 2))
                    mm.then_inc(v_done, 1)

                def forward(s, j):
                    m = j % 2
                    wait(pe, qk_sb, s, NPP, j + 1)
                    wait(pe, spec_sb, s, NPP, j)
                    for part in range(2):
                        for k in range(2):
                            mm = nc.tensor.matmul(fps[:, part, :].rearrange("p (b n) -> p b n", b=B)[:, :, HID * k:HID * k + HID], dft[:, 2 * k + part, :],
                                                  qk[m][:, :, HID * k:HID * k + HID], start=True, stop=True)
                    mm.then_inc(spec_done, 1)

                def back(s, j):
                    m = j % 2
                    wait(pe, comb_done, s, NPP, j + 1)
                    wait(pe, vo_done, s, NPP, j - 1)
                    for a in range(2):
                        mm = nc.tensor.matmul(ips[m][:, P * a:P * a + P], spo[m][:, 2 * a:2 * a + 2, :].rearrange("p b n -> p (b n)"),
                                              dft[:, 4, :], start=True, stop=True)
                    mm.then_inc(back_done, 1)

                def merge(s, h):
                    wait(pe, vo_done, s, NPP, 3 * h + 3)
                    wait(pe, x_done, s, 2, h)
                    for a in range(2):
                        mm = nc.tensor.matmul(ops[:, 0:HALF], wo[:, a, :], vo[:, a, HALF * h:HALF * h + HALF], start=(a == 0), stop=(a == 1))
                    mm.then_inc(out_done, 1)

                def body(s, i, n, first, last):
                    project(s, i, n, 0)
                    if not first:
                        back(s + (-1), NPP - 1)
                    project(s, i, n, 1)
                    if not first:
                        merge(s + (-1), 1)
                    values(s, i, 0)
                    forward(s, 0)
                    values(s, i, 1)
                    for j in range(2, NPP):
                        project(s, i, n, j)
                        forward(s, j - 1)
                        back(s, j - 2)
                    values(s, i, 2)
                    forward(s, NPP - 1)
                    values(s, i, 3)
                    back(s, NPP - 2)
                    merge(s, 0)
                    if last:
                        back(s, NPP - 1)
                        merge(s, 1)
                pe.wait_ge(wk_ready, 2)
                strips(pe, body)


def host_l3(wh, bh, wd, bdw, wo, bo):
    wh, wd = wh.reshape(192, C), wd.reshape(192, 3, 3)
    whid = np.concatenate([np.tile(wh.T, (3, 1)), np.tile(bh, (3, 1))], 0)
    t = wd.transpose(2, 1, 0)
    wdw = np.concatenate([np.repeat(t, C, 0), t], 0)
    bd = np.zeros((KS, 192), np.float32)
    bd[3 * C + 1] = bdw
    wout = wo.reshape(C, HID).T
    ones = np.zeros((3, B, H + 2, W), np.float32)
    ones[:, :, 1:H + 1] = 1
    ones[0, :, :, 0] = 0
    ones[2, :, :, W - 1] = 0
    r, c = np.arange(64) // 8, np.arange(64) % 8
    th = 2 * np.pi * (r[:, None] * r[None] + c[:, None] * c[None]) / 8
    z = np.zeros((5, P, P))
    for q in range(2):
        s = slice(64 * q, 64 * q + 64)
        z[0, s, s] = np.cos(th) + np.sin(th)
        z[1, s, s] = np.cos(th) - np.sin(th)
        z[2, s, s] = np.cos(th)
        z[3, s, s] = np.sin(th)
        z[4, s, s] = (np.cos(th) + np.sin(th)) / 64
    return dict(whid=whid, wdw=wdw, bdw=bd, wout=wout, bout=np.tile(bo, 4)[:, None], ones=ones.reshape(3, B, -1),
                dft=np.ascontiguousarray(z.transpose(1, 0, 2)).astype(np.float32))




def program(nc, a, out):
    dram = lambda n, s: nc.dram_tensor(n, s, F, kind="Internal").ap()
    with ExitStack() as ctx:
        x_sb = ctx.enter_context(nc.sbuf_tensor("x_sb", [P, NPIX], F))
        stage_attention(nc, a["x"], x_sb, a["wqkvT"], a["rel"], a["halves"], a["headmask"], a["unitmask"], a["ident"],
                        dram("attention_queries", [P, NROW, NROW, Q64]))
        with ExitStack() as deform:
            x_save = dram("deform_save", [P, NPIX])
            far = deform.enter_context(nc.sbuf_tensor("far", [1, 1], I32))[:, :]
            stage_deform_near(nc, x_sb, a["near_convw"], a["near_convb"], a["near_rep"], a["near_sel"], a["near_dcnbd"],
                              a["near_shifts"], a["ident"], x_save, far)
            stage_deform_far(nc, x_sb, a["convw"], a["bias"], a["coord"], a["ixb"], a["dcn"], a["ident"],
                             dram("deform_image", [P, TY, TY]), dram("deform_table", [1 + B * TROWS * TX, ENTRY]), x_save, far)
        stage_fourier(nc, x_sb, a["fw"], a["fh"], a["ch"], a["ih"], a["iw"], a["w1"], a["w2"],
                      a["lin1"], a["b1"], a["lin2"], a["b2"], a["ident"])
        stage_fftconv(nc, x_sb, a["whid"], a["wdw"], a["bdw"], a["wout"], a["bout"], a["ones"], a["dft"], out)


def kernel(**inputs):
    import concourse.bacc as bacc
    from concourse.bass_utils import run_bass_kernel_spmd

    i = {k: np.asarray(v) for k, v in inputs.items()}
    qkv = i["L0_conv_w_qkv"].reshape(3, C, C).transpose(2, 0, 1)
    rel = np.concatenate([i["L0_conv_rel_h"].reshape(WIN, D // 2), i["L0_conv_rel_w"].reshape(WIN, D // 2)], 1).T
    deform = [i["L1_conv_" + n] for n in ("offset_w", "offset_b", "mask_w", "mask_b", "dcn_w")]
    arrays = dict(
        x=i["x"].reshape(P, NPIX), wqkvT=qkv, rel=np.tile(rel, (P // D, 1)), **host_consts(),
        **host_l1(*deform), **{"near_" + k: v for k, v in host_l1d(*deform).items()},
        **host_l2(), w1=i["L2_conv_w1"], w2=i["L2_conv_w2"], lin1=i["L2_conv_lin1_w"], b1=i["L2_conv_lin1_b"][:, None],
        lin2=i["L2_conv_lin2_w"], b2=np.tile(i["L2_conv_lin2_b"], B)[:, None],
        **host_l3(*(i["L3_conv_" + n] for n in ("w_hidden", "b_hidden", "w_dw", "b_dw", "w_out", "b_out"))))
    arrays = {k: np.ascontiguousarray(v) for k, v in arrays.items()}
    nc = bacc.Bacc("TRN2", target_bir_lowering=False, num_devices=1)
    handles = {k: nc.dram_tensor("in_" + k, v.shape, mybir.dt.from_np(v.dtype), kind="ExternalInput").ap()
               for k, v in arrays.items()}
    out = nc.dram_tensor("out", [P, NPIX], F, kind="ExternalOutput").ap()
    program(nc, handles, out)
    r = run_bass_kernel_spmd(nc, [{"in_" + k: v for k, v in arrays.items()}], core_ids=[0])
    return r.results[0]["out"].reshape(B, C, H, W)
```
